# Optimizing a Trainium2 kernel written in Bass

```python
import numpy as np
import jax
import jax.numpy as jnp

def _softmax(x, axis=-1):
    return jax.nn.softmax(x, axis=axis)

def _gelu(x):
    return jax.nn.gelu(x, approximate=True)

def _silu(x):
    return jax.nn.silu(x)

def _sigmoid(x):
    return jax.nn.sigmoid(x)

def _layernorm(x, axis=-1, eps=1e-05):
    m = jnp.mean(x, axis=axis, keepdims=True)
    v = jnp.var(x, axis=axis, keepdims=True)
    return (x - m) / jnp.sqrt(v + eps)

def _scatter_add(tgt, idx, src, axis=0):
    return tgt.at[idx].add(src)

def _segment_sum(src, seg, n):
    return jax.ops.segment_sum(src, seg, n)
kernel_name = 'mk_decoder_postln_d2_seqx_r8_01f5c1'

def setup_inputs(seed: int=0):
    np.random.seed(seed)
    _w = jnp.asarray

    def _rec_inputs():
        import jax
        import jax.numpy as jnp
        _rk = jax.random.key(seed)
        x = -0.0002928 + 1 * jax.random.normal(jax.random.fold_in(_rk, 1), (32, 128, 128), jnp.float32)
        _lenS = 128 - jax.random.randint(jax.random.fold_in(_rk, 7), (32,), 0, max(1, 128 // 4) + 1, jnp.int32)
        _lenS2 = 128 - jax.random.randint(jax.random.fold_in(_rk, 8), (32,), 0, max(1, 128 // 4) + 1, jnp.int32)
        _ctx_1024P = jax.random.normal(jax.random.fold_in(_rk, 11), (32, 16, 128), jnp.float32)
        _ctx_1024c = jax.random.dirichlet(jax.random.fold_in(_rk, 511), 0.3 * jnp.ones((16,), jnp.float32), (32, 128))
        _ctx_1024t = jnp.einsum('bsk,bkd->bsd', _ctx_1024c, _ctx_1024P)
        _ctx_1024t = _ctx_1024t * jax.lax.rsqrt(jnp.mean(jnp.square(_ctx_1024t)) + 1e-12) * 0.953939
        ctx_1024 = 4.13588e-05 + 0.999923 * (_ctx_1024t + 0.3 * jax.random.normal(jax.random.fold_in(_rk, 611), (32, 128, 128), jnp.float32))
        return (x, ctx_1024)
    x, ctx_1024 = _rec_inputs()

    def _L0_attn_setup():
        import jax, jax.numpy as jnp
        import numpy as np
        import itertools
        B, T, C, H = (2, 256, 128, 8)
        HD = C // H

        def _head_dirs():
            signs = [-1.0, 1.0]
            tri = np.array(list(itertools.product(signs, repeat=3)), dtype=np.float32)
            tri = tri / np.linalg.norm(tri, axis=1, keepdims=True)
            return jnp.asarray(tri[:H])
        key = jax.random.key(seed)
        ks = jax.random.split(key, 5)
        w = lambda k, sh: jax.random.normal(k, sh, dtype=jnp.float32) * 0.02
        return {'x': jax.random.normal(ks[0], (B, T, C), dtype=jnp.float32), 'Wq': w(ks[1], (H * 3, C)), 'Wk': w(ks[2], (H * 3, C)), 'Wv': w(ks[3], (C, C)), 'Wo': w(ks[4], (C, C)), 'scale': jnp.asarray(1.0 / np.sqrt(3.0), dtype=jnp.float32)}
    _L0_attn_all = _L0_attn_setup()
    _L0_attn_in = {k: v for k, v in _L0_attn_all.items() if k in ('Wq', 'Wk', 'Wv', 'Wo', 'scale')}
    del _L0_attn_all

    def _L0_xattn_setup():
        import jax, jax.numpy as jnp
        import numpy as np
        DIM = 128
        NUM_HEADS = 16
        DIM_HEAD = 64
        INNER = NUM_HEADS * DIM_HEAD
        SCALE = DIM_HEAD ** (-0.5)

        def _layernorm(x, gamma, beta, eps=1e-05):
            mu = jnp.mean(x, axis=-1, keepdims=True)
            var = jnp.mean(jnp.square(x - mu), axis=-1, keepdims=True)
            return (x - mu) * jax.lax.rsqrt(var + eps) * gamma + beta
        key = jax.random.key(seed)
        ks = jax.random.split(key, 8)
        B, SQ, SK = (2, 256, 512)
        x = jax.random.normal(ks[0], (B, SQ, DIM), dtype=jnp.float32)
        context = jax.random.normal(ks[1], (B, SK, DIM), dtype=jnp.float32)
        ln_gamma = jnp.ones((DIM,), jnp.float32)
        ln_beta = jnp.zeros((DIM,), jnp.float32)
        w_q = jax.random.normal(ks[2], (DIM, INNER), dtype=jnp.float32) / np.sqrt(DIM)
        w_kv = jax.random.normal(ks[3], (DIM, 2 * INNER), dtype=jnp.float32) / np.sqrt(DIM)
        w_out = jax.random.normal(ks[4], (INNER, DIM), dtype=jnp.float32) / np.sqrt(INNER)
        b_out = jnp.zeros((DIM,), jnp.float32)
        gate = jnp.array([0.5], jnp.float32)
        return {'x': x, 'context': context, 'ln_gamma': ln_gamma, 'ln_beta': ln_beta, 'w_q': w_q, 'w_kv': w_kv, 'w_out': w_out, 'b_out': b_out, 'gate': gate}
    _L0_xattn_all = _L0_xattn_setup()
    _L0_xattn_in = {k: v for k, v in _L0_xattn_all.items() if k in ('ln_gamma', 'ln_beta', 'w_q', 'w_kv', 'w_out', 'b_out', 'gate')}
    del _L0_xattn_all

    def _L0_ffn_setup():
        import jax, jax.numpy as jnp
        import numpy as np
        NUM_EXPERTS = 8
        TOP_K = 2
        B, T, D, F = (4, 256, 128, 352)
        key = jax.random.key(seed)
        ks = jax.random.split(key, 5)
        return {'x': jax.random.normal(ks[0], (B, T, D), dtype=jnp.float32), 'router_w': jax.random.normal(ks[1], (D, NUM_EXPERTS), dtype=jnp.float32) * 0.02, 'gate_proj': jax.random.normal(ks[2], (NUM_EXPERTS, D, F), dtype=jnp.float32) * 0.02, 'up_proj': jax.random.normal(ks[3], (NUM_EXPERTS, D, F), dtype=jnp.float32) * 0.02, 'down_proj': jax.random.normal(ks[4], (NUM_EXPERTS, F, D), dtype=jnp.float32) * 0.02}
    _L0_ffn_all = _L0_ffn_setup()
    _L0_ffn_in = {k: v for k, v in _L0_ffn_all.items() if k in ('router_w', 'gate_proj', 'up_proj', 'down_proj')}
    del _L0_ffn_all

    def _L1_attn_setup():
        import jax, jax.numpy as jnp
        import numpy as np
        D_CONV = 4
        CHUNK = 64

        def segsum(x):
            T = x.shape[-1]
            strict = jnp.tril(jnp.ones((T, T), dtype=bool), -1)
            xr = jnp.where(strict, x[..., :, None], 0.0)
            x_segsum = jnp.cumsum(xr, axis=-2)
            return jnp.where(jnp.tril(jnp.ones((T, T), dtype=bool)), x_segsum, -jnp.inf)

        def ssd(x, A, B, C, chunk):
            b, s, h, p = x.shape
            c = s // chunk
            x = x.reshape(b, c, chunk, h, p)
            B = B.reshape(b, c, chunk, h, -1)
            C = C.reshape(b, c, chunk, h, -1)
            A = A.reshape(b, c, chunk, h).transpose(0, 3, 1, 2)
            A_cumsum = jnp.cumsum(A, axis=-1)
            L = jnp.exp(segsum(A))
            Y_diag = jnp.einsum('bclhn,bcshn,bhcls,bcshp->bclhp', C, B, L, x)
            decay_states = jnp.exp(A_cumsum[..., -1:] - A_cumsum)
            states = jnp.einsum('bclhn,bhcl,bclhp->bchpn', B, decay_states, x)
            states = jnp.concatenate([jnp.zeros_like(states[:, :1]), states], axis=1)
            A_last = jnp.pad(A_cumsum[..., -1], ((0, 0), (0, 0), (1, 0)))
            decay_chunk = jnp.exp(segsum(A_last))
            states = jnp.einsum('bhzc,bchpn->bzhpn', decay_chunk, states)[:, :-1]
            Y_off = jnp.einsum('bclhn,bchpn,bhcl->bclhp', C, states, jnp.exp(A_cumsum))
            return (Y_diag + Y_off).reshape(b, s, h, p)
        key = jax.random.key(seed)
        ks = jax.random.split(key, 6)
        d_model, d_state, d_inner, n_heads = (128, 128, 128, 16)
        d_in_proj = 2 * d_state + d_inner + n_heads
        d_conv_c = 2 * d_state + d_inner
        b, s = (4, 512)

        def xavier(k, shape):
            bnd = float(np.sqrt(6.0 / (shape[0] + shape[1])))
            return jax.random.uniform(k, shape, minval=-bnd, maxval=bnd, dtype=jnp.float32)
        return {'x': jax.random.normal(ks[0], (b, s, d_model), dtype=jnp.float32), 'W_in': xavier(ks[1], (d_in_proj, d_model)), 'conv_w': jax.random.uniform(ks[2], (d_conv_c, D_CONV), minval=-0.8, maxval=0.8, dtype=jnp.float32), 'conv_b': jnp.zeros((d_conv_c,), dtype=jnp.float32), 'A_param': jax.random.uniform(ks[3], (16,), minval=-0.01, maxval=0.01, dtype=jnp.float32), 'dt_bias': jax.random.uniform(ks[4], (16,), minval=-0.1, maxval=0.1, dtype=jnp.float32), 'W_out': xavier(ks[5], (d_model, d_inner))}
    _L1_attn_all = _L1_attn_setup()
    _L1_attn_in = {k: v for k, v in _L1_attn_all.items() if k in ('W_in', 'conv_w', 'conv_b', 'A_param', 'dt_bias', 'W_out')}
    del _L1_attn_all

    def _L1_xattn_setup():
        import jax, jax.numpy as jnp
        import numpy as np
        H = 128
        B = 8
        L_CHAR = 256
        L_SUB = 128

        def _linear(x, W, b):
            return jnp.einsum('blh,oh->blo', x, W) + b

        def _interp_linear(x, out_len):
            L_in = x.shape[1]
            pos = (jnp.arange(out_len, dtype=x.dtype) + 0.5) * (L_in / out_len) - 0.5
            pos = jnp.clip(pos, 0.0, L_in - 1)
            lo = jnp.floor(pos).astype(jnp.int32)
            hi = jnp.minimum(lo + 1, L_in - 1)
            w = (pos - lo.astype(x.dtype))[None, :, None]
            return x[:, lo] * (1 - w) + x[:, hi] * w
        key = jax.random.key(seed)
        ks = jax.random.split(key, 18)
        s = 0.02
        inp = {'char_emb': jax.random.normal(ks[0], (B, L_CHAR, H), jnp.float32), 'subword_emb': jax.random.normal(ks[1], (B, L_SUB, H), jnp.float32)}
        names = ['Wq_c', 'Wk_s', 'Wv_s', 'Wq_s', 'Wk_c', 'Wv_c']
        for i, n in enumerate(names):
            inp[n] = jax.random.normal(ks[2 + 2 * i], (H, H), jnp.float32) * s
            inp['b' + n[1:]] = jax.random.normal(ks[3 + 2 * i], (H,), jnp.float32) * s
        inp['Wg'] = jax.random.normal(ks[14], (H, 2 * H), jnp.float32) * s
        inp['bg'] = jax.random.normal(ks[15], (H,), jnp.float32) * s
        return inp
    _L1_xattn_all = _L1_xattn_setup()
    _L1_xattn_in = {k: v for k, v in _L1_xattn_all.items() if k in ('Wq_c', 'bq_c', 'Wk_s', 'bk_s', 'Wv_s', 'bv_s', 'Wq_s', 'bq_s', 'Wk_c', 'bk_c', 'Wv_c', 'bv_c', 'Wg', 'bg')}
    del _L1_xattn_all

    def _L1_ffn_setup():
        import jax, jax.numpy as jnp
        import numpy as np
        D_MODEL = 128
        D_FF = 512
        NUM_EXPERTS = 8
        B, N = (16, 128)
        key = jax.random.key(seed)
        ks = jax.random.split(key, 7)
        s_in = 1.0 / np.sqrt(D_MODEL)
        s_ff = 1.0 / np.sqrt(D_FF)
        return {'x': jax.random.normal(ks[0], (B, N, D_MODEL), dtype=jnp.float32), 'Wr': jax.random.uniform(ks[1], (D_MODEL, NUM_EXPERTS), jnp.float32, -s_in, s_in), 'br': jax.random.uniform(ks[2], (NUM_EXPERTS,), jnp.float32, -s_in, s_in), 'W1': jax.random.uniform(ks[3], (NUM_EXPERTS, D_MODEL, D_FF), jnp.float32, -s_in, s_in), 'b1': jax.random.uniform(ks[4], (NUM_EXPERTS, D_FF), jnp.float32, -s_in, s_in), 'W2': jax.random.uniform(ks[5], (NUM_EXPERTS, D_FF, D_MODEL), jnp.float32, -s_ff, s_ff), 'b2': jax.random.uniform(ks[6], (NUM_EXPERTS, D_MODEL), jnp.float32, -s_ff, s_ff)}
    _L1_ffn_all = _L1_ffn_setup()
    _L1_ffn_in = {k: v for k, v in _L1_ffn_all.items() if k in ('Wr', 'br', 'W1', 'b1', 'W2', 'b2')}
    del _L1_ffn_all
    return {'x': x, 'ctx_1024': ctx_1024, 'L0_attn_Wq': _L0_attn_in['Wq'], 'L0_attn_Wk': _L0_attn_in['Wk'], 'L0_attn_Wv': _L0_attn_in['Wv'], 'L0_attn_Wo': _L0_attn_in['Wo'], 'L0_attn_scale': _L0_attn_in['scale'], 'L0_xattn_ln_gamma': _L0_xattn_in['ln_gamma'], 'L0_xattn_ln_beta': _L0_xattn_in['ln_beta'], 'L0_xattn_w_q': _L0_xattn_in['w_q'], 'L0_xattn_w_kv': _L0_xattn_in['w_kv'], 'L0_xattn_w_out': _L0_xattn_in['w_out'], 'L0_xattn_b_out': _L0_xattn_in['b_out'], 'L0_xattn_gate': _L0_xattn_in['gate'], 'L0_ffn_router_w': _L0_ffn_in['router_w'], 'L0_ffn_gate_proj': _L0_ffn_in['gate_proj'], 'L0_ffn_up_proj': _L0_ffn_in['up_proj'], 'L0_ffn_down_proj': _L0_ffn_in['down_proj'], 'L1_attn_W_in': _L1_attn_in['W_in'], 'L1_attn_conv_w': _L1_attn_in['conv_w'], 'L1_attn_conv_b': _L1_attn_in['conv_b'], 'L1_attn_A_param': _L1_attn_in['A_param'], 'L1_attn_dt_bias': _L1_attn_in['dt_bias'], 'L1_attn_W_out': _L1_attn_in['W_out'], 'L1_xattn_Wq_c': _L1_xattn_in['Wq_c'], 'L1_xattn_bq_c': _L1_xattn_in['bq_c'], 'L1_xattn_Wk_s': _L1_xattn_in['Wk_s'], 'L1_xattn_bk_s': _L1_xattn_in['bk_s'], 'L1_xattn_Wv_s': _L1_xattn_in['Wv_s'], 'L1_xattn_bv_s': _L1_xattn_in['bv_s'], 'L1_xattn_Wq_s': _L1_xattn_in['Wq_s'], 'L1_xattn_bq_s': _L1_xattn_in['bq_s'], 'L1_xattn_Wk_c': _L1_xattn_in['Wk_c'], 'L1_xattn_bk_c': _L1_xattn_in['bk_c'], 'L1_xattn_Wv_c': _L1_xattn_in['Wv_c'], 'L1_xattn_bv_c': _L1_xattn_in['bv_c'], 'L1_xattn_Wg': _L1_xattn_in['Wg'], 'L1_xattn_bg': _L1_xattn_in['bg'], 'L1_ffn_Wr': _L1_ffn_in['Wr'], 'L1_ffn_br': _L1_ffn_in['br'], 'L1_ffn_W1': _L1_ffn_in['W1'], 'L1_ffn_b1': _L1_ffn_in['b1'], 'L1_ffn_W2': _L1_ffn_in['W2'], 'L1_ffn_b2': _L1_ffn_in['b2']}

def reference(x, ctx_1024, L0_attn_Wq, L0_attn_Wk, L0_attn_Wv, L0_attn_Wo, L0_attn_scale, L0_xattn_ln_gamma, L0_xattn_ln_beta, L0_xattn_w_q, L0_xattn_w_kv, L0_xattn_w_out, L0_xattn_b_out, L0_xattn_gate, L0_ffn_router_w, L0_ffn_gate_proj, L0_ffn_up_proj, L0_ffn_down_proj, L1_attn_W_in, L1_attn_conv_w, L1_attn_conv_b, L1_attn_A_param, L1_attn_dt_bias, L1_attn_W_out, L1_xattn_Wq_c, L1_xattn_bq_c, L1_xattn_Wk_s, L1_xattn_bk_s, L1_xattn_Wv_s, L1_xattn_bv_s, L1_xattn_Wq_s, L1_xattn_bq_s, L1_xattn_Wk_c, L1_xattn_bk_c, L1_xattn_Wv_c, L1_xattn_bv_c, L1_xattn_Wg, L1_xattn_bg, L1_ffn_Wr, L1_ffn_br, L1_ffn_W1, L1_ffn_b1, L1_ffn_W2, L1_ffn_b2):
    import jax
    import jax.numpy as jnp

    def _L0_attn_ref(x, Wq, Wk, Wv, Wo, scale):
        import jax, jax.numpy as jnp
        import numpy as np
        import itertools
        B, T, C, H = (2, 256, 128, 8)
        HD = C // H

        def _head_dirs():
            signs = [-1.0, 1.0]
            tri = np.array(list(itertools.product(signs, repeat=3)), dtype=np.float32)
            tri = tri / np.linalg.norm(tri, axis=1, keepdims=True)
            return jnp.asarray(tri[:H])
        Bb, Tt, Cc = x.shape
        dirs = _head_dirs()
        q3 = (x @ Wq.T).reshape(Bb, Tt, H, 3).transpose(0, 2, 1, 3)
        k3 = (x @ Wk.T).reshape(Bb, Tt, H, 3).transpose(0, 2, 1, 3)
        v = (x @ Wv.T).reshape(Bb, Tt, H, HD).transpose(0, 2, 1, 3)
        q_on_dir = jnp.einsum('bhtd,hd->bht', q3, dirs)
        k_on_dir = jnp.einsum('bhtd,hd->bht', k3, dirs)
        scores = jnp.einsum('bhtd,bhsd->bhts', q3, k3) * scale + q_on_dir[..., :, None] * k_on_dir[..., None, :]
        causal = jnp.tril(jnp.ones((Tt, Tt), dtype=bool))
        scores = jnp.where(causal, scores, -jnp.inf)
        attn = jax.nn.softmax(scores, axis=-1)
        out = jnp.einsum('bhts,bhsd->bhtd', attn, v)
        out = out.transpose(0, 2, 1, 3).reshape(Bb, Tt, Cc)
        return out @ Wo.T

    def _L0_xattn_ref(x, context, ln_gamma, ln_beta, w_q, w_kv, w_out, b_out, gate):
        import jax, jax.numpy as jnp
        import numpy as np
        DIM = 128
        NUM_HEADS = 16
        DIM_HEAD = 64
        INNER = NUM_HEADS * DIM_HEAD
        SCALE = DIM_HEAD ** (-0.5)

        def _layernorm(x, gamma, beta, eps=1e-05):
            mu = jnp.mean(x, axis=-1, keepdims=True)
            var = jnp.mean(jnp.square(x - mu), axis=-1, keepdims=True)
            return (x - mu) * jax.lax.rsqrt(var + eps) * gamma + beta
        B, SQ, _ = x.shape
        SK = context.shape[1]
        xn = _layernorm(x, ln_gamma, ln_beta)
        q = (xn @ w_q).reshape(B, SQ, NUM_HEADS, DIM_HEAD)
        kv = context @ w_kv
        k, v = jnp.split(kv, 2, axis=-1)
        k = k.reshape(B, SK, NUM_HEADS, DIM_HEAD)
        v = v.reshape(B, SK, NUM_HEADS, DIM_HEAD)
        scores = jnp.einsum('bqhd,bkhd->bhqk', q * SCALE, k)
        attn = jax.nn.softmax(scores, axis=-1)
        out = jnp.einsum('bhqk,bkhd->bqhd', attn, v).reshape(B, SQ, INNER)
        out = out @ w_out + b_out
        return out * jnp.tanh(gate[0])

    def _L0_ffn_ref(x, router_w, gate_proj, up_proj, down_proj):
        import jax, jax.numpy as jnp
        import numpy as np
        NUM_EXPERTS = 8
        TOP_K = 2
        B, T, D, F = (4, 256, 128, 352)
        scores = jnp.einsum('btd,de->bte', x, router_w).astype(jnp.float32)
        probs = jax.nn.softmax(scores, axis=-1)
        routing_weights, routing_idx = jax.lax.top_k(probs, TOP_K)
        routing_weights = (routing_weights / jnp.sum(routing_weights, axis=-1, keepdims=True)).astype(x.dtype)
        one_hot = jax.nn.one_hot(routing_idx, NUM_EXPERTS, dtype=x.dtype)
        expert_w = jnp.einsum('btke,btk->bte', one_hot, routing_weights)
        dispatched = jnp.einsum('btd,btke->bted', x, one_hot)
        gate = jnp.einsum('bted,edf->btef', dispatched, gate_proj)
        up = jnp.einsum('bted,edf->btef', dispatched, up_proj)
        acts = jax.nn.silu(gate) * up
        expert_out = jnp.einsum('btef,efd->bted', acts, down_proj)
        return jnp.einsum('bted,bte->btd', expert_out, expert_w)

    def _L1_attn_ref(x, W_in, conv_w, conv_b, A_param, dt_bias, W_out):
        import jax, jax.numpy as jnp
        import numpy as np
        D_CONV = 4
        CHUNK = 64

        def segsum(x):
            T = x.shape[-1]
            strict = jnp.tril(jnp.ones((T, T), dtype=bool), -1)
            xr = jnp.where(strict, x[..., :, None], 0.0)
            x_segsum = jnp.cumsum(xr, axis=-2)
            return jnp.where(jnp.tril(jnp.ones((T, T), dtype=bool)), x_segsum, -jnp.inf)

        def ssd(x, A, B, C, chunk):
            b, s, h, p = x.shape
            c = s // chunk
            x = x.reshape(b, c, chunk, h, p)
            B = B.reshape(b, c, chunk, h, -1)
            C = C.reshape(b, c, chunk, h, -1)
            A = A.reshape(b, c, chunk, h).transpose(0, 3, 1, 2)
            A_cumsum = jnp.cumsum(A, axis=-1)
            L = jnp.exp(segsum(A))
            Y_diag = jnp.einsum('bclhn,bcshn,bhcls,bcshp->bclhp', C, B, L, x)
            decay_states = jnp.exp(A_cumsum[..., -1:] - A_cumsum)
            states = jnp.einsum('bclhn,bhcl,bclhp->bchpn', B, decay_states, x)
            states = jnp.concatenate([jnp.zeros_like(states[:, :1]), states], axis=1)
            A_last = jnp.pad(A_cumsum[..., -1], ((0, 0), (0, 0), (1, 0)))
            decay_chunk = jnp.exp(segsum(A_last))
            states = jnp.einsum('bhzc,bchpn->bzhpn', decay_chunk, states)[:, :-1]
            Y_off = jnp.einsum('bclhn,bchpn,bhcl->bclhp', C, states, jnp.exp(A_cumsum))
            return (Y_diag + Y_off).reshape(b, s, h, p)
        b, src_len, d_model = x.shape
        n_heads = A_param.shape[0]
        d_conv_c = conv_w.shape[0]
        d_inner = W_out.shape[1]
        d_state = (d_conv_c - d_inner) // 2
        pad = -src_len % CHUNK
        xs = jnp.pad(x, ((0, 0), (0, pad), (0, 0)))
        s = xs.shape[1]
        proj = xs @ W_in.T
        xBC, dt = (proj[..., :d_conv_c], proj[..., d_conv_c:])
        xp = jnp.pad(xBC, ((0, 0), (D_CONV - 1, 0), (0, 0)))
        conv_out = sum((xp[:, k:k + s, :] * conv_w[:, k] for k in range(D_CONV))) + conv_b
        C_ = conv_out[..., :d_state]
        B_ = conv_out[..., d_state:2 * d_state]
        xin = conv_out[..., 2 * d_state:]
        dt = jax.nn.softplus(dt + dt_bias)
        Ch = C_.reshape(b, s, n_heads, -1)
        Bh = B_.reshape(b, s, n_heads, -1)
        xh = xin.reshape(b, s, n_heads, -1)
        A = A_param * dt
        cumA = jnp.cumsum(A, axis=1)
        norm = (jnp.exp(cumA) * jnp.cumsum(jnp.exp(-cumA), axis=1))[..., None]
        Y = ssd(xh, A, Bh, Ch, CHUNK)
        out = Y[0] / norm
        out = out.reshape(b, s, -1) @ W_out.T
        return out[:, :src_len]

    def _L1_xattn_ref(char_emb, subword_emb, Wq_c, bq_c, Wk_s, bk_s, Wv_s, bv_s, Wq_s, bq_s, Wk_c, bk_c, Wv_c, bv_c, Wg, bg):
        import jax, jax.numpy as jnp
        import numpy as np
        H = 128
        B = 8
        L_CHAR = 256
        L_SUB = 128

        def _linear(x, W, b):
            return jnp.einsum('blh,oh->blo', x, W) + b

        def _interp_linear(x, out_len):
            L_in = x.shape[1]
            pos = (jnp.arange(out_len, dtype=x.dtype) + 0.5) * (L_in / out_len) - 0.5
            pos = jnp.clip(pos, 0.0, L_in - 1)
            lo = jnp.floor(pos).astype(jnp.int32)
            hi = jnp.minimum(lo + 1, L_in - 1)
            w = (pos - lo.astype(x.dtype))[None, :, None]
            return x[:, lo] * (1 - w) + x[:, hi] * w
        h = char_emb.shape[-1]
        scale = 1.0 / jnp.sqrt(jnp.asarray(h, char_emb.dtype))
        Q_char = _linear(char_emb, Wq_c, bq_c)
        K_sub = _linear(subword_emb, Wk_s, bk_s)
        V_sub = _linear(subword_emb, Wv_s, bv_s)
        scores = jnp.einsum('bqh,bkh->bqk', Q_char, K_sub) * scale
        char2sub = jnp.einsum('bqk,bkh->bqh', jax.nn.softmax(scores, axis=-1), V_sub)
        Q_sub = _linear(subword_emb, Wq_s, bq_s)
        K_char = _linear(char_emb, Wk_c, bk_c)
        V_char = _linear(char_emb, Wv_c, bv_c)
        scores2 = jnp.einsum('bqh,bkh->bqk', Q_sub, K_char) * scale
        sub2char = jnp.einsum('bqk,bkh->bqh', jax.nn.softmax(scores2, axis=-1), V_char)
        L_char = char_emb.shape[1]
        if sub2char.shape[1] != L_char:
            sub2char = _interp_linear(sub2char, L_char)
        gate_in = jnp.concatenate([char2sub, sub2char], axis=-1)
        gate = jax.nn.sigmoid(jnp.einsum('blh,oh->blo', gate_in, Wg) + bg)
        return gate * char2sub + (1 - gate) * sub2char

    def _L1_ffn_ref(x, Wr, br, W1, b1, W2, b2):
        import jax, jax.numpy as jnp
        import numpy as np
        D_MODEL = 128
        D_FF = 512
        NUM_EXPERTS = 8
        B, N = (16, 128)
        scores = jnp.einsum('bh,he->be', x.mean(axis=1), Wr) + br
        top1 = jnp.argmax(scores, axis=-1)
        w1 = W1[top1]
        c1 = b1[top1]
        w2 = W2[top1]
        c2 = b2[top1]
        h = jax.nn.relu(jnp.einsum('bnh,bhf->bnf', x, w1) + c1[:, None, :])
        out = jnp.einsum('bnf,bfh->bnh', h, w2) + c2[:, None, :]
        return out
    x = _layernorm(x + _L0_attn_ref(x, L0_attn_Wq, L0_attn_Wk, L0_attn_Wv, L0_attn_Wo, L0_attn_scale), axis=-1)
    x = _layernorm(x + _L0_xattn_ref(x, ctx_1024, L0_xattn_ln_gamma, L0_xattn_ln_beta, L0_xattn_w_q, L0_xattn_w_kv, L0_xattn_w_out, L0_xattn_b_out, L0_xattn_gate), axis=-1)
    x = _layernorm(x + _L0_ffn_ref(x, L0_ffn_router_w, L0_ffn_gate_proj, L0_ffn_up_proj, L0_ffn_down_proj), axis=-1)
    x = _layernorm(x + _L1_attn_ref(x, L1_attn_W_in, L1_attn_conv_w, L1_attn_conv_b, L1_attn_A_param, L1_attn_dt_bias, L1_attn_W_out), axis=-1)
    x = _layernorm(x + _L1_xattn_ref(x, ctx_1024, L1_xattn_Wq_c, L1_xattn_bq_c, L1_xattn_Wk_s, L1_xattn_bk_s, L1_xattn_Wv_s, L1_xattn_bv_s, L1_xattn_Wq_s, L1_xattn_bq_s, L1_xattn_Wk_c, L1_xattn_bk_c, L1_xattn_Wv_c, L1_xattn_bv_c, L1_xattn_Wg, L1_xattn_bg), axis=-1)
    x = _layernorm(x + _L1_ffn_ref(x, L1_ffn_Wr, L1_ffn_br, L1_ffn_W1, L1_ffn_b1, L1_ffn_W2, L1_ffn_b2), axis=-1)
    return x

_drawn_inputs = setup_inputs


def setup_inputs(seed=0):
    import zlib

    import numpy as np

    out = dict(_drawn_inputs(seed))
    spreads = {'L0_xattn_ln_gamma': (1.0, 0.6),
     'L0_xattn_ln_beta': (0.0, 0.1),
     'L0_xattn_b_out': (0.0, 0.1),
     'L1_attn_conv_b': (0.0, 0.1)}
    factors = {'L0_attn_Wq': 8.0,
     'L0_attn_Wk': 8.0,
     'L0_ffn_router_w': 8.0,
     'L0_ffn_gate_proj': 8.0,
     'L0_ffn_up_proj': 8.0,
     'L0_ffn_down_proj': 8.0,
     'L1_attn_dt_bias': 64.0,
     'L1_xattn_Wq_c': 8.0,
     'L1_xattn_bq_c': 42.769,
     'L1_xattn_Wk_s': 8.0,
     'L1_xattn_bk_s': 64.0,
     'L1_xattn_Wq_s': 8.0,
     'L1_xattn_bq_s': 8.0,
     'L1_xattn_Wk_c': 8.0,
     'L1_xattn_bk_c': 64.0,
     'L1_xattn_bv_c': 5.561,
     'L1_xattn_Wg': 8.0,
     'L1_ffn_b1': 2.951,
     'L1_attn_A_param': 5.998,
     'L1_xattn_bg': 8.0}
    for name, (base, spread) in spreads.items():
        noise = np.random.default_rng([zlib.crc32(name.encode()), seed]).standard_normal(out[name].shape)
        drawn = base * np.exp(spread * noise) if base else spread * noise
        out[name] = jnp.asarray(drawn.astype(out[name].dtype))
    for name, factor in factors.items():
        out[name] = (out[name] * factor).astype(out[name].dtype)
    return out
```

```python
from contextlib import ExitStack

import numpy as np
import concourse.bass as bass
from concourse import mybir

F32 = mybir.dt.float32
BF16 = mybir.dt.bfloat16
I32 = mybir.dt.int32
U32 = mybir.dt.uint32
ALU = mybir.AluOpType
ACT = mybir.ActivationFunctionType
AX = mybir.AxisListType

NB = 32
HB = 16
NT = 39
EPS = 1e-5
NEG = -1e38
WE = 1152
WF = 1030

S_SCALE, S_GAMMA, S_BETA, S_GATE, S_DTB, S_AP = 0, 1, 2, 3, 4, 5
S_CW, S_CB = 6, 18
S_BQC, S_BKS, S_BVS, S_BQS, S_BKC, S_BVC, S_BG = 21, 22, 23, 24, 25, 26, 27
S_BR = 28
S_WR0, S_WR1 = 36, 44
S_N = 52

C_ID, C_MASK, C_TRI, C_ONE, C_MASKS = 0, 128, 256, 384, 512
C_E, C_DD = 640, 896
C_SEL = 1152
C_HM = C_SEL + 1024
C_I16 = C_HM + 16
C_E8 = C_I16 + 16
C_RST = C_E8 + 8
C_J = C_RST + 128
C_N = C_J + 40


def constants():
    c = np.zeros((128, C_N), np.float32)
    p = np.arange(128)
    c[:, C_ID:C_ID + 128] = np.eye(128)
    c[:, C_MASK:C_MASK + 128] = np.where(p[None, :] > p[:, None], NEG, 0.0)
    c[:, C_TRI:C_TRI + 128] = (p[:, None] < p[None, :])
    c[:, C_ONE:C_ONE + 128] = 1.0
    c[:, C_MASKS:C_MASKS + 128] = np.where(p[None, :] < p[:, None], NEG, 0.0)
    signs = np.array([[a, b, d] for a in (-1, 1) for b in (-1, 1) for d in (-1, 1)], np.float32)
    dirs = signs / np.linalg.norm(signs, axis=1, keepdims=True)
    for h in range(8):
        col = 128 * (h // 4) + 32 * (h % 4)
        for i in range(3):
            c[3 * h + i, C_E + col + i] = 1.0
            for j in range(3):
                c[3 * h + j, C_DD + col + i] = dirs[h, i] * dirs[h, j]
    for b in range(8):
        for h in range(16):
            c[16 * b + h, C_SEL + 128 * b + 8 * h:C_SEL + 128 * b + 8 * h + 8] = 1.0
    c[p, C_HM + p // 8] = 1.0
    c[p[:16], C_I16 + p[:16]] = 1.0
    c[:, C_E8:C_E8 + 8] = 8.0 - np.arange(8)
    c[:, C_RST:C_RST + 128] = (p % 16 != 0)
    c[:, C_J:C_J + 40] = np.arange(40)
    return c


class Prog:

    def __init__(self, nc, ctx):
        self.nc, self.ctx = nc, ctx
        self.q = {n: [] for n in ("pe", "dve", "act", "pool", "sp")}
        self.sems, self.count, self.seen = {}, {}, {}

    def add(self, eng, fn, wait, inc, step=1):
        waits = []
        for t in wait:
            if t is not None and self.seen.get((eng, t[0]), 0) < t[1]:
                self.seen[(eng, t[0])] = t[1]
                waits.append(t)
        if inc is not None:
            inc = (inc.split(".")[0] if step == 1 else inc) + "." + eng
        if inc is not None and inc not in self.sems:
            self.sems[inc] = self.ctx.enter_context(self.nc.semaphore(inc.replace(".", "_")))
            self.count[inc] = 0
        self.q[eng].append((waits, fn, inc, step))
        if inc is None:
            return None
        self.count[inc] += step
        return (inc, self.count[inc])

    def play(self, eng, e):
        for waits, fn, inc, step in self.q[eng]:
            for n, v in waits:
                e.wait_ge(self.sems[n], v)
            ins = fn(e)
            if inc is not None:
                ins.then_inc(self.sems[inc], step)


def build(nc, a, out, stop="F"):
    with ExitStack() as ctx:
        P = Prog(nc, ctx)

        def mm(o, lhsT, rhs, start=True, stop=True, wait=(), inc=None):
            return P.add("pe", lambda e: e.matmul(o, lhsT, rhs, start=start, stop=stop,
                                                  skip_group_check=True), wait, inc)

        def tp(o, i, wait=(), inc=None):
            return P.add("pe", lambda e: e.transpose(o, i, ident), wait, inc)

        def tt(o, x, y, op, wait=(), inc=None, eng="dve"):
            return P.add(eng, lambda e: e.tensor_tensor(o, x, y, op), wait, inc)

        def ts(o, x, s1, s2, op0, op1=None, wait=(), inc=None, eng="dve"):
            if op1 is None:
                return P.add(eng, lambda e: e.tensor_scalar(o, x, s1, None, op0), wait, inc)
            return P.add(eng, lambda e: e.tensor_scalar(o, x, s1, s2, op0, op1), wait, inc)

        def stt(o, x, s, y, op0, op1, wait=(), inc=None):
            return P.add("dve", lambda e: e.scalar_tensor_tensor(out=o, in0=x, scalar=s, in1=y, op0=op0, op1=op1),
                         wait, inc)

        def red(o, x, op, wait=(), inc=None, neg=False):
            return P.add("dve", lambda e: e.tensor_reduce(o, x, AX.X, op, negate=neg), wait, inc)

        def scan(o, x, y, wait=(), inc=None):
            return P.add("dve", lambda e: e.tensor_tensor_scan(o, x, y, 0.0, ALU.mult, ALU.add), wait, inc)

        def cp(o, x, wait=(), inc=None, eng="dve"):
            if eng == "act":
                return P.add("act", lambda e: e.activation(o, x, ACT.Copy), wait, inc)
            return P.add(eng, lambda e: e.tensor_copy(o, x), wait, inc)

        def rcp(o, x, wait=(), inc=None):
            return P.add("dve", lambda e: e.reciprocal(o, x), wait, inc)

        def act(o, x, f, wait=(), inc=None, bias=0.0, scale=1.0, accum=None):
            if accum is None:
                return P.add("act", lambda e: e.activation(o, x, f, bias=bias, scale=scale), wait, inc)
            return P.add("act", lambda e: e.activation(o, x, f, bias=bias, scale=scale, accum_out=accum), wait, inc)

        def fill(o, v, wait=(), inc=None, eng="dve"):
            return P.add(eng, lambda e: e.memset(o, v), wait, inc)

        def dma(o, x, wait=(), inc=None, eng="sp"):
            return P.add(eng, lambda e: e.dma_start(o, x), wait, inc, 16)

        top = [nc.sbuf_base + (-nc.sbuf_base) % 64]

        def at(name, cols, dt=F32, off=None):
            size = cols * (2 if dt == BF16 else 4)
            size += -size % 64
            if off is None:
                off = top[0]
                top[0] += size
            return nc.alloc_sbuf_tensor_at(name, [128, cols], dt, offset=off)

        def region(cols):
            r = top[0]
            top[0] += cols * 4
            return r

        X = at("X", NB * 128)[:, :].rearrange("p (b c) -> p b c", b=NB)
        r0 = top[0]
        XT = at("XT", NB * 128)[:, :]
        CT = at("CT", NB * 128)[:, :]
        KON = at("KON", C_N)[:, :]
        PAR = at("PAR", S_N + 64)[:, :]
        ident = KON[:, C_ID:C_ID + 128]
        identb = at("identb", 128, BF16)[:, :]
        maskb = at("maskb", 512, BF16)[:, :]
        masksb = at("masksb", 512, BF16)[:, :]
        trib = at("trib", 128, BF16)[:, :]
        oneb = at("oneb", 128, BF16)[:, :]
        r1 = region(8 * WE)
        KB = [at(f"KB{i}", 4096, off=r1 + 16384 * i)[:, :].rearrange("p (t b j s) -> p t b j s", t=2, b=4, j=4)
              for i in range(2)]
        WCt = at("WCt", 8 * WE, off=r1)[:, :]
        r2 = region(12288)
        QB = [at(f"QB{i}", 4096, off=r2 + 16384 * i)[:, :].rearrange("p (h t) -> p h t", h=16) for i in range(2)]
        VB = [at(f"VB{i}", 2048, off=r2 + 32768 + 8192 * i)[:, :].rearrange("p (b d) -> p b d", b=2) for i in range(2)]
        WFt = at("WFt", 8 * WF, off=r2)[:, :]
        r3 = region(2048 + 1024 + 1024)
        AH = at("AH", 2048, off=r3)[:, :].rearrange("p (h c) -> p h c", h=16)
        WVB = at("WVB", 1024, off=r3 + 8192)[:, :]
        WOB = at("WOB", 1024, off=r3 + 12288)[:, :].rearrange("p (k c) -> p k c", k=8)
        r4 = region(256 * 3 + 256 + 2 * 1024 + 4 * 256)
        WQA = at("WQA", 256, off=r4)[:, :].rearrange("p (t c) -> p t c", t=2)
        WKA = at("WKA", 256, off=r4 + 1024)[:, :].rearrange("p (t c) -> p t c", t=2)
        WVA = at("WVA", 256, off=r4 + 2048)[:, :]
        WOA = at("WOA", 256, off=r4 + 3072)[:, :].rearrange("p (t c) -> p t c", t=2)
        QA = [at(f"QA{i}", 1024, off=r4 + 4096 + 4096 * i)[:, :].rearrange("p (t n) -> p t n", t=2) for i in range(2)]
        VA = [at(f"VA{i}", 256, off=r4 + 12288 + 1024 * i)[:, :] for i in range(4)]
        PP = [at(f"PP{i}", 512)[:, :].rearrange("p (j s) -> p j s", j=4) for i in range(3)]
        PT = [at(f"PT{i}", 512)[:, :].rearrange("p (j s) -> p j s", j=4) for i in range(3)]
        o_ot = top[0]
        OT = [at(f"OT{i}", 1024)[:, :] for i in range(2)]
        SM = at("SM", 16)[:, :].rearrange("p (k j) -> p k j", k=4)
        MX = at("MX", 16)[:, :].rearrange("p (k j) -> p k j", k=4)
        RS = at("RS", 16)[:, :].rearrange("p (k j) -> p k j", k=4)
        ST = [at(f"ST{i}", 8)[:, :] for i in range(8)]
        MV = [at(f"MV{i}", 4)[:, :] for i in range(8)]
        XH = [at(f"XH{i}", 128)[:, :] for i in range(4)]
        SW = at("SW", 16)[:, :]
        BT = at("BT", 128)[:, :]
        BTZ = at("BTZ", 128)[:, :]
        RTE = at("RTE", 360)[:, :]

        PS = [ctx.enter_context(nc.psum_tensor(f"bank{i}", [128, 512], F32)) for i in range(8)]
        bank = [t[:, :] for t in PS]

        rel = {}

        def last(key):
            return rel.get(key, [])

        t_par = dma(PAR[:, 0:S_N], a["par"], inc="ld.par")
        t_kon = dma(KON, a["kon"], inc="ld.kon", eng="act")
        t_wk = dma(WKA, a["wk"], inc="ld.wk")
        t_wv = dma(WVA, a["wv"], inc="ld.wv", eng="act")
        t_wo = dma(WOA, a["wo"], inc="ld.wo", eng="act")
        WQR = at("WQR", 128, off=r3 + 12288)[:, :]
        t_wqr = dma(WQR[0:24, :], a["wqr"], inc="ld.wqr")
        t_xt, t_x = [], []
        for c in range(8):
            t_xt.append(dma(XT[:, 512 * c:512 * c + 512], a["xT"][:, 512 * c:512 * c + 512], inc=f"ld.xt{c}",
                            eng="sp"))
        for c in range(2):
            t_x.append(dma(X[:, 16 * c:16 * c + 16, :], a["x"][:, 16 * c:16 * c + 16, :], inc=f"ld.x{c}", eng="act"))
        WQT = at("WQT", 2048, off=r2)[0:64, :].rearrange("p (k c) -> p k c", k=16)
        WKT = at("WKT", 2048, off=r2 + 8192)[0:64, :].rearrange("p (k c) -> p k c", k=16)
        t_wqt = dma(WQT, a["wqT"], inc="ld.wqt", eng="act")
        t_wkt = dma(WKT, a["wkT"], inc="ld.wkt", eng="act")
        t_ct = dma(CT, a["cT"], inc="ld.ct")
        t_bo = dma(BT, a["bo"], inc="ld.bo")

        cp(identb, ident, wait=[t_kon], inc="k.bf")
        for j in range(4):
            cp(maskb[:, 128 * j:128 * j + 128], KON[:, C_MASK:C_MASK + 128])
            cp(masksb[:, 128 * j:128 * j + 128], KON[:, C_MASKS:C_MASKS + 128])
        cp(trib, KON[:, C_TRI:C_TRI + 128])
        t_bf = cp(oneb, KON[:, C_ONE:C_ONE + 128], inc="k.bf")
        t_sw = fill(SW[:, 0:1], -0.5, inc="k.sw", eng="pool")
        t_kb = [fill(KB[0], 0.0, inc="k.kb", eng="dve"), fill(KB[1], 0.0, inc="k.kb1", eng="pool")]
        MF = at("MF", 256, off=r3 + 8192 + 1024)[:, :]
        t_mf = stt(MF[0:24, :], KON[0:24, C_E:C_E + 256], PAR[0:24, S_SCALE:S_SCALE + 1],
                   KON[0:24, C_DD:C_DD + 256], ALU.mult, ALU.add, wait=[t_par, t_kon], inc="A.mf")
        t = mm(bank[7][:, 0:256], WQR[0:24, :], MF[0:24, :], wait=[t_mf, t_wqr], inc="A.wq")
        t_wq = cp(WQA, bank[7][:, 0:256].rearrange("p (t c) -> p t c", t=2), wait=[t], inc="A.wqc")
        rel["Y"] = [t_wq]
        t_wvb = dma(WVB, a["wvb"], wait=[t], inc="ld.wvb")
        t_wob = dma(WOB, a["wob"], wait=[t], inc="ld.wob")

        nln = [0]

        def ln_stats(z, wait):
            k = nln[0] % 8
            nln[0] += 1
            t = P.add("dve", lambda e: e.bn_stats(ST[k][:, 0:6], z), list(wait) + last(("ln", k)), "ln.st")
            t = P.add("dve", lambda e: e.bn_aggr(MV[k][:, 0:2], ST[k][:, 0:6]), [t], "ln.ag")
            t = ts(MV[k][:, 2:3], MV[k][:, 1:2], EPS, None, ALU.add, wait=[t], inc="ln.ep")
            t = tt(MV[k][:, 3:4], MV[k][:, 2:3], SW[:, 0:1], ALU.pow, wait=[t, t_sw], inc="ln.pw", eng="pool")
            return k, t

        def ln_apply(o, z, st, wait, inc):
            k, t = st
            t = ts(o, z, MV[k][:, 0:1], MV[k][:, 3:4], ALU.subtract, ALU.mult, wait=list(wait) + [t], inc=inc)
            rel[("ln", k)] = [t]
            return t

        def sm_max(ph, u, sb, t_s):
            return red(MX[:, u % 4, :], sb, ALU.max, wait=[t_s] + last(("MX", u % 4)), inc=ph + ".max", neg=True)

        def sm_exp(ph, u, sb, t_m):
            for j in range(4):
                t = act(PP[u % 3][:, j, :], sb[:, j, :], ACT.Exp, bias=MX[:, u % 4, j:j + 1],
                        accum=SM[:, u % 4, j:j + 1],
                        wait=([t_m] + last(("PP", u % 3)) + last(("SM", u % 4))) if j == 0 else (),
                        inc=ph + ".exp")
            rel[("MX", u % 4)] = [t]
            return t

        def sm_rec(ph, u, t_e):
            t = rcp(RS[:, u % 4, :], SM[:, u % 4, :], wait=[t_e] + last(("RS", u % 4)), inc=ph + ".rec")
            rel[("SM", u % 4)] = [t]
            return t

        def sm_nrm(ph, u, t_r):
            t = tt(PP[u % 3], PP[u % 3], RS[:, u % 4, :].unsqueeze(2).broadcast_to((128, 4, 128)), ALU.mult,
                   wait=[t_r], inc=ph + ".nrm", eng="pool")
            rel[("RS", u % 4)] = [t]
            return t

        def sm_tp(ph, u, tb, t_n, free):
            for j in range(4):
                t = tp(tb[:, 128 * j:128 * j + 128], PP[u % 3][:, j, :], wait=([t_n] + free) if j == 0 else (),
                       inc=ph + ".tp" if j == 3 else None)
            rel[("PP", u % 3)] = [t]
            return t

        nM = [0]

        def m_bank():
            k = 5 + nM[0] % 2
            nM[0] += 1
            return k

        tA = {}

        def A_proj(c):
            for t in range(2):
                m = m_bank()
                g = mm(bank[m], WQA[:, t, :], XT[:, 512 * c:512 * c + 512], wait=[t_wq, t_xt[c]] + last(("M", m)),
                       inc="A.q")
                g = cp(QA[c % 2][:, t, :], bank[m], wait=[g] + last(("QA", c % 2)), inc="A.qc", eng="act")
                rel[("M", m)] = [g]
                tA["q", c, t] = g
                m = m_bank()
                g = mm(bank[m], WKA[:, t, :], XT[:, 512 * c:512 * c + 512], wait=[t_wk] + last(("M", m)), inc="A.k")
                for j in range(4):
                    r = slice(32 * j, 32 * j + 32)
                    g = cp(KB[c % 2][r, t, :, j, :], bank[m][r, :].rearrange("p (b s) -> p b s", b=4),
                           wait=([g, t_kb[c % 2]] + last(("KB", c % 2))) if j == 0 else (),
                           inc="A.kc", eng="dve")
                rel[("M", m)] = [g]
                tA["k", c, t] = g

        def A_v(b):
            m = m_bank()
            g = mm(bank[m][:, 0:256], XT[:, 128 * b:128 * b + 128], WVA, wait=[t_wv, t_xt[b // 4]] + last(("M", m)),
                   inc="A.v")
            rel[("XT", b)] = [g]
            g = cp(VA[b % 4], bank[m][:, 0:256], wait=[g] + last(("VA", b % 4)), inc="A.vc", eng="act")
            rel[("M", m)] = [g]
            tA["v", b] = g

        def A_S(u):
            b, t = u // 2, u % 2
            c = b // 4
            sb = bank[u % 2]
            mm(sb, identb, maskb, start=True, stop=False,
               wait=[t_bf, tA["q", c, t], tA["k", c, t]] + last(("S", u % 2)))
            g = mm(sb, QA[c % 2][:, t, 128 * (b % 4):128 * (b % 4) + 128], KB[c % 2][:, t, b % 4, :, :],
                   start=False, stop=True, inc="A.s")
            if u % 8 == 7:
                rel[("QA", c % 2)] = [g]
                rel[("KB", c % 2)] = [g]
            s3 = sb.rearrange("p (j s) -> p j s", j=4)
            g = sm_max("A", u, s3, g)
            g = sm_exp("A", u, s3, g)
            rel[("S", u % 2)] = [g]
            tA["e", u] = g

        def A_norm(u):
            tA["n", u] = sm_nrm("A", u, sm_rec("A", u, tA["e", u]))

        def A_T(u):
            tb = bank[2 + u % 2]
            g = sm_tp("A", u, tb, tA["n", u], last(("T", u % 2)))
            g = cp(PT[u % 3], tb.rearrange("p (j s) -> p j s", j=4), wait=[g] + last(("PT", u % 3)), inc="A.pt",
                   eng="dve" if u % 2 else "act")
            rel[("T", u % 2)] = [g]
            tA["pt", u] = g

        def A_AV(u):
            b, t = u // 2, u % 2
            for j in range(4):
                g = mm(bank[4][32 * j:32 * j + 32, 128 * t:128 * t + 128],
                       VA[b % 4][:, 128 * t + 32 * j:128 * t + 32 * j + 32], PT[u % 3][:, j, :],
                       wait=([tA["pt", u], tA["v", b]] + (last("O") if t == 0 else [])) if j == 0 else (),
                       inc="A.av" if j == 3 else None)
            rel[("PT", u % 3)] = [g]
            if t == 1:
                rel[("VA", b % 4)] = [g]
                g = cp(OT[b % 2][:, 0:256], bank[4][:, 0:256], wait=[g] + last(("OT", b % 2)), inc="A.ot", eng="dve")
                rel["O"] = [g]
                tA["ot", b] = g

        def A_out(b):
            for t in range(2):
                g = mm(bank[7][:, 0:128], OT[b % 2][:, 128 * t:128 * t + 128], WOA[:, t, :], start=(t == 0),
                       stop=(t == 1), wait=([tA["ot", b], t_wo] + last("Y")) if t == 0 else (),
                       inc="A.y" if t else None)
            rel[("OT", b % 2)] = [g]
            g = tt(X[:, b, :], bank[7][:, 0:128], X[:, b, :], ALU.add, wait=[g, t_x[b // 16]], inc="A.z")
            rel["Y"] = [g]
            tA["ln", b] = ln_stats(X[:, b, :], [g])

        def A_ln(b):
            g = ln_apply(X[:, b, :], X[:, b, :], tA["ln", b], [], "A.x1")
            tA["x1", b] = g
            tA["ln2", b] = ln_stats(X[:, b, :], [g])

        def A_ln2(b):
            g = ln_apply(XH[b % 4], X[:, b, :], tA["ln2", b], last(("XH", b % 4)), "A.xh")
            tA["xh", b] = g
            tA["xb", b] = tt(X[:, b, :], X[:, b, :], BT, ALU.add, wait=[g, t_bt], inc="A.xb", eng="pool")

        def A_xn(b):
            m = m_bank()
            g = tp(bank[m][:, 0:128], XH[b % 4], wait=[tA["xh", b]] + last(("M", m)), inc="A.xt")
            rel[("XH", b % 4)] = [g]
            tA["xt_pe"] = g
            g = ts(XT[:, 128 * b:128 * b + 128], bank[m][:, 0:128], PAR[:, S_GAMMA:S_GAMMA + 1],
                   PAR[:, S_BETA:S_BETA + 1], ALU.mult, ALU.add, wait=[g] + last(("XT", b)), inc="A.xn")
            rel[("M", m)] = [g]
            tA["xn", b] = g

        A_proj(0)
        A_v(0)
        t_tg = act(PAR[:, S_N:S_N + 1], PAR[:, S_GATE:S_GATE + 1], ACT.Tanh, wait=[t_par], inc="B.tg")
        t_bt = ts(BT, BT, PAR[:, S_N:S_N + 1], None, ALU.mult, wait=[t_tg, t_bo], inc="B.bt")
        t_wob = ts(WOB, WOB, PAR[:, S_N:S_N + 1], None, ALU.mult, wait=[t_tg, t_wob], inc="B.wob", eng="pool")

        def B_ah(k):
            m = m_bank()
            for j in range(4):
                h = 4 * k + j
                g = mm(bank[m][:, 128 * j:128 * j + 128], WQT[:, h, :], WKT[:, h, :],
                       wait=([t_wqt, t_wkt] + last(("M", m))) if j == 0 else (), inc="B.ah" if j == 3 else None)
            rel["WQT"] = [g]
            g = act(AH[:, 4 * k:4 * k + 4, :], bank[m].rearrange("p (h c) -> p h c", h=4), ACT.Copy, scale=0.125,
                    wait=[g], inc="B.ahc")
            rel[("M", m)] = [g]
            tA["ah", k] = g

        NU = 2 * NB
        for i in range(NU + 16):
            if i < NU:
                A_S(i)
            if 1 <= i <= NU:
                A_norm(i - 1)
            if i < NU:
                if i % 2 == 0 and i // 2 + 1 < NB:
                    A_v(i // 2 + 1)
                if i % 8 == 4 and i // 8 + 1 < 8:
                    A_proj(i // 8 + 1)
            if i in (3, 9, 13, 19):
                B_ah((3, 9, 13, 19).index(i))
            if 2 <= i < NU + 2:
                A_T(i - 2)
            if 3 <= i < NU + 3:
                A_AV(i - 3)
            for fn, lag in ((A_xn, 10), (A_ln2, 8), (A_ln, 6), (A_out, 5)):
                j = i - lag
                if j >= 0 and j % 2 == 0 and j // 2 < NB:
                    fn(j // 2)

        tA["end"] = tA["kc_end"] = tA["xn", NB - 1]
        tA["end_pe"] = tA["xt_pe"]
        if stop == "A":
            finish(P, nc, dma, X, out, [tA["xb", b] for b in range(NB)])
            return

        tB = {}

        def B_q(c, k):
            m = m_bank()
            for j in range(2):
                h = 2 * k + j
                g = mm(bank[m][:, 256 * j:256 * j + 256], AH[:, h, :], XT[:, 256 * c:256 * c + 256],
                       wait=([tA["ah", h // 4], tA["xn", 2 * c], tA["xn", 2 * c + 1]] + last(("M", m)))
                       if j == 0 else (), inc="B.q" if j else None)
            g = cp(QB[c % 2][:, 2 * k:2 * k + 2, :], bank[m].rearrange("p (h t) -> p h t", h=2),
                   wait=[g] + last(("QB", c % 2)) + last("WQT"), inc="B.qc", eng="act" if k % 2 else "dve")
            rel[("M", m)] = [g]
            tB["q", c, k] = g

        def B_v(c, k):
            m = m_bank()
            b = 2 * c + k // 2
            g = mm(bank[m], CT[:, 128 * b:128 * b + 128], WVB[:, 512 * (k % 2):512 * (k % 2) + 512],
                   wait=[t_ct, t_wvb] + last(("M", m)), inc="B.v")
            g = cp(VB[c % 2][:, k // 2, 512 * (k % 2):512 * (k % 2) + 512], bank[m],
                   wait=[g] + last(("VB", c % 2)), inc="B.vc", eng="act" if k % 2 else "dve")
            rel[("M", m)] = [g]
            tB["v", c, k] = g

        def B_S(u):
            c, bb, hq = u // 8, (u // 4) % 2, u % 4
            b = 2 * c + bb
            sb = bank[u % 2]
            for j in range(4):
                h = 4 * hq + j
                g = mm(sb[:, 128 * j:128 * j + 128], QB[c % 2][:, h, 128 * bb:128 * bb + 128],
                       CT[:, 128 * b:128 * b + 128],
                       wait=([t_ct, tB["q", c, 2 * hq], tB["q", c, 2 * hq + 1]] + last(("S", u % 2)))
                       if j == 0 else (), inc="B.s" if j == 3 else None)
            if u % 8 == 7:
                rel[("QB", c % 2)] = [g]
            s3 = sb.rearrange("p (j s) -> p j s", j=4)
            g = sm_max("B", u, s3, g)
            g = sm_exp("B", u, s3, g)
            rel[("S", u % 2)] = [g]
            tB["e", u] = g

        def B_norm(u):
            tB["n", u] = sm_nrm("B", u, sm_rec("B", u, tB["e", u]))

        def B_T(u):
            tb = bank[2 + u % 2]
            g = sm_tp("B", u, tb, tB["n", u], last(("T", u % 2)))
            g = cp(PT[u % 3], tb.rearrange("p (j s) -> p j s", j=4), wait=[g] + last(("PT", u % 3)), inc="B.pt",
                   eng="dve")
            rel[("T", u % 2)] = [g]
            tB["pt", u] = g

        def B_AV(u):
            c, bb, hq = u // 8, (u // 4) % 2, u % 4
            b = 2 * c + bb
            for j in range(4):
                h = 4 * hq + j
                g = mm(bank[4][64 * (j % 2):64 * (j % 2) + 64, 128 * (j // 2):128 * (j // 2) + 128],
                       VB[c % 2][:, bb, 64 * h:64 * h + 64], PT[u % 3][:, j, :],
                       wait=([tB["pt", u], tB["v", c, 2 * bb + hq // 2]] + last("O")) if j == 0 else (),
                       inc="B.av" if j == 3 else None)
            rel[("PT", u % 3)] = [g]
            tB["av_pe"] = g
            if u % 8 == 7:
                rel[("VB", c % 2)] = [g]
            g = cp(OT[b % 2][:, 256 * hq:256 * hq + 256], bank[4][:, 0:256],
                   wait=[g] + (last(("OT", b % 2)) if hq == 0 else []), inc="B.ot", eng="dve")
            rel["O"] = [g]
            tB["ot", b] = g

        def B_out(b):
            for k in range(8):
                g = mm(bank[7][:, 0:128], OT[b % 2][:, 128 * k:128 * k + 128], WOB[:, k, :], start=(k == 0),
                       stop=(k == 7), wait=([tB["ot", b], t_wob] + last("Y")) if k == 0 else (),
                       inc="B.y" if k == 7 else None)
            rel[("OT", b % 2)] = [g]
            tB["y_pe"] = g
            g = tt(X[:, b, :], bank[7][:, 0:128], X[:, b, :], ALU.add, wait=[g, tA["xb", b]], inc="B.z")
            rel["Y"] = [g]
            tB["ln", b] = ln_stats(X[:, b, :], [g])

        def B_ln(b):
            tB["x2", b] = ln_apply(X[:, b, :], X[:, b, :], tB["ln", b], [], "B.x2")

        def B_tp(b):
            m = m_bank()
            g = tp(bank[m][:, 0:128], X[:, b, :], wait=[tB["x2", b]] + last(("M", m)), inc="B.xt")
            g = cp(XH[b % 4], bank[m][:, 0:128], wait=[g] + last(("XH", b % 4)), inc="B.xtc", eng="act")
            rel[("M", m)] = [g]
            tB["xt", b] = g

        SC = at("SC", 256)[:, :].rearrange("p (b e) -> p b e", e=8)

        def B_route(b):
            m = m_bank()
            g = mm(bank[m][:, 0:8], XH[b % 4], PAR[:, S_WR0:S_WR0 + 8], wait=[tB["xt", b]] + last(("M", m)),
                   inc="B.r")
            rel[("XH", b % 4)] = [g]
            g = cp(SC[:, b, :], bank[m][:, 0:8], wait=[g], inc="B.rc")
            rel[("M", m)] = [g]
            tB["r", b] = g

        def jobs(c):
            return [lambda k=k: B_q(c, k) for k in range(8)] + [lambda k=k: B_v(c, k) for k in range(4)]

        def jobs_mixed(c):
            q = [lambda k=k: B_q(c, k) for k in range(8)]
            v = [lambda k=k: B_v(c, k) for k in range(4)]
            return q[0:2] + v[0:1] + q[2:4] + v[1:2] + q[4:6] + v[2:3] + q[6:8] + v[3:4]

        RW = [at(f"RW{k}", 128, off=r4 + 512 * k)[:, :] for k in range(10)]
        POS = [at(f"POS{h}", 32, I32, off=r4 + 5120 + 128 * h)[:, :].rearrange("p (k b) -> p k b", k=2)
               for h in range(2)]
        WR = [at(f"WR{h}", 32, off=r4 + 5376 + 128 * h)[:, :].rearrange("p (k b) -> p k b", k=2) for h in range(2)]
        TE = [at(f"TE{h}", 40, I32, off=r4 + 5632 + 192 * h)[:, :] for h in range(2)]
        RV = at("RV", 16 * 12, off=r4 + 6016)[:, :].rearrange("p (k b) -> p k b", k=12)
        MB = at("MB", 128, BF16, off=r4 + 6784)[:, :]
        GA = [at(f"GA{k}", 256, off=r4 + 7168 + 1024 * k)[:, :].rearrange("p (k c) -> p k c", k=2) for k in range(4)]
        XS = [at(f"XS{k}", 128, off=r4 + 11264 + 512 * k)[:, :] for k in range(4)]
        YS = [at(f"YS{k}", 128, off=r4 + 13312 + 512 * k)[:, :] for k in range(4)]
        XST = [at(f"XST{k}", 128, off=r4 + 15360 + 512 * k)[:, :] for k in range(2)]
        NTI = at("NTI", 8, I32)[:, :]
        xs = [nc.dram_tensor(f"xs{h}", [NT * 128, 128], F32, kind="Internal").ap() for h in range(2)]
        ys = [nc.dram_tensor(f"ys{h}", [NT * 128, 128], F32, kind="Internal").ap() for h in range(2)]
        t_z = fill(BTZ, 0.0, inc="k.z", eng="pool")
        t_xz = [dma(xs[h].rearrange("(t p) c -> p t c", p=128), BTZ.unsqueeze(1).broadcast_to((128, NT, 128)),
                    wait=[t_z], inc=f"C.xz{h}", eng="act") for h in range(2)]
        tC = {}

        def route(h):
            s = SC[:, HB * h:HB * h + HB, :]

            def v3(x):
                return x.rearrange("p (b e) -> p b e", e=8)

            def wide(x):
                return x.unsqueeze(2).broadcast_to((128, HB, 8))

            e8 = KON[:, C_E8:C_E8 + 8].unsqueeze(1).broadcast_to((128, HB, 8))
            p, oh1, oh2, t1, t2 = (v3(RW[k]) for k in range(5))
            m1, mp, m2, mv, mv2, den = (RV[:, k, :] for k in range(6))
            n = "R"
            g = red(m1, s, ALU.max, wait=[tB["r", HB * h + HB - 1], tA["end"]] + last("route"), inc=n)
            yield
            g = tt(t1, s, wide(m1), ALU.subtract, wait=[g], inc=n)
            yield
            g = act(p, t1, ACT.Exp, wait=[g], inc=n)
            yield
            g = red(mp, p, ALU.max, wait=[g], inc=n)
            yield
            for oh, m, v in ((oh1, mp, mv), (oh2, m2, mv2)):
                src = p if oh is oh1 else t1
                if oh is oh2:
                    g = stt(RW[3], RW[1], -2.0, RW[0], ALU.mult, ALU.add, wait=[g], inc=n)
                    yield
                    g = red(m, t1, ALU.max, wait=[g], inc=n)
                    yield
                g = tt(t2, src, wide(m), ALU.is_equal, wait=[g], inc=n)
                yield
                g = tt(t2, t2, e8, ALU.mult, wait=[g], inc=n)
                yield
                g = red(v, t2, ALU.max, wait=[g], inc=n)
                yield
                g = tt(oh, t2, wide(v), ALU.is_equal, wait=[g], inc=n)
                yield
            g = tt(MB, RW[1], RW[2], ALU.add, wait=[g], inc=n)
            m = m_bank()
            mm(bank[m][:, 0:128], trib, MB, wait=[g, t_bf] + last(("M", m)))
            k = mm(bank[m][:, 128:256], oneb, MB, inc="R.mm")
            excl, cnt, incl, off = RW[5], RW[6], RW[7], RW[8]

            def eb(x):
                return x.rearrange("p (e b) -> p e b", b=HB)

            g = cp(excl, bank[m][:, 0:128], wait=[g, k], inc=n)
            g = cp(eb(cnt), bank[m][:, 128:256].rearrange("p (b e) -> p e b", e=8), wait=[g], inc=n)
            rel[("M", m)] = [g]
            yield
            g = tt(den, mp, m2, ALU.add, wait=[g], inc=n)
            g = rcp(RV[:, 6, :], den, wait=[g], inc=n)
            yield
            g = tt(WR[h][:, 0, :], mp, RV[:, 6, :], ALU.mult, wait=[g], inc=n)
            g = tt(WR[h][:, 1, :], m2, RV[:, 6, :], ALU.mult, wait=[g], inc=n)
            yield
            g = scan(incl, KON[:, C_RST:C_RST + 128], cnt, wait=[g], inc=n)
            yield
            g = tt(off, incl, cnt, ALU.subtract, wait=[g], inc=n)
            yield
            nt, tend, tst = (RV[:, k, 0:8] for k in (7, 8, 9))
            g = ts(NTI, eb(incl)[:, :, HB - 1], 127.0, None, ALU.add, wait=[g], inc=n)
            yield
            g = ts(NTI, NTI, 7, None, ALU.logical_shift_right, wait=[g], inc=n)
            g = cp(nt, NTI, wait=[g], inc=n)
            yield
            g = scan(tend, KON[:, C_ONE:C_ONE + 8], nt, wait=[g], inc=n)
            g = tt(tst, tend, nt, ALU.subtract, wait=[g], inc=n)
            yield
            g = ts(tst, tst, 128.0, None, ALU.mult, wait=[g], inc=n)
            g = tt(eb(off), eb(off), tst.unsqueeze(2).broadcast_to((128, 8, HB)), ALU.add, wait=[g], inc=n)
            yield
            g = tt(v3(excl), v3(excl), off.rearrange("p (e b) -> p b e", b=HB), ALU.add, wait=[g], inc=n)
            yield
            for k, oh in enumerate((oh1, oh2)):
                g = tt(t1, oh, v3(excl), ALU.mult, wait=[g], inc=n)
                yield
                g = red(RV[:, 10, :], t1, ALU.add, wait=[g], inc=n)
                g = cp(POS[h][:, k, :], RV[:, 10, :], wait=[g], inc=n)
                yield
            tC["pos", h] = g
            te = RTE[0:1, 0:NT * 8].rearrange("p (j e) -> p j e", e=8)
            g = tt(te, KON[0:1, C_J:C_J + NT].unsqueeze(2).broadcast_to((1, NT, 8)),
                   tend[0:1, :].unsqueeze(1).broadcast_to((1, NT, 8)), ALU.is_ge, wait=[g], inc=n)
            yield
            g = red(RTE[0:1, 320:320 + NT], te, ALU.add, wait=[g], inc=n)
            yield
            g = ts(TE[h][0:1, 0:NT], RTE[0:1, 320:320 + NT], 7.0, None, ALU.min, wait=[g], inc=n)
            tC["te", h] = g
            rel["route"] = [g]
            yield

        def scatter(h):
            for b in range(HB * h, HB * h + HB):
                for k in range(2):
                    idx = POS[h][:, k, b - HB * h:b - HB * h + 1]
                    tC["sc", h] = P.add("pool", lambda e, idx=idx, b=b: e.indirect_dma_start(
                        xs[h], bass.IndirectOffsetOnAxis(ap=idx, axis=0), X[:, b, :], None),
                        [tC["pos", h], tB["x2", b], t_xz[h]], f"C.sc{h}", 16)
                    yield

        t_bend = []
        for j in jobs(0):
            j()
        NU = 4 * NB
        todo = []

        def steps(gens):
            for g in gens:
                yield from g()

        t_wc = dma(WCt, a["we"], wait=[tA["end_pe"], tA["end"]], inc="ld.wc")
        bg = steps([lambda: route(0), lambda: scatter(0)])
        for i in range(NU + 14):
            if i < NU:
                B_S(i)
            if 1 <= i <= NU:
                B_norm(i - 1)
            if i < NU:
                if i % 8 == 0 and i // 8 + 1 < NB // 2:
                    todo = jobs_mixed(i // 8 + 1)
                n = 2 if i % 2 == 0 else 1
                for _ in range(n):
                    if todo:
                        todo.pop(0)()
            if 2 <= i < NU + 2:
                B_T(i - 2)
            if 3 <= i < NU + 3:
                B_AV(i - 3)
            for fn, lag in ((B_route, 11), (B_tp, 10), (B_ln, 8), (B_out, 7)):
                j = i - lag
                if j >= 0 and j % 4 == 0 and j // 4 < NB:
                    fn(j // 4)
            if i > 4 * HB + 8:
                next(bg, None)
                next(bg, None)
        for _ in bg:
            pass

        if stop == "B":
            finish(P, nc, dma, X, out, [tB["x2", b] for b in range(NB)])
            return

        WS = [at(f"WS{k}", WE, off=r3 + 4608 * k)[:, :] for k in range(3)]
        HS = [at(f"HS{k}", 384, off=o_ot + 1536 * k)[:, :] for k in range(2)]
        AC = [at(f"AC{k}", 384, off=o_ot + 3072 + 1536 * k)[:, :] for k in range(2)]
        b_end = [tB["r", NB - 1], tB["ot", NB - 1], tB["y_pe"]]
        regs = {}

        def staged(o, w, width, idx, wait, inc):
            def fn(e):
                if "r" not in regs:
                    regs["r"] = e.alloc_register("expert")
                e.reg_load(regs["r"], idx)
                v = e.snap(regs["r"], min_val=0, max_val=7)
                return e.tensor_copy(o, w[:, bass.ds(v * width, width)])
            return P.add("dve", fn, wait, inc)

        def C_load(h, j):
            k = j % 4
            tC["xs", h, j] = dma(XS[k], xs[h][128 * j:128 * j + 128, :],
                                 wait=[tC["sc", h], tA["end"], tA["end_pe"]] + last(("XS", k)), inc=f"C.xs{k}")

        def C_T(h, j):
            m = m_bank()
            g = tp(bank[m][:, 0:128], XS[j % 4], wait=[tC["xs", h, j]] + last(("M", m)), inc="C.t")
            rel[("XS", j % 4)] = [g]
            g = cp(XST[j % 2], bank[m][:, 0:128], wait=[g] + last(("XST", j % 2)), inc="C.tc", eng="act")
            rel[("M", m)] = [g]
            tC["xt", h, j] = g
            tC["ws", h, j] = staged(WS[j % 3], WCt, WE, TE[h][0:1, j:j + 1],
                                    [tC["te", h], t_wc] + last(("WS", j % 3)) + b_end, "C.ws")

        def C_GU(h, j):
            for u in range(2):
                bk = 1 + 2 * u + j % 2
                for f in range(3):
                    g = mm(bank[bk][:, 128 * f:128 * f + 128], WS[j % 3][:, 384 * u + 128 * f:384 * u + 128 * f + 128],
                           XST[j % 2], wait=([tC["xt", h, j], tC["ws", h, j]] + last(("GU", bk))) if f == 0 else (),
                           inc="C.gu" if f == 2 else None)
                if u == 0:
                    s = act(HS[j % 2], bank[bk][:, 0:384], ACT.Silu, wait=[g] + last(("HS", j % 2)), inc="C.si")
                    rel[("GU", bk)] = [s]
            rel[("XST", j % 2)] = [g]
            g = tt(AC[j % 2], HS[j % 2], bank[3 + j % 2][:, 0:384], ALU.mult, wait=[s, g] + last(("AC", j % 2)),
                   inc="C.ac")
            rel[("GU", 3 + j % 2)] = [g]
            rel[("HS", j % 2)] = [g]
            tC["ac", h, j] = g

        def C_D(h, j):
            for f in range(3):
                g = mm(bank[7][:, 0:128], AC[j % 2][:, 128 * f:128 * f + 128],
                       WS[j % 3][:, 768 + 128 * f:768 + 128 * f + 128], start=(f == 0), stop=(f == 2),
                       wait=([tC["ac", h, j]] + last("CY")) if f == 0 else (), inc="C.d" if f == 2 else None)
            rel[("WS", j % 3)] = [g]
            rel[("AC", j % 2)] = [g]
            tC["d_pe"] = g
            k = j % 4
            g = cp(YS[k], bank[7][:, 0:128], wait=[g] + last(("YS", k)), inc="C.yc", eng="act")
            rel["CY"] = [g]
            tC["y_act"] = g
            g = dma(ys[h][128 * j:128 * j + 128, :], YS[k], wait=[g], inc=f"C.ys{k}")
            rel[("YS", k)] = [g]
            tC["ys", h, k] = g

        rel["DT"], rel["CY"] = last(("S", 0)), last("Y")
        for k, key in ((1, ("S", 1)), (2, ("T", 0)), (3, ("T", 1)), (4, "O")):
            rel[("GU", k)] = last(key)

        def experts(h, beside, late=()):
            for i in range(NT + 5):
                if i < NT:
                    C_load(h, i)
                if 2 <= i < NT + 2:
                    C_T(h, i - 2)
                if 3 <= i < NT + 3:
                    C_GU(h, i - 3)
                if 4 <= i < NT + 4:
                    C_D(h, i - 4)
                beside()
            for f in late:
                f(i)

        def gather(b):
            h, k = b // HB, b % 4
            for n in range(2):
                idx = POS[h][:, n, b - HB * h:b - HB * h + 1]
                g = P.add("pool", lambda e, idx=idx, n=n: e.indirect_dma_start(
                    GA[k][:, n, :], None, ys[h], bass.IndirectOffsetOnAxis(ap=idx, axis=0)),
                    [tC["ys", h, q] for q in range(4)] + last(("GA", k)), f"C.ga{k}", 16)
            return g

        def combine(b, g):
            h, k = b // HB, b % 4
            g = stt(X[:, b, :], GA[k][:, 0, :], WR[h][:, 0, b % HB:b % HB + 1], X[:, b, :], ALU.mult, ALU.add,
                    wait=[g], inc="C.z")
            g = stt(X[:, b, :], GA[k][:, 1, :], WR[h][:, 1, b % HB:b % HB + 1], X[:, b, :], ALU.mult, ALU.add,
                    wait=[g], inc="C.z")
            rel[("GA", k)] = [g]
            return ln_stats(X[:, b, :], [g])

        bg = steps([lambda: route(1), lambda: scatter(1)])

        def two():
            next(bg, None)
            next(bg, None)

        experts(0, two)
        for _ in bg:
            pass

        CU = at("CU", 2048, off=r0)[0:16, :].rearrange("p (h l) -> p h l", h=16)
        XP = at("XP", 3 * 132, off=r0 + 8192)[:, :].rearrange("p (k s) -> p k s", k=3)
        CO = at("CO", 384, off=r0 + 9792)[:, :].rearrange("p (k s) -> p k s", k=3)
        XTK = at("XTK", 128, off=r0 + 11328)[:, :]
        CUT = at("CUT", 16, off=r0 + 11840)[:, :]
        WDT = at("WDT", 1024, off=r0 + 12288)[:, :].rearrange("p (b c) -> p b c", b=8)
        CM = at("CM", 2048, off=r2 + 33024)[:, :].rearrange("p (h l) -> p h l", h=16)
        X3T = [at(f"X3T{k}", 128, off=r2 + 41216 + 512 * k)[:, :] for k in range(4)]
        WIN = at("WIN", 384, off=r2 + 43264)[:, :].rearrange("p (k c) -> p k c", k=3)
        WOD = at("WOD", 128, off=r2 + 44800)[:, :]
        EL = at("EL", 512, off=r2 + 45312)[:, :].rearrange("p (j l) -> p j l", j=4)
        Y0 = at("Y0", 128, off=r2 + 47360)[:, :]
        Y0T = at("Y0T", 128, off=r2 + 47872)[:, :]
        RN = [at(f"RN{g}", 128, off=o_ot + 6144 + 512 * g)[:, :] for g in range(4)]
        DW = [at(f"DW{k}", 128)[:, :] for k in range(4)]
        DO = [at(f"DO{k}", 128)[:, :] for k in range(2)]
        WX = at("WX", 1024, off=r4)[:, :].rearrange("p (k c) -> p k c", k=8)
        SEL = KON[:, C_SEL:C_SEL + 1024].rearrange("p (b c) -> p b c", b=8)
        ones = KON[:, C_ONE:C_ONE + 128]
        t_win = dma(WIN, a["win"], wait=b_end + [tB["av_pe"]], inc="ld.win", eng="act")
        t_wdt = dma(WDT, a["wdt"], wait=b_end, inc="ld.wdt", eng="act")
        t_wod = dma(WOD, a["wod"], wait=b_end + [tB["av_pe"]], inc="ld.wod", eng="act")
        t_wf = dma(WFt, a["wf"], wait=b_end + [tB["av_pe"]], inc="ld.wf", eng="act")
        t_wx = dma(WX, a["wx"], wait=[tC["te", 1]] + last("route"), inc="ld.wx", eng="act")
        t_xp = fill(XP, 0.0, wait=b_end, inc="D.xp", eng="pool")
        tD = {}
        queue = []

        def D_tp(b):
            m = m_bank()
            g = tp(bank[m][:, 0:128], X[:, b, :], wait=[tC["x3", b]] + last(("M", m)), inc="D.xt")
            g = cp(X3T[b % 4], bank[m][:, 0:128], wait=[g, tB["av_pe"]] + last(("X3T", b % 4)), inc="D.xtc", eng="act")
            rel[("M", m)] = [g]
            tD["x3t", b] = g

        def D_dt(b):
            g = mm(bank[0][:, 0:128], WDT[:, b % 8, :], X3T[b % 4], start=(b % 8 == 0), stop=(b % 8 == 7),
                   wait=[tD["x3t", b], t_wdt] + (last("DT") if b % 8 == 0 else []), inc="D.dt")
            rel[("X3T", b % 4)] = [g]
            tD["dt", b] = g

        def D_conv():
            m = m_bank()
            for k in range(3):
                g = mm(bank[m][:, 128 * k:128 * k + 128], WIN[:, k, :], X3T[0],
                       wait=([tD["x3t", 0], t_win] + last(("M", m))) if k == 0 else (), inc="D.in" if k == 2 else None)
            rel[("X3T", 0)] = [g]
            g = cp(XP[:, :, 3:131], bank[m][:, 0:384].rearrange("p (k s) -> p k s", k=3), wait=[g, t_xp], inc="S")
            rel[("M", m)] = [g]
            tD["conv"] = g

        def ssd():
            g = tD["conv"]
            for k in range(3):
                w = S_CW + 4 * k
                g = ts(CO[:, k, :], XP[:, k, 0:128], PAR[:, w:w + 1], PAR[:, S_CB + k:S_CB + k + 1], ALU.mult, ALU.add,
                       wait=[g, t_xp], inc="S")
                for i in range(1, 4):
                    g = stt(CO[:, k, :], XP[:, k, i:i + 128], PAR[:, w + i:w + i + 1], CO[:, k, :], ALU.mult, ALU.add,
                            wait=[g], inc="S")
                    yield
            c = tt(CM, CO[:, 0, :].unsqueeze(1).broadcast_to((128, 16, 128)),
                   KON[:, C_HM:C_HM + 16].unsqueeze(2).broadcast_to((128, 16, 128)), ALU.mult,
                   wait=[g, tB["av_pe"]], inc="S", eng="pool")
            m = m_bank()
            k = tp(bank[m][:, 0:128], CO[:, 2, :], wait=[g] + last(("M", m)), inc="S")
            k = cp(XTK, bank[m][:, 0:128], wait=[k], inc="S")
            rel[("M", m)] = [k]
            yield
            u = tt(CU, DW[2][0:16, :].unsqueeze(1).broadcast_to((16, 16, 128)),
                   KON[0:16, C_I16:C_I16 + 16].unsqueeze(2).broadcast_to((16, 16, 128)), ALU.mult,
                   wait=[tD["cum", 0], t_kon] + b_end, inc="S")
            m = m_bank()
            q = P.add("pe", lambda e: e.transpose(bank[m][:, 0:16], DW[2][0:16, :], ident[0:16, 0:16]),
                      [tD["cum", 0]] + last(("M", m)), "S")
            q = ts(CUT, bank[m][:, 0:16], -1.0, None, ALU.mult, wait=[q], inc="S")
            rel[("M", m)] = [q]
            rel["DW2"] = [q, u]
            yield
            for hg in range(4):
                m = m_bank()
                mm(bank[m], identb, masksb, start=True, stop=False, wait=[t_bf] + last(("M", m)))
                d = mm(bank[m], ones[0:16, :], CU[:, 4 * hg:4 * hg + 4, :], start=False, stop=True, wait=[u], inc="S")
                for j in range(4):
                    d = act(EL[:, j, :], bank[m][:, 128 * j:128 * j + 128], ACT.Exp,
                            bias=CUT[:, 4 * hg + j:4 * hg + j + 1], wait=[d, q, tB["av_pe"]] + last("EL"), inc="S")
                rel[("M", m)] = [d]
                m = m_bank()
                w = mm(bank[m], CO[:, 1, :], CM[:, 4 * hg:4 * hg + 4, :], wait=[c, g] + last(("M", m)), inc="S")
                w = tt(EL, EL, bank[m].rearrange("p (j l) -> p j l", j=4), ALU.mult, wait=[w, d], inc="S")
                rel[("M", m)] = [w]
                yield
                yield
                m = m_bank()
                for j in range(4):
                    h = 4 * hg + j
                    y = mm(bank[m][:, 8 * j:8 * j + 8], EL[:, j, :], XTK[:, 8 * h:8 * h + 8],
                           wait=([w, k] + last(("M", m))) if j == 0 else (), inc="S")
                rel["EL"] = [y]
                y = cp(Y0[:, 32 * hg:32 * hg + 32], bank[m][:, 0:32], wait=[y, tB["av_pe"]], inc="S")
                rel[("M", m)] = [y]
                yield
            m = m_bank()
            y = tp(bank[m][:, 0:128], Y0, wait=[y] + last(("M", m)), inc="S")
            y = cp(Y0T, bank[m][:, 0:128], wait=[y], inc="S")
            rel[("M", m)] = [y]
            tD["y0"] = y
            yield

        def dgroup(g):
            n = "D.n"
            x = stt(DW[1], RN[g], -1.0, RN[g], ALU.mult, ALU.max, wait=[tD["dtb", g]] + last("DW"), inc=n)
            yield
            x = act(DW[1], DW[1], ACT.Exp, scale=-1.0, wait=[x], inc=n)
            x = act(DW[1], DW[1], ACT.Ln, bias=1.0, wait=[x], inc=n)
            yield
            x = stt(DW[0], RN[g], 0.0, DW[1], ALU.max, ALU.add, wait=[x], inc=n)
            x = ts(DW[0], DW[0], PAR[:, S_AP:S_AP + 1], None, ALU.mult, wait=[x], inc=n)
            yield
            x = scan(DW[2], ones, DW[0], wait=[x] + last("DW2"), inc=n)
            tD["cum", g] = x
            yield
            y = act(DW[1], DW[2], ACT.Exp, wait=[x], inc=n)
            x = act(DW[0], DW[2], ACT.Exp, scale=-1.0, wait=[x], inc=n)
            yield
            rel["DW2"] = [x]
            x = scan(DW[3], ones, DW[0], wait=[x], inc=n)
            yield
            x = tt(DW[1], DW[1], DW[3], ALU.mult, wait=[x, y], inc=n)
            x = rcp(RN[g], DW[1], wait=[x, tB["y_pe"]], inc=n)
            rel["DW"] = [x]
            tD["rn", g] = x
            yield
            if g == 0:
                yield from ssd()

        def front(bs):
            st = {}
            n = len(bs)
            for i in range(n + 7):
                if i < n:
                    st["g", i] = gather(bs[i])
                if 2 <= i < n + 2:
                    st["l", i - 2] = combine(bs[i - 2], st["g", i - 2])
                if 3 <= i < n + 3:
                    b = bs[i - 3]
                    tC["x3", b] = ln_apply(X[:, b, :], X[:, b, :], st["l", i - 3], [], "C.x3")
                if 4 <= i < n + 4:
                    D_tp(bs[i - 4])
                if 5 <= i < n + 5:
                    b = bs[i - 5]
                    D_dt(b)
                    if b == 0:
                        D_conv()
                    if b % 8 == 7:
                        tD["dtb", b // 8] = ts(RN[b // 8], bank[0][:, 0:128], PAR[:, S_DTB:S_DTB + 1], None, ALU.add,
                                               wait=[tD["dt", b], tB["y_pe"]], inc="D.n")
                        rel["DT"] = [tD["dtb", b // 8]]
                        queue.append(dgroup(b // 8))
                yield

        def from_queue():
            if queue and next(queue[0], "end") == "end":
                queue.pop(0)

        fr = front(range(HB))

        def beside():
            next(fr, None)
            from_queue()

        experts(1, beside)
        while queue:
            from_queue()
        if stop == "C":
            finish(P, nc, dma, X, out, [tC["x3", b] for b in range(HB)] + [t_wod, t_wf, t_wx])
            return

        def D_expand(b):
            m = m_bank()
            g = mm(bank[m][:, 0:128], SEL[:, b % 8, :], RN[b // 8], wait=[tD["rn", b // 8]] + last(("M", m)),
                   inc="D.e")
            g = tt(DO[b % 2], bank[m][:, 0:128], Y0T, ALU.mult, wait=[g, tD["y0"]] + last(("DO", b % 2)), inc="D.o")
            rel[("M", m)] = [g]
            tD["o", b] = g

        def D_out(b):
            m = m_bank()
            g = mm(bank[m][:, 0:128], DO[b % 2], WOD, wait=[tD["o", b], t_wod] + last(("M", m)), inc="D.y")
            rel[("DO", b % 2)] = [g]
            g = tt(X[:, b, :], bank[m][:, 0:128], X[:, b, :], ALU.add, wait=[g, tC["x3", b], tD["x3t", b]], inc="D.z")
            rel[("M", m)] = [g]
            tD["ln", b] = ln_stats(X[:, b, :], [g])

        def D_ln(b):
            tD["x4", b] = ln_apply(X[:, b, :], X[:, b, :], tD["ln", b], [], "D.x4")

        def D_x4t(b):
            m = m_bank()
            g = tp(bank[m][:, 0:128], X[:, b, :], wait=[tD["x4", b]] + last(("M", m)), inc="D.x4t")
            g = cp(XT[:, 128 * b:128 * b + 128], bank[m][:, 0:128], wait=[g, tD["y0"], tD["rn", 3] if b >= 24 else None],
                   inc="D.x4c", eng="act")
            rel[("M", m)] = [g]
            tD["x4t", b] = g

        EQ = [at(f"EQ{k}", 1024, off=r1 + 4096 * k)[:, :].rearrange("p (k n) -> p k n", k=4) for k in range(3)]
        EV = [at(f"EV{k}", 512, off=r1 + 12288 + 2048 * k)[:, :].rearrange("p (j c) -> p j c", j=4) for k in range(3)]
        WSF = [at(f"WSF{k}", WF, off=r1 + 18432 + 4160 * k)[:, :] for k in range(3)]
        EC = [at(f"EC{k}", 512, off=r3 + 2048 * k)[:, :].rearrange("p (d n) -> p d n", d=2) for k in range(2)]
        EX = [at(f"EX{k}", 256, off=r3 + 4096 + 1024 * k)[:, :] for k in range(2)]
        ED = [at(f"ED{k}", 256, off=r3 + 6144 + 1024 * k)[:, :] for k in range(2)]
        EZ = [at(f"EZ{k}", 256, off=r3 + 8192 + 1024 * k)[:, :] for k in range(2)]
        HT = [at(f"HT{k}", 512, off=r3 + 10240 + 2048 * k)[:, :].rearrange("p (k n) -> p k n", k=4) for k in range(2)]
        X5T = [at(f"X5T{k}", 128, off=r1 + 30912 + 512 * k)[:, :] for k in range(8)]
        FZ = [at(f"FZ{k}", 128, off=r4 + 11264 + 512 * k)[:, :] for k in range(2)]
        FS = at("FS", 64, off=r4 + 12288)[:, :].rearrange("p (k e) -> p k e", k=8)
        FI = at("FI", 64, U32, off=r4 + 12544)[:, :].rearrange("p (k e) -> p k e", k=8)
        MS = at("MS", 16, off=r4 + 12800)[:, :]
        c_end = [tC["ac", 1, NT - 1], tC["d_pe"], tC["y_act"]] + [tC["ys", 1, q] for q in range(4)]
        SCL = float(1.0 / np.sqrt(np.float32(128.0)))
        t_nbg = ts(PAR[:, S_N + 1:S_N + 2], PAR[:, S_BG:S_BG + 1], -1.0, None, ALU.mult, wait=[t_par], inc="E.nbg")
        tE = {}

        def par(k):
            return PAR[:, k:k + 1]

        def E_proj(v):
            x4 = XT[:, 256 * v:256 * v + 256]
            cx = CT[:, 256 * v:256 * v + 256]
            r = v % 3
            xw = [tD["x4t", 2 * v], tD["x4t", 2 * v + 1], t_wx]
            m = m_bank()
            mm(bank[m][:, 0:256], WX[:, 0, :], x4, wait=xw + last(("M", m)))
            g = mm(bank[m][:, 256:512], WX[:, 3, :], cx, inc="E.q")
            g0 = ts(EQ[r][:, 0, :], bank[m][:, 0:256], par(S_BQC), SCL, ALU.add, ALU.mult,
                    wait=[g] + last(("EQ", r)) + c_end, inc="E.qc")
            tE["q", v] = ts(EQ[r][:, 1, :], bank[m][:, 256:512], par(S_BQS), SCL, ALU.add, ALU.mult, inc="E.qc")
            rel[("M", m)] = [tE["q", v]]
            m = m_bank()
            mm(bank[m][:, 0:256], WX[:, 1, :], cx, wait=last(("M", m)))
            g = mm(bank[m][:, 256:512], WX[:, 4, :], x4, inc="E.k")
            act(EQ[r][:, 2, :], bank[m][:, 0:256], ACT.Identity, bias=par(S_BKS), wait=[g] + last(("EQ", r)) + c_end)
            tE["k", v] = act(EQ[r][:, 3, :], bank[m][:, 256:512], ACT.Identity, bias=par(S_BKC), inc="E.kc")
            rel[("M", m)] = [tE["k", v]]
            m = m_bank()
            for j in range(4):
                src = (cx if j < 2 else x4)[:, 128 * (j % 2):128 * (j % 2) + 128]
                g = mm(bank[m][:, 128 * j:128 * j + 128], src, WX[:, 2 if j < 2 else 5, :],
                       wait=last(("M", m)) if j == 0 else (), inc="E.v" if j == 3 else None)
            tE["v", v] = cp(EV[r], bank[m].rearrange("p (j c) -> p j c", j=4), wait=[g] + last(("EV", r)) + c_end,
                            inc="E.vc", eng="act")
            rel[("M", m)] = [tE["v", v]]

        def E_S(v):
            sb, r = bank[1 + v % 2], v % 3
            for j in range(4):
                c = slice(128 * (j % 2), 128 * (j % 2) + 128)
                g = mm(sb[:, 128 * j:128 * j + 128], EQ[r][:, j // 2, c], EQ[r][:, 2 + j // 2, c],
                       wait=([tE["q", v], tE["k", v]] + last(("ES", v % 2))) if j == 0 else (),
                       inc="E.s" if j == 3 else None)
            rel[("EQ", r)] = [g]
            s3 = sb.rearrange("p (j s) -> p j s", j=4)
            g = sm_max("E", v, s3, g)
            g = sm_exp("E", v, s3, g)
            rel[("ES", v % 2)] = [g]
            tE["e", v] = g

        def E_norm(v):
            tE["n", v] = sm_nrm("E", v, sm_rec("E", v, tE["e", v]))

        def E_T(v):
            g = sm_tp("E", v, bank[3], tE["n", v], last("ET"))
            g = cp(PT[v % 3], bank[3].rearrange("p (j s) -> p j s", j=4), wait=[g] + last(("PT", v % 3)), inc="E.pt")
            rel["ET"] = [g]
            tE["pt", v] = g

        def E_AV(v):
            for j in range(4):
                g = mm(bank[4][:, 128 * j:128 * j + 128], EV[v % 3][:, j, :], PT[v % 3][:, j, :],
                       wait=([tE["pt", v], tE["v", v]] + last("EO")) if j == 0 else (), inc="E.av" if j == 3 else None)
            rel[("PT", v % 3)] = [g]
            rel[("EV", v % 3)] = [g]
            act(EC[v % 2][:, 0, :], bank[4][:, 0:256], ACT.Identity, bias=par(S_BVS),
                wait=[g] + last(("EC", v % 2)) + c_end)
            g = act(EC[v % 2][:, 1, :], bank[4][:, 256:512], ACT.Identity, bias=par(S_BVC), inc="E.ec")
            rel["EO"] = [g]
            tE["ec", v] = g
            tE["d", v] = tt(ED[v % 2], EC[v % 2][:, 0, :], EC[v % 2][:, 1, :], ALU.subtract,
                            wait=[g] + last(("ED", v % 2)) + c_end, inc="E.d", eng="pool")

        def E_gate(v):
            m = m_bank()
            mm(bank[m][:, 0:256], WX[:, 6, :], EC[v % 2][:, 0, :], start=True, stop=False,
               wait=[tE["ec", v]] + last(("M", m)))
            g = mm(bank[m][:, 0:256], WX[:, 7, :], EC[v % 2][:, 1, :], start=False, stop=True, inc="E.g")
            k = g
            g = act(EX[v % 2], bank[m][:, 0:256], ACT.Exp, bias=PAR[:, S_N + 1:S_N + 2], scale=-1.0,
                    wait=[g, t_nbg] + last(("EX", v % 2)) + c_end, inc="E.ex")
            rel[("M", m)] = [g]
            g = ts(EX[v % 2], EX[v % 2], 1.0, None, ALU.add, wait=[g], inc="E.e1")
            g = rcp(EX[v % 2], EX[v % 2], wait=[g], inc="E.r")
            g = tt(ED[v % 2], ED[v % 2], EX[v % 2], ALU.mult, wait=[g, tE["d", v]], inc="E.m", eng="pool")
            rel[("EX", v % 2)] = [g]
            g = tt(ED[v % 2], ED[v % 2], EC[v % 2][:, 1, :], ALU.add, wait=[g], inc="E.m", eng="pool")
            rel[("EC", v % 2)] = [g, k]
            g = tt(EZ[v % 2], ED[v % 2], XT[:, 256 * v:256 * v + 256], ALU.add, wait=[g] + last(("EZ", v % 2)) + c_end,
                   inc="E.z", eng="pool")
            rel[("ED", v % 2)] = [g]
            tE["z", v] = g

        def E_ln(v):
            m = m_bank()
            for j in range(2):
                g = tp(bank[m][:, 128 * j:128 * j + 128], EZ[v % 2][:, 128 * j:128 * j + 128],
                       wait=([tE["z", v]] + last(("M", m))) if j == 0 else (), inc="E.zt" if j else None)
            rel[("EZ", v % 2)] = [g]
            st = [ln_stats(bank[m][:, 128 * j:128 * j + 128], [g]) for j in range(2)]
            for j in range(2):
                b = 2 * v + j
                g = ln_apply(X[:, b, :], bank[m][:, 128 * j:128 * j + 128], st[j], [tD["x4t", b]], "E.x5")
            rel[("M", m)] = [g]
            tE["x5", v] = g

        tF = {}

        def F_top(v):
            m = m_bank()
            for j in range(2):
                g = tp(bank[m][:, 128 * j:128 * j + 128], X[:, 2 * v + j, :],
                       wait=([tE["x5", v]] + last(("M", m))) if j == 0 else (), inc="F.xt" if j else None)
            tF["xt", v] = g
            for j in range(2):
                b = 2 * v + j
                g = act(X5T[b % 8], bank[m][:, 128 * j:128 * j + 128], ACT.Copy, accum=MS[:, b % 16:b % 16 + 1],
                        wait=[tF["xt", v]] + last(("X5T", b % 8)) + last(("MS", b % 16)) + c_end, inc="F.x")
                tF["x", b] = g
            rel[("M", m)] = [g]

        def F_score(v):
            m = m_bank()
            for j in range(2):
                b = 2 * v + j
                g = mm(bank[m][0:1, 8 * j:8 * j + 8], MS[:, b % 16:b % 16 + 1], PAR[:, S_WR1:S_WR1 + 8],
                       wait=[tF["x", b]] + (last(("M", m)) if j == 0 else []), inc="F.s")
                rel[("MS", b % 16)] = [g]
            for j in range(2):
                b = 2 * v + j
                k = b % 4
                s = FS[0:1, k, :]
                q = stt(s, bank[m][0:1, 8 * j:8 * j + 8], 1.0 / 128, PAR[0:1, S_BR:S_BR + 8], ALU.mult, ALU.add,
                        wait=[g] + c_end, inc="F.t")
                if j == 1:
                    rel[("M", m)] = [q]
                q = P.add("dve", lambda e, k=k: e.max(FS[0:1, 4 + k, :], FS[0:1, k, :]), [q], "F.t")
                q = P.add("dve", lambda e, k=k: e.max_index(FI[0:1, k, :], FS[0:1, 4 + k, :], FS[0:1, k, :]),
                          [q], "F.t")
                tF["i", b] = q

        def F_w(b):
            tF["w", b] = staged(WSF[b % 3], WFt, WF, FI[0:1, b % 4, 0:1], [tF["i", b], t_wf] + last(("WSF", b % 3))
                                + c_end, "F.w")

        def F_h(b):
            w, k = WSF[b % 3], b % 2
            for f in range(4):
                g = mm(bank[7][:, 128 * f:128 * f + 128], w[:, 128 * f:128 * f + 128], X5T[b % 8],
                       wait=([tF["w", b], tF["x", b]] + last("FH")) if f == 0 else (), inc="F.h" if f == 3 else None)
            for f in range(4):
                q = act(HT[k][:, f, :], bank[7][:, 128 * f:128 * f + 128], ACT.Relu, bias=w[:, 1024 + f:1025 + f],
                        wait=([g] + last(("HT", k)) + c_end) if f == 0 else (), inc="F.r" if f == 3 else None)
            rel["FH"] = [q]
            tF["h", b] = q

        def F_out(b):
            w, k = WSF[b % 3], b % 2
            m = m_bank()
            for f in range(4):
                g = mm(bank[m][:, 0:128], w[:, 512 + 128 * f:640 + 128 * f], HT[k][:, f, :], start=(f == 0),
                       stop=(f == 3), wait=([tF["h", b]] + last(("M", m))) if f == 0 else (),
                       inc="F.o" if f == 3 else None)
            rel[("HT", k)] = [g]
            g = stt(FZ[k], bank[m][:, 0:128], w[:, 1028:1029], X5T[b % 8], ALU.add, ALU.add,
                    wait=[g] + last(("FZ", k)) + c_end, inc="F.z")
            rel[("M", m)] = [g]
            rel[("WSF", b % 3)] = [g]
            rel[("X5T", b % 8)] = [g]
            tF["z", b] = g

        def F_ln(b):
            m = m_bank()
            g = tp(bank[m][:, 0:128], FZ[b % 2], wait=[tF["z", b]] + last(("M", m)), inc="F.zt")
            rel[("FZ", b % 2)] = [g]
            st = ln_stats(bank[m][:, 0:128], [g])
            g = ln_apply(X[:, b, :], bank[m][:, 0:128], st, [tF["xt", b // 2]], "F.y")
            rel[("M", m)] = [g]
            tF["st"] = dma(out[b], X[:, b, :], wait=[g], inc="st")

        fr = front(range(HB, NB))
        rel["FH"], rel["EO"], rel["ET"] = last("CY"), last(("GU", 4)), last(("GU", 3))
        rel[("ES", 0)], rel[("ES", 1)] = last(("GU", 1)), last(("GU", 2))
        NV = NB // 2

        def each(fn):
            def two(v):
                fn(2 * v)
                fn(2 * v + 1)
            return two

        plan = ((each(D_expand), 0), (E_S, 3), (F_score, 9), (E_norm, 4), (each(D_out), 0), (E_gate, 6), (each(D_ln), 1),
                (E_T, 5), (each(F_w), 10), (E_AV, 5), (E_proj, 2), (each(D_x4t), 1), (F_top, 8),
                (E_ln, 7))
        for s in range(NV + 13):
            for _ in range(3):
                next(fr, None)
            for _ in range(4):
                from_queue()
            for fn, lag in plan:
                if 0 <= s - lag < NV:
                    fn(s - lag)
            for j in range(2):
                b = 2 * (s - 10) + j
                if 0 <= b - 1 < NB:
                    F_out(b - 1)
                if 0 <= b - 2 < NB:
                    F_ln(b - 2)
                if 0 <= b < NB:
                    F_h(b)
        finish(P, nc, dma, X, out, [], [tF["st"]])


def finish(P, nc, dma, X, out, toks, done=None):
    if done is None:
        done = [dma(out.rearrange("b t c -> t b c"), X, wait=toks, inc="st")]
    P.add("sp", lambda e: e.nop(), done, None)
    with nc.Block() as blk:
        @blk.sync
        def _(e):
            P.play("sp", e)

        @blk.scalar
        def _(e):
            P.play("act", e)

        @blk.vector
        def _(e):
            P.play("dve", e)

        @blk.gpsimd
        def _(e):
            P.play("pool", e)

        @blk.tensor
        def _(e):
            P.play("pe", e)


def layouts(i):
    f = np.float32

    def pad_heads(w):
        n = w.shape[0] // 8
        o = np.zeros((128, 8, 32), f)
        o[:, :, :n] = w.T.reshape(128, 8, n)
        return o.reshape(128, 256)

    par = np.zeros((128, S_N), f)
    par[:, S_SCALE] = i["L0_attn_scale"]
    par[:, S_GAMMA] = i["L0_xattn_ln_gamma"]
    par[:, S_BETA] = i["L0_xattn_ln_beta"]
    par[:, S_GATE] = i["L0_xattn_gate"][0]
    par[:, S_DTB] = np.tile(i["L1_attn_dt_bias"], 8)
    par[:, S_AP] = np.tile(i["L1_attn_A_param"], 8)
    par[:, S_CW:S_CW + 12] = i["L1_attn_conv_w"].reshape(3, 128, 4).transpose(1, 0, 2).reshape(128, 12)
    par[:, S_CB:S_CB + 3] = i["L1_attn_conv_b"].reshape(3, 128).T
    for k, n in enumerate(("bq_c", "bk_s", "bv_s", "bq_s", "bk_c", "bv_c", "bg")):
        par[:, S_BQC + k] = i["L1_xattn_" + n]
    par[:, S_BR:S_BR + 8] = i["L1_ffn_br"]
    par[:, S_WR0:S_WR0 + 8] = i["L0_ffn_router_w"]
    par[:, S_WR1:S_WR1 + 8] = i["L1_ffn_Wr"]

    x, ctx = i["x"], i["ctx_1024"]
    wo = np.zeros((8, 32, 128), f)
    wo[:, :16] = i["L0_attn_Wo"].T.reshape(8, 16, 128)
    wkv = i["L0_xattn_w_kv"]
    we = np.zeros((128, 8, WE), f)
    we[:, :, 0:352] = i["L0_ffn_gate_proj"].transpose(1, 0, 2)
    we[:, :, 384:736] = i["L0_ffn_up_proj"].transpose(1, 0, 2)
    dn = np.zeros((8, 384, 128), f)
    dn[:, :352] = i["L0_ffn_down_proj"]
    we[:, :, 768:1152] = dn.reshape(8, 3, 128, 128).transpose(2, 0, 1, 3).reshape(128, 8, 384)
    win = i["L1_attn_W_in"]
    wdt = np.zeros((128, 8, 8, 16), f)
    for b in range(8):
        wdt[:, b, b, :] = win[384:400].T
    wf = np.zeros((128, 8, WF), f)
    wf[:, :, 0:512] = i["L1_ffn_W1"].transpose(1, 0, 2)
    wf[:, :, 512:1024] = i["L1_ffn_W2"].reshape(8, 4, 128, 128).transpose(2, 0, 1, 3).reshape(128, 8, 512)
    wf[:, :, 1024:1028] = i["L1_ffn_b1"].reshape(8, 4, 128).transpose(2, 0, 1)
    wf[:, :, 1028] = i["L1_ffn_b2"].T
    wg = i["L1_xattn_Wg"]
    wx = np.stack([i["L1_xattn_" + n].T for n in ("Wq_c", "Wk_s", "Wv_s", "Wq_s", "Wk_c", "Wv_c")]
                  + [wg[:, :128].T, wg[:, 128:].T], 1)
    return {
        "par": par, "kon": constants(),
        "x": x.transpose(1, 0, 2), "xT": x.transpose(2, 0, 1).reshape(128, 4096),
        "cT": ctx.transpose(2, 0, 1).reshape(128, 4096),
        "wqr": i["L0_attn_Wq"], "wk": pad_heads(i["L0_attn_Wk"]).reshape(128, 2, 128),
        "wv": pad_heads(i["L0_attn_Wv"]),
        "wo": wo.reshape(2, 128, 128).transpose(1, 0, 2),
        "wqT": i["L0_xattn_w_q"].T.reshape(16, 64, 128).transpose(1, 0, 2),
        "wkT": wkv[:, :1024].T.reshape(16, 64, 128).transpose(1, 0, 2),
        "wvb": wkv[:, 1024:], "wob": i["L0_xattn_w_out"].reshape(8, 128, 128).transpose(1, 0, 2),
        "bo": np.broadcast_to(i["L0_xattn_b_out"], (128, 128)),
        "we": we.reshape(128, 8 * WE),
        "win": win[0:384].reshape(3, 128, 128).transpose(2, 0, 1), "wdt": wdt.reshape(128, 1024),
        "wod": i["L1_attn_W_out"].T, "wx": wx, "wf": wf.reshape(128, 8 * WF),
    }


def kernel(**inputs):
    import concourse.bacc as bacc
    from concourse.bass_utils import run_bass_kernel_spmd

    arrays = {n: np.ascontiguousarray(v) for n, v in layouts({k: np.asarray(v) for k, v in inputs.items()}).items()}
    nc = bacc.Bacc("TRN2", target_bir_lowering=False, num_devices=1)
    aps = {n: nc.dram_tensor(n, v.shape, mybir.dt.from_np(v.dtype), kind="ExternalInput").ap()
           for n, v in arrays.items()}
    out = nc.dram_tensor("out", (NB, 128, 128), F32, kind="ExternalOutput").ap()
    build(nc, aps, out)
    r = run_bass_kernel_spmd(nc, [arrays], core_ids=[0])
    return r.results[0]["out"]
```

```python
from contextlib import ExitStack

import numpy as np
import concourse.bass as bass
from concourse import mybir

F32 = mybir.dt.float32
F32R = mybir.dt.float32r
BF16 = mybir.dt.bfloat16
I32 = mybir.dt.int32
U32 = mybir.dt.uint32
ALU = mybir.AluOpType
ACT = mybir.ActivationFunctionType
AX = mybir.AxisListType

NB = 32
HB = 16
NT = 39
EPS = 1e-5
NEG = -1e38
WE = 1152
WF = 1030

S_SCALE, S_GAMMA, S_BETA, S_GATE, S_DTB, S_AP = 0, 1, 2, 3, 4, 5
S_CW, S_CB = 6, 18
S_BQC, S_BKS, S_BVS, S_BQS, S_BKC, S_BVC, S_BG = 21, 22, 23, 24, 25, 26, 27
S_BR = 28
S_WR0, S_WR1 = 36, 44
S_N = 52

C_E, C_DD, C_MQ, C_MK, C_N0 = 0, 256, 512, 513, 514
C_ID, C_MASK, C_N1 = 514, 642, 770
C_TRI, C_ONE, C_MASKS = 770, 898, 1026
C_SEL = 1154
C_HM = C_SEL + 1024
C_I16 = C_HM + 16
C_E8 = C_I16 + 16
C_RST = C_E8 + 8
C_J = C_RST + 128
C_N = C_J + 40


def constants():
    c = np.zeros((128, C_N), np.float32)
    p = np.arange(128)
    c[:, C_ID:C_ID + 128] = np.eye(128)
    c[:, C_MASK:C_MASK + 128] = np.where(p[None, :] > p[:, None], NEG, 0.0)
    c[:, C_TRI:C_TRI + 128] = (p[:, None] < p[None, :])
    c[:, C_ONE:C_ONE + 128] = 1.0
    c[:, C_MASKS:C_MASKS + 128] = np.where(p[None, :] < p[:, None], NEG, 0.0)
    signs = np.array([[a, b, d] for a in (-1, 1) for b in (-1, 1) for d in (-1, 1)], np.float32)
    dirs = signs / np.linalg.norm(signs, axis=1, keepdims=True)
    for h in range(8):
        col = 128 * (h // 4) + 32 * (h % 4)
        for i in range(3):
            for r in range(4):
                c[3 * h + i, C_E + col + 3 * r + i] = 1.0
                for j in range(3):
                    c[3 * h + j, C_DD + col + 3 * r + i] = dirs[h, i] * dirs[h, j]
    for b in range(8):
        for h in range(16):
            c[16 * b + h, C_SEL + 128 * b + 8 * h:C_SEL + 128 * b + 8 * h + 8] = 1.0
    c[p, C_HM + p // 8] = 1.0
    c[p[:16], C_I16 + p[:16]] = 1.0
    c[:, C_E8:C_E8 + 8] = 8.0 - np.arange(8)
    c[:, C_RST:C_RST + 128] = (p % 16 != 0)
    c[:, C_J:C_J + 40] = np.arange(40)
    c[:, C_MQ] = np.where((p % 32) // 6 == 1, -1.0, 0.0)
    c[:, C_MK] = np.where((p % 32) // 3 % 2 == 1, -1.0, 0.0)
    return c


class Prog:

    def __init__(self, nc, ctx):
        self.nc, self.ctx = nc, ctx
        self.q = {n: [] for n in ("pe", "dve", "act", "pool", "sp")}
        self.sems, self.count, self.seen = {}, {}, {}

    def add(self, eng, fn, wait, inc, step=1):
        waits = []
        for t in wait:
            if t is not None and self.seen.get((eng, t[0]), 0) < t[1]:
                self.seen[(eng, t[0])] = t[1]
                waits.append(t)
        if inc is not None:
            inc = (inc.split(".")[0] if step == 1 else inc) + "." + eng
        if inc is not None and inc not in self.sems:
            self.sems[inc] = self.ctx.enter_context(self.nc.semaphore(inc.replace(".", "_")))
            self.count[inc] = 0
        self.q[eng].append((waits, fn, inc, step))
        if inc is None:
            return None
        self.count[inc] += step
        return (inc, self.count[inc])

    def play(self, eng, e):
        for waits, fn, inc, step in self.q[eng]:
            for n, v in waits:
                e.wait_ge(self.sems[n], v)
            ins = fn(e)
            if inc is not None:
                ins.then_inc(self.sems[inc], step)


def build(nc, a, out, stop="F"):
    with ExitStack() as ctx:
        P = Prog(nc, ctx)

        def mm(o, lhsT, rhs, start=True, stop=True, wait=(), inc=None):
            return P.add("pe", lambda e: e.matmul(o, lhsT, rhs, start=start, stop=stop,
                                                  skip_group_check=True), wait, inc)

        def tp(o, i, wait=(), inc=None):
            return P.add("pe", lambda e: e.transpose(o, i, ident), wait, inc)

        def tt(o, x, y, op, wait=(), inc=None, eng="dve"):
            return P.add(eng, lambda e: e.tensor_tensor(o, x, y, op), wait, inc)

        def ts(o, x, s1, s2, op0, op1=None, wait=(), inc=None, eng="dve"):
            if op1 is None:
                return P.add(eng, lambda e: e.tensor_scalar(o, x, s1, None, op0), wait, inc)
            return P.add(eng, lambda e: e.tensor_scalar(o, x, s1, s2, op0, op1), wait, inc)

        def stt(o, x, s, y, op0, op1, wait=(), inc=None):
            return P.add("dve", lambda e: e.scalar_tensor_tensor(out=o, in0=x, scalar=s, in1=y, op0=op0, op1=op1),
                         wait, inc)

        def red(o, x, op, wait=(), inc=None, neg=False):
            return P.add("dve", lambda e: e.tensor_reduce(o, x, AX.X, op, negate=neg), wait, inc)

        def scan(o, x, y, wait=(), inc=None):
            return P.add("dve", lambda e: e.tensor_tensor_scan(o, x, y, 0.0, ALU.mult, ALU.add), wait, inc)

        def cp(o, x, wait=(), inc=None, eng="dve"):
            if eng == "act":
                return P.add("act", lambda e: e.activation(o, x, ACT.Copy), wait, inc)
            return P.add(eng, lambda e: e.tensor_copy(o, x), wait, inc)

        def rcp(o, x, wait=(), inc=None):
            return P.add("dve", lambda e: e.reciprocal(o, x), wait, inc)

        def act(o, x, f, wait=(), inc=None, bias=0.0, scale=1.0, accum=None):
            if accum is None:
                return P.add("act", lambda e: e.activation(o, x, f, bias=bias, scale=scale), wait, inc)
            return P.add("act", lambda e: e.activation(o, x, f, bias=bias, scale=scale, accum_out=accum), wait, inc)

        def fill(o, v, wait=(), inc=None, eng="dve"):
            return P.add(eng, lambda e: e.memset(o, v), wait, inc)

        def dma(o, x, wait=(), inc=None, eng="sp"):
            return P.add(eng, lambda e: e.dma_start(o, x), wait, inc, 16)

        top = [nc.sbuf_base + (-nc.sbuf_base) % 64]

        def at(name, cols, dt=F32, off=None):
            size = cols * (2 if dt == BF16 else 4)
            size += -size % 64
            if off is None:
                off = top[0]
                top[0] += size
            return nc.alloc_sbuf_tensor_at(name, [128, cols], dt, offset=off)

        def region(cols):
            r = top[0]
            top[0] += cols * 4
            return r

        X = at("X", NB * 128)[:, :].rearrange("p (b c) -> p b c", b=NB)
        r0 = top[0]
        XT = at("XT", NB * 128)[:, :]
        CT = at("CT", NB * 128)[:, :]
        KON = at("KON", C_N)[:, :]
        PAR = at("PAR", S_N + 64)[:, :]
        ident = KON[:, C_ID:C_ID + 128]
        identb = at("identb", 128, BF16)[:, :]
        maskb = at("maskb", 512, BF16)[:, :]
        masksb = at("masksb", 512, BF16)[:, :]
        trib = at("trib", 128, BF16)[:, :]
        oneb = at("oneb", 128, BF16)[:, :]
        r1 = region(8 * WE)
        KB = [at(f"KB{i}", 4096, F32R, off=r1 + 16384 * i)[:, :].rearrange("p (t b j s) -> p t b j s", t=2, b=4, j=4)
              for i in range(2)]
        WCt = at("WCt", 8 * WE, off=r1)[:, :]
        r2 = region(12288)
        QB = [at(f"QB{i}", 4096, off=r2 + 16384 * i)[:, :].rearrange("p (h t) -> p h t", h=16) for i in range(2)]
        VB = [at(f"VB{i}", 2048, off=r2 + 32768 + 8192 * i)[:, :].rearrange("p (b d) -> p b d", b=2) for i in range(2)]
        HI = [at(f"HI{i}", 512, F32R, off=r2 + 40960 + 2048 * i)[:, :] for i in range(2)]
        KS = [at(f"KS{i}", 512, F32R, off=r2 + 45056 + 2048 * i)[:, :] for i in range(2)]
        WFt = at("WFt", 8 * WF, off=r2)[:, :]
        r3 = region(2048 + 1024 + 1024)
        AH = at("AH", 2048, off=r3)[:, :].rearrange("p (h c) -> p h c", h=16)
        WVB = at("WVB", 1024, off=r3 + 8192)[:, :]
        WOB = at("WOB", 1024, off=r3 + 12288)[:, :].rearrange("p (k c) -> p k c", k=8)
        r4 = region(256 * 3 + 256 + 2 * 1024 + 4 * 256)
        WQA = at("WQA", 256, off=r4)[:, :].rearrange("p (t c) -> p t c", t=2)
        WKA = at("WKA", 256, off=r4 + 1024)[:, :].rearrange("p (t c) -> p t c", t=2)
        WVA = at("WVA", 256, off=r4 + 2048)[:, :]
        WOA = at("WOA", 256, off=r4 + 3072)[:, :].rearrange("p (t c) -> p t c", t=2)
        QA = [at(f"QA{i}", 1024, F32R, off=r4 + 4096 + 4096 * i)[:, :].rearrange("p (t n) -> p t n", t=2) for i in range(2)]
        VA = [at(f"VA{i}", 256, off=r4 + 12288 + 1024 * i)[:, :] for i in range(4)]
        PP = [at(f"PP{i}", 512)[:, :].rearrange("p (j s) -> p j s", j=4) for i in range(4)]
        PT = [at(f"PT{i}", 512)[:, :].rearrange("p (j s) -> p j s", j=4) for i in range(3)]
        o_ot = top[0]
        OT = [at(f"OT{i}", 1024)[:, :] for i in range(2)]
        SM = at("SM", 16)[:, :].rearrange("p (k j) -> p k j", k=4)
        MX = at("MX", 16)[:, :].rearrange("p (k j) -> p k j", k=4)
        RS = at("RS", 16)[:, :].rearrange("p (k j) -> p k j", k=4)
        ST = [at(f"ST{i}", 8)[:, :] for i in range(12)]
        MV = [at(f"MV{i}", 4)[:, :] for i in range(12)]
        XH = [at(f"XH{i}", 128)[:, :] for i in range(4)]
        SW = at("SW", 16)[:, :]
        o_bt = top[0]
        BT = at("BT", 128)[:, :]
        BTZ = at("BTZ", 128)[:, :]
        RTE = at("RTE", 360)[:, :]

        PS = [ctx.enter_context(nc.psum_tensor(f"bank{i}", [128, 512], F32)) for i in range(8)]
        bank = [t[:, :] for t in PS]

        rel = {}

        def last(key):
            return rel.get(key, [])

        WQR = at("WQR", 128, off=r3 + 12288)[:, :]
        t_kon0 = dma(KON[0:128, 0:C_N0], a["kon"][:, 0:C_N0], inc="ld.kon0", eng="act")
        t_par = dma(PAR[:, 0:S_N], a["par"], inc="ld.par")
        t_wqr = dma(WQR[0:24, :], a["wqr"], inc="ld.wqr")
        t_wk = dma(WKA, a["wk"], inc="ld.wk")
        t_kon1 = dma(KON[:, C_N0:C_N1], a["kon"][:, C_N0:C_N1], inc="ld.kon1", eng="act")
        t_wv = dma(WVA, a["wv"], inc="ld.wv", eng="act")
        t_xt, t_x = [], []
        for c in range(8):
            t_xt.append(dma(XT[:, 512 * c:512 * c + 512], a["xT"][:, 512 * c:512 * c + 512], inc=f"ld.xt{c}"))
            if c == 0:
                t_wo = dma(WOA, a["wo"], inc="ld.wo")
                t_bo = dma(BT, a["bo"], inc="ld.bo")
            t_x.append(dma(X[:, 4 * c:4 * c + 4, :], a["x"][:, 4 * c:4 * c + 4, :], inc=f"ld.x{c}"))
        WQT = at("WQT", 2048, off=r2)[0:64, :].rearrange("p (k c) -> p k c", k=16)
        WKT = at("WKT", 2048, off=r2 + 8192)[0:64, :].rearrange("p (k c) -> p k c", k=16)

        t_kb = [fill(KB[0].bitcast(F32), 0.0, inc="k.kb", eng="dve"), fill(KB[1].bitcast(F32), 0.0, inc="k.kb", eng="pool")]
        MF = at("MF", 256, off=r3 + 8192 + 1024)[:, :]
        t_mf = stt(MF[0:24, :], KON[0:24, C_E:C_E + 256], PAR[0:24, S_SCALE:S_SCALE + 1],
                   KON[0:24, C_DD:C_DD + 256], ALU.mult, ALU.add, wait=[t_par, t_kon0], inc="A.mf")
        t = mm(bank[7][:, 0:256], WQR[0:24, :], MF[0:24, :], wait=[t_mf, t_wqr], inc="A.wq")
        t_wq = cp(WQA, bank[7][:, 0:256].rearrange("p (t c) -> p t c", t=2), wait=[t], inc="A.wqc")
        rel["Y"] = [t_wq]
        t_mfr = t
        cp(identb, ident, wait=[t_kon1], inc="k.bf")
        for j in range(4):
            t_bf = cp(maskb[:, 128 * j:128 * j + 128], KON[:, C_MASK:C_MASK + 128], inc="k.bf")
        t_sw = fill(SW[:, 0:1], -0.5, inc="k.sw", eng="pool")

        nln = [0]

        def ln_stats(z, wait):
            k = nln[0] % 12
            nln[0] += 1
            t = P.add("dve", lambda e: e.bn_stats(ST[k][:, 0:6], z), list(wait) + last(("ln", k)), "ln.st")
            t = P.add("dve", lambda e: e.bn_aggr(MV[k][:, 0:2], ST[k][:, 0:6]), [t], "ln.ag")
            t = ts(MV[k][:, 2:3], MV[k][:, 1:2], EPS, None, ALU.add, wait=[t], inc="ln.ep")
            t = tt(MV[k][:, 3:4], MV[k][:, 2:3], SW[:, 0:1], ALU.pow, wait=[t, t_sw], inc="ln.pw", eng="pool")
            return k, t

        def ln_apply(o, z, st, wait, inc):
            k, t = st
            t = ts(o, z, MV[k][:, 0:1], MV[k][:, 3:4], ALU.subtract, ALU.mult, wait=list(wait) + [t], inc=inc)
            rel[("ln", k)] = [t]
            return t

        def sm_max(ph, u, sb, t_s):
            return red(MX[:, u % 4, :], sb, ALU.max, wait=[t_s] + last(("MX", u % 4)), inc=ph + ".max", neg=True)

        def sm_exp(ph, u, sb, t_m):
            for j in range(4):
                t = act(PP[u % 4][:, j, :], sb[:, j, :], ACT.Exp, bias=MX[:, u % 4, j:j + 1],
                        accum=SM[:, u % 4, j:j + 1],
                        wait=([t_m] + last(("PP", u % 4)) + last(("SM", u % 4))) if j == 0 else (),
                        inc=ph + ".exp")
            rel[("MX", u % 4)] = [t]
            return t

        def sm_rec(ph, u, t_e):
            t = rcp(RS[:, u % 4, :], SM[:, u % 4, :], wait=[t_e] + last(("RS", u % 4)), inc=ph + ".rec")
            rel[("SM", u % 4)] = [t]
            return t

        def sm_nrm(ph, u, t_r):
            t = tt(PP[u % 4], PP[u % 4], RS[:, u % 4, :].unsqueeze(2).broadcast_to((128, 4, 128)), ALU.mult,
                   wait=[t_r], inc=ph + ".nrm", eng="pool")
            rel[("RS", u % 4)] = [t]
            return t

        def sm_tp(ph, u, tb, t_n, free):
            for j in range(4):
                t = tp(tb[:, 128 * j:128 * j + 128], PP[u % 4][:, j, :], wait=([t_n] + free) if j == 0 else (),
                       inc=ph + ".tp" if j == 3 else None)
            rel[("PP", u % 4)] = [t]
            return t

        nM, ring = [0], [5]

        def m_bank():
            k = ring[nM[0] % len(ring)]
            nM[0] += 1
            return k

        tA = {}

        def A_q(c, t):
            g = mm(bank[3], WQA[:, t, :], XT[:, 512 * c:512 * c + 512], wait=[t_wq, t_xt[c]] + last("P"), inc="A.q")
            tA["qh", c, t] = cp(HI[0], bank[3], wait=[g] + last(("HI", 0)), inc="A.hi", eng="act")

        def A_q2(c, t):
            g = stt(QA[c % 2][:, t, :], HI[0], KON[:, C_MQ:C_MQ + 1], bank[3], ALU.mult, ALU.add,
                    wait=[tA["qh", c, t]] + last(("QA", c % 2)), inc="A.qc")
            rel["P"] = rel[("HI", 0)] = [g]
            tA["q", c, t] = g

        def A_k(c, t):
            g = mm(bank[3], WKA[:, t, :], XT[:, 512 * c:512 * c + 512], wait=[t_wk, t_xt[c]] + last("P"), inc="A.k")
            tA["kh", c, t] = cp(HI[1], bank[3], wait=[g] + last(("HI", 1)), inc="A.hi", eng="act")

        def A_k2(c, t):
            g = stt(KS[t], HI[1], KON[:, C_MK:C_MK + 1], bank[3], ALU.mult, ALU.add,
                    wait=[tA["kh", c, t]] + last(("KS", t)), inc="A.kc")
            rel["P"] = rel[("HI", 1)] = [g]
            for j in range(4):
                r = slice(32 * j, 32 * j + 32)
                src = KS[t][r, :].rearrange("p (b s) -> p b s", b=4)
                if c == 0:
                    k = cp(KB[0][r, t, :, j, :], src, wait=[g, t_kb[0]], inc="A.kd")
                else:
                    k = dma(KB[c % 2][r, t, :, j, :].bitcast(F32), src.bitcast(F32),
                            wait=[g, t_kb[c % 2]] + last(("KB", c % 2)), inc=f"A.kd{c % 2}{t}")
            rel[("KS", t)] = [k]
            tA["k", c, t] = k

        def A_v(b):
            m = m_bank()
            g = mm(bank[m][:, 0:256], XT[:, 128 * b:128 * b + 128], WVA, wait=[t_wv, t_xt[b // 4]] + last(("M", m)),
                   inc="A.v")
            rel[("XT", b)] = [g]
            g = cp(VA[b % 4], bank[m][:, 0:256], wait=[g] + last(("VA", b % 4)), inc="A.vc", eng="act")
            rel[("M", m)] = [g]
            tA["v", b] = g

        def A_S(u):
            b, t = u // 2, u % 2
            c = b // 4
            sb = bank[u % 2]
            mm(sb, identb, maskb, start=True, stop=False,
               wait=[t_bf, tA["q", c, t], tA["k", c, t]] + last(("S", u % 2)))
            g = mm(sb, QA[c % 2][:, t, 128 * (b % 4):128 * (b % 4) + 128], KB[c % 2][:, t, b % 4, :, :],
                   start=False, stop=True, inc="A.s")
            if u % 8 == 7:
                rel[("QA", c % 2)] = [g]
                rel[("KB", c % 2)] = [g]
            s3 = sb.rearrange("p (j s) -> p j s", j=4)
            g = sm_max("A", u, s3, g)
            g = sm_exp("A", u, s3, g)
            rel[("S", u % 2)] = [g]
            tA["e", u] = g

        def A_norm(u):
            tA["n", u] = sm_nrm("A", u, sm_rec("A", u, tA["e", u]))

        def A_T(u):
            tb = bank[(2, 6)[u % 2]]
            g = sm_tp("A", u, tb, tA["n", u], last(("T", u % 2)))
            g = cp(PT[u % 3], tb.rearrange("p (j s) -> p j s", j=4), wait=[g] + last(("PT", u % 3)), inc="A.pt",
                   eng="act")
            rel[("T", u % 2)] = [g]
            tA["pt", u] = g

        def A_AV(u):
            b, t = u // 2, u % 2
            for j in range(4):
                g = mm(bank[4][32 * j:32 * j + 32, 128 * t:128 * t + 128],
                       VA[b % 4][:, 128 * t + 32 * j:128 * t + 32 * j + 32], PT[u % 3][:, j, :],
                       wait=([tA["pt", u], tA["v", b]] + (last("O") if t == 0 else [])) if j == 0 else (),
                       inc="A.av" if j == 3 else None)
            rel[("PT", u % 3)] = [g]
            if t == 1:
                rel[("VA", b % 4)] = [g]
                g = cp(OT[b % 2][:, 0:256], bank[4][:, 0:256], wait=[g] + last(("OT", b % 2)), inc="A.ot", eng="dve")
                rel["O"] = [g]
                tA["ot", b] = g

        def A_out(b):
            for t in range(2):
                g = mm(bank[7][:, 0:128], OT[b % 2][:, 128 * t:128 * t + 128], WOA[:, t, :], start=(t == 0),
                       stop=(t == 1), wait=([tA["ot", b], t_wo] + last("Y")) if t == 0 else (),
                       inc="A.y" if t else None)
            rel[("OT", b % 2)] = [g]
            g = tt(X[:, b, :], bank[7][:, 0:128], X[:, b, :], ALU.add, wait=[g, t_x[b // 4]], inc="A.z")
            rel["Y"] = [g]
            tA["ln", b] = ln_stats(X[:, b, :], [g])

        def A_ln(b):
            g = ln_apply(X[:, b, :], X[:, b, :], tA["ln", b], [], "A.x1")
            tA["x1", b] = g
            tA["ln2", b] = ln_stats(X[:, b, :], [g])

        def A_ln2(b):
            g = ln_apply(XH[b % 4], X[:, b, :], tA["ln2", b], last(("XH", b % 4)), "A.xh")
            tA["xh", b] = g
            tA["xb", b] = tt(X[:, b, :], X[:, b, :], BT, ALU.add, wait=[g, t_bt], inc="A.xb", eng="pool")

        def A_xn(b):
            m = 7
            g = tp(bank[m][:, 0:128], XH[b % 4], wait=[tA["xh", b]] + last("Y"), inc="A.xt")
            rel[("XH", b % 4)] = [g]
            tA["xt_pe"] = g
            g = ts(XT[:, 128 * b:128 * b + 128], bank[m][:, 0:128], PAR[:, S_GAMMA:S_GAMMA + 1],
                   PAR[:, S_BETA:S_BETA + 1], ALU.mult, ALU.add, wait=[g] + last(("XT", b)), inc="A.xn")
            rel["Y"] = [g]
            tA["xn", b] = g

        for t in range(2):
            A_q(0, t)
            A_q2(0, t)
            A_k(0, t)
            A_k2(0, t)
        t_tg = act(PAR[:, S_N:S_N + 1], PAR[:, S_GATE:S_GATE + 1], ACT.Tanh, wait=[t_par], inc="B.tg")
        t_bt = ts(BT, BT, PAR[:, S_N:S_N + 1], None, ALU.mult, wait=[t_tg, t_bo], inc="B.bt")
        def B_ah(k):
            m = m_bank()
            for j in range(4):
                h = 4 * k + j
                g = mm(bank[m][:, 128 * j:128 * j + 128], WQT[:, h, :], WKT[:, h, :],
                       wait=([t_wqt, t_wkt] + last(("M", m))) if j == 0 else (), inc="B.ah" if j == 3 else None)
            rel["WQT"] = [g]
            g = act(AH[:, 4 * k:4 * k + 4, :], bank[m].rearrange("p (h c) -> p h c", h=4), ACT.Copy, scale=0.125,
                    wait=[g], inc="B.ahc")
            rel[("M", m)] = [g]
            tA["ah", k] = g

        NU = 2 * NB
        sched = {}
        for c in range(1, 8):
            for n, (fn, t) in enumerate(((A_k, 0), (A_k, 1), (A_q, 0), (A_q, 1))):
                sched[max(8 * c - 9 + 2 * n, n)] = (fn, c, t)
        for i in range(NU + 19):
            if i < NU:
                A_S(i)
            if i < NU:
                if i % 2 == 0:
                    A_v(i // 2)
            if i == 9:
                t_wqt = dma(WQT, a["wqT"], inc="ld.wqt")
                t_wkt = dma(WKT, a["wkT"], inc="ld.wkt")
                t_ct = dma(CT, a["cT"], inc="ld.ct")
                t_kon = dma(KON[:, C_N1:C_N], a["kon"][:, C_N1:C_N], inc="ld.kon")
                t_wvb = dma(WVB, a["wvb"], wait=[t_mfr], inc="ld.wvb")
                t_wob = dma(WOB, a["wob"], wait=[t_mfr], inc="ld.wob")
            if i in (27, 31, 35, 39):
                B_ah((27, 31, 35, 39).index(i))
            if i == 50:
                t_wob = ts(WOB, WOB, PAR[:, S_N:S_N + 1], None, ALU.mult, wait=[t_tg, t_wob], inc="B.wob", eng="pool")
            if 3 <= i < NU + 3:
                A_T(i - 3)
            if 5 <= i < NU + 5:
                A_AV(i - 5)
            for fn, lag in ((A_xn, 13), (A_ln2, 11), (A_ln, 9), (A_out, 8)):
                j = i - lag
                if j >= 0 and j % 2 == 0 and j // 2 < NB:
                    fn(j // 2)
            if i - 1 in sched:
                fn, c, t = sched[i - 1]
                (A_k2 if fn is A_k else A_q2)(c, t)
            if i in sched:
                fn, c, t = sched[i]
                fn(c, t)
            if 1 <= i <= NU:
                A_norm(i - 1)

        tA["end"] = tA["xn", NB - 1]
        rel[("VB", 1)] = last(("HI", 0)) + last(("HI", 1)) + last(("KS", 0)) + last(("KS", 1))
        rel[("M", 6)] = last(("T", 1))
        rel[("T", 1)] = last("P")
        ring.append(6)
        tA["end_pe"] = tA["xt_pe"]
        if stop == "A":
            finish(P, nc, dma, X, out, [tA["xb", b] for b in range(NB)])
            return

        tB = {}
        for j in range(4):
            cp(masksb[:, 128 * j:128 * j + 128], KON[:, C_MASKS:C_MASKS + 128], wait=[t_kon], eng="act")
        cp(trib, KON[:, C_TRI:C_TRI + 128], eng="act")
        t_bf2 = cp(oneb, KON[:, C_ONE:C_ONE + 128], inc="k.bf", eng="act")

        def B_q(c, k):
            m = m_bank()
            for j in range(2):
                h = 2 * k + j
                g = mm(bank[m][:, 256 * j:256 * j + 256], AH[:, h, :], XT[:, 256 * c:256 * c + 256],
                       wait=([tA["ah", h // 4], tA["xn", 2 * c], tA["xn", 2 * c + 1]] + last(("M", m)))
                       if j == 0 else (), inc="B.q" if j else None)
            g = cp(QB[c % 2][:, 2 * k:2 * k + 2, :], bank[m].rearrange("p (h t) -> p h t", h=2),
                   wait=[g] + last(("QB", c % 2)) + last("WQT"), inc="B.qc", eng="act" if k % 2 else "dve")
            rel[("M", m)] = [g]
            tB["q", c, k] = g

        def B_v(c, k):
            m = m_bank()
            b = 2 * c + k // 2
            g = mm(bank[m], CT[:, 128 * b:128 * b + 128], WVB[:, 512 * (k % 2):512 * (k % 2) + 512],
                   wait=[t_ct, t_wvb] + last(("M", m)), inc="B.v")
            g = cp(VB[c % 2][:, k // 2, 512 * (k % 2):512 * (k % 2) + 512], bank[m],
                   wait=[g] + last(("VB", c % 2)), inc="B.vc", eng="act" if k % 2 else "dve")
            rel[("M", m)] = [g]
            tB["v", c, k] = g

        def B_S(u):
            c, bb, hq = u // 8, (u // 4) % 2, u % 4
            b = 2 * c + bb
            sb = bank[u % 2]
            for j in range(4):
                h = 4 * hq + j
                g = mm(sb[:, 128 * j:128 * j + 128], QB[c % 2][:, h, 128 * bb:128 * bb + 128],
                       CT[:, 128 * b:128 * b + 128],
                       wait=([t_ct, tB["q", c, 2 * hq], tB["q", c, 2 * hq + 1]] + last(("S", u % 2)))
                       if j == 0 else (), inc="B.s" if j == 3 else None)
            if u % 8 == 7:
                rel[("QB", c % 2)] = [g]
            s3 = sb.rearrange("p (j s) -> p j s", j=4)
            g = sm_max("B", u, s3, g)
            g = sm_exp("B", u, s3, g)
            rel[("S", u % 2)] = [g]
            tB["e", u] = g

        def B_norm(u):
            tB["n", u] = sm_nrm("B", u, sm_rec("B", u, tB["e", u]))

        def B_T(u):
            tb = bank[2 + u % 2]
            g = sm_tp("B", u, tb, tB["n", u], last(("T", u % 2)))
            g = cp(PT[u % 3], tb.rearrange("p (j s) -> p j s", j=4), wait=[g] + last(("PT", u % 3)), inc="B.pt",
                   eng="dve")
            rel[("T", u % 2)] = [g]
            tB["pt", u] = g

        def B_AV(u):
            c, bb, hq = u // 8, (u // 4) % 2, u % 4
            b = 2 * c + bb
            for j in range(4):
                h = 4 * hq + j
                g = mm(bank[4][64 * (j % 2):64 * (j % 2) + 64, 128 * (j // 2):128 * (j // 2) + 128],
                       VB[c % 2][:, bb, 64 * h:64 * h + 64], PT[u % 3][:, j, :],
                       wait=([tB["pt", u], tB["v", c, 2 * bb + hq // 2]] + last("O")) if j == 0 else (),
                       inc="B.av" if j == 3 else None)
            rel[("PT", u % 3)] = [g]
            tB["av_pe"] = g
            if u % 8 == 7:
                rel[("VB", c % 2)] = [g]
            g = cp(OT[b % 2][:, 256 * hq:256 * hq + 256], bank[4][:, 0:256],
                   wait=[g] + (last(("OT", b % 2)) if hq == 0 else []), inc="B.ot", eng="dve")
            rel["O"] = [g]
            tB["ot", b] = g

        def B_out(b):
            for k in range(8):
                g = mm(bank[7][:, 0:128], OT[b % 2][:, 128 * k:128 * k + 128], WOB[:, k, :], start=(k == 0),
                       stop=(k == 7), wait=([tB["ot", b], t_wob] + last("Y")) if k == 0 else (),
                       inc="B.y" if k == 7 else None)
            rel[("OT", b % 2)] = [g]
            tB["y_pe"] = g
            g = tt(X[:, b, :], bank[7][:, 0:128], X[:, b, :], ALU.add, wait=[g, tA["xb", b]], inc="B.z")
            rel["Y"] = [g]
            tB["ln", b] = ln_stats(X[:, b, :], [g])

        def B_ln(b):
            tB["x2", b] = ln_apply(X[:, b, :], X[:, b, :], tB["ln", b], [], "B.x2")

        def B_tp(b):
            m = m_bank()
            g = tp(bank[m][:, 0:128], X[:, b, :], wait=[tB["x2", b]] + last(("M", m)), inc="B.xt")
            g = cp(XH[b % 4], bank[m][:, 0:128], wait=[g] + last(("XH", b % 4)), inc="B.xtc", eng="act")
            rel[("M", m)] = [g]
            tB["xt", b] = g

        SC = at("SC", 256)[:, :].rearrange("p (b e) -> p b e", e=8)

        def B_route(b):
            m = m_bank()
            g = mm(bank[m][:, 0:8], XH[b % 4], PAR[:, S_WR0:S_WR0 + 8], wait=[tB["xt", b]] + last(("M", m)),
                   inc="B.r")
            rel[("XH", b % 4)] = [g]
            g = cp(SC[:, b, :], bank[m][:, 0:8], wait=[g], inc="B.rc")
            rel[("M", m)] = [g]
            tB["r", b] = g

        def jobs(c):
            return [lambda k=k: B_q(c, k) for k in range(8)] + [lambda k=k: B_v(c, k) for k in range(4)]

        def jobs_mixed(c):
            q = [lambda k=k: B_q(c, k) for k in range(8)]
            v = [lambda k=k: B_v(c, k) for k in range(4)]
            return q[0:2] + v[0:1] + q[2:4] + v[1:2] + q[4:6] + v[2:3] + q[6:8] + v[3:4]

        RW = [at(f"RW{k}", 128, off=r4 + 512 * k)[:, :] for k in range(10)]
        POS = [at(f"POS{h}", 32, I32, off=r4 + 5120 + 128 * h)[:, :].rearrange("p (k b) -> p k b", k=2)
               for h in range(2)]
        WR = [at(f"WR{h}", 32, off=r4 + 5376 + 128 * h)[:, :].rearrange("p (k b) -> p k b", k=2) for h in range(2)]
        TE = [at(f"TE{h}", 40, I32, off=r4 + 5632 + 192 * h)[:, :] for h in range(2)]
        RV = at("RV", 16 * 12, off=r4 + 6016)[:, :].rearrange("p (k b) -> p k b", k=12)
        MB = at("MB", 128, BF16, off=r4 + 6784)[:, :]
        GA = [at(f"GA{k}", 256, off=r4 + 7168 + 1024 * k)[:, :].rearrange("p (k c) -> p k c", k=2) for k in range(4)]
        XS = [at(f"XS{k}", 128, off=r4 + 11264 + 512 * k)[:, :] for k in range(4)]
        YS = [at(f"YS{k}", 128, off=r4 + 13312 + 512 * k)[:, :] for k in range(4)]
        XST = [at(f"XST{k}", 128, off=r4 + 15360 + 512 * k)[:, :] for k in range(2)]
        NTI = at("NTI", 8, I32)[:, :]
        xs = [nc.dram_tensor(f"xs{h}", [NT * 128, 128], F32, kind="Internal").ap() for h in range(2)]
        ys = [nc.dram_tensor(f"ys{h}", [NT * 128, 128], F32, kind="Internal").ap() for h in range(2)]
        t_z = fill(BTZ, 0.0, inc="k.z", eng="pool")
        t_xz = [dma(xs[h].rearrange("(t p) c -> p t c", p=128), BTZ.unsqueeze(1).broadcast_to((128, NT, 128)),
                    wait=[t_z], inc=f"C.xz{h}", eng="act") for h in range(2)]
        tC = {}

        def route(h):
            s = SC[:, HB * h:HB * h + HB, :]

            def v3(x):
                return x.rearrange("p (b e) -> p b e", e=8)

            def wide(x):
                return x.unsqueeze(2).broadcast_to((128, HB, 8))

            e8 = KON[:, C_E8:C_E8 + 8].unsqueeze(1).broadcast_to((128, HB, 8))
            p, oh1, oh2, t1, t2 = (v3(RW[k]) for k in range(5))
            m1, mp, m2, mv, mv2, den = (RV[:, k, :] for k in range(6))
            n = "R"
            g = red(m1, s, ALU.max, wait=[tB["r", HB * h + HB - 1], tA["end"]] + last("route"), inc=n)
            yield
            g = tt(t1, s, wide(m1), ALU.subtract, wait=[g], inc=n)
            yield
            g = act(p, t1, ACT.Exp, wait=[g], inc=n)
            yield
            g = red(mp, p, ALU.max, wait=[g], inc=n)
            yield
            for oh, m, v in ((oh1, mp, mv), (oh2, m2, mv2)):
                src = p if oh is oh1 else t1
                if oh is oh2:
                    g = stt(RW[3], RW[1], -2.0, RW[0], ALU.mult, ALU.add, wait=[g], inc=n)
                    yield
                    g = red(m, t1, ALU.max, wait=[g], inc=n)
                    yield
                g = tt(t2, src, wide(m), ALU.is_equal, wait=[g], inc=n)
                yield
                g = tt(t2, t2, e8, ALU.mult, wait=[g], inc=n)
                yield
                g = red(v, t2, ALU.max, wait=[g], inc=n)
                yield
                g = tt(oh, t2, wide(v), ALU.is_equal, wait=[g], inc=n)
                yield
            g = tt(MB, RW[1], RW[2], ALU.add, wait=[g], inc=n)
            m = m_bank()
            mm(bank[m][:, 0:128], trib, MB, wait=[g, t_bf2] + last(("M", m)))
            k = mm(bank[m][:, 128:256], oneb, MB, inc="R.mm")
            excl, cnt, incl, off = RW[5], RW[6], RW[7], RW[8]

            def eb(x):
                return x.rearrange("p (e b) -> p e b", b=HB)

            g = cp(excl, bank[m][:, 0:128], wait=[g, k], inc=n)
            g = cp(eb(cnt), bank[m][:, 128:256].rearrange("p (b e) -> p e b", e=8), wait=[g], inc=n)
            rel[("M", m)] = [g]
            yield
            g = tt(den, mp, m2, ALU.add, wait=[g], inc=n)
            g = rcp(RV[:, 6, :], den, wait=[g], inc=n)
            yield
            g = tt(WR[h][:, 0, :], mp, RV[:, 6, :], ALU.mult, wait=[g], inc=n)
            g = tt(WR[h][:, 1, :], m2, RV[:, 6, :], ALU.mult, wait=[g], inc=n)
            yield
            g = scan(incl, KON[:, C_RST:C_RST + 128], cnt, wait=[g], inc=n)
            yield
            g = tt(off, incl, cnt, ALU.subtract, wait=[g], inc=n)
            yield
            nt, tend, tst = (RV[:, k, 0:8] for k in (7, 8, 9))
            g = ts(NTI, eb(incl)[:, :, HB - 1], 127.0, None, ALU.add, wait=[g], inc=n)
            yield
            g = ts(NTI, NTI, 7, None, ALU.logical_shift_right, wait=[g], inc=n)
            g = cp(nt, NTI, wait=[g], inc=n)
            yield
            g = scan(tend, KON[:, C_ONE:C_ONE + 8], nt, wait=[g], inc=n)
            g = tt(tst, tend, nt, ALU.subtract, wait=[g], inc=n)
            yield
            g = ts(tst, tst, 128.0, None, ALU.mult, wait=[g], inc=n)
            g = tt(eb(off), eb(off), tst.unsqueeze(2).broadcast_to((128, 8, HB)), ALU.add, wait=[g], inc=n)
            yield
            g = tt(v3(excl), v3(excl), off.rearrange("p (e b) -> p b e", b=HB), ALU.add, wait=[g], inc=n)
            yield
            for k, oh in enumerate((oh1, oh2)):
                g = tt(t1, oh, v3(excl), ALU.mult, wait=[g], inc=n)
                yield
                g = red(RV[:, 10, :], t1, ALU.add, wait=[g], inc=n)
                g = cp(POS[h][:, k, :], RV[:, 10, :], wait=[g], inc=n)
                yield
            tC["pos", h] = g
            te = RTE[0:1, 0:NT * 8].rearrange("p (j e) -> p j e", e=8)
            g = tt(te, KON[0:1, C_J:C_J + NT].unsqueeze(2).broadcast_to((1, NT, 8)),
                   tend[0:1, :].unsqueeze(1).broadcast_to((1, NT, 8)), ALU.is_ge, wait=[g], inc=n)
            yield
            g = red(RTE[0:1, 320:320 + NT], te, ALU.add, wait=[g], inc=n)
            yield
            g = ts(TE[h][0:1, 0:NT], RTE[0:1, 320:320 + NT], 7.0, None, ALU.min, wait=[g], inc=n)
            tC["te", h] = g
            rel["route"] = [g]
            yield

        def scatter(h):
            for b in range(HB * h, HB * h + HB):
                for k in range(2):
                    idx = POS[h][:, k, b - HB * h:b - HB * h + 1]
                    tC["sc", h] = P.add("pool", lambda e, idx=idx, b=b: e.indirect_dma_start(
                        xs[h], bass.IndirectOffsetOnAxis(ap=idx, axis=0), X[:, b, :], None),
                        [tC["pos", h], tB["x2", b], t_xz[h]], f"C.sc{h}", 16)
                    yield

        t_bend = []
        for j in jobs(0):
            j()
        NU = 4 * NB
        todo = []

        def steps(gens):
            for g in gens:
                yield from g()

        t_wc = dma(WCt, a["we"], wait=[tA["end_pe"], tA["end"]], inc="ld.wc")
        bg = steps([lambda: route(0), lambda: scatter(0)])
        for i in range(NU + 14):
            if i < NU:
                B_S(i)
            if 1 <= i <= NU:
                B_norm(i - 1)
            if i < NU:
                if i % 8 == 0 and i // 8 + 1 < NB // 2:
                    todo = jobs_mixed(i // 8 + 1)
                n = 2 if i % 2 == 0 else 1
                for _ in range(n):
                    if todo:
                        todo.pop(0)()
            if 2 <= i < NU + 2:
                B_T(i - 2)
            if 3 <= i < NU + 3:
                B_AV(i - 3)
            for fn, lag in ((B_route, 11), (B_tp, 10), (B_ln, 8), (B_out, 7)):
                j = i - lag
                if j >= 0 and j % 4 == 0 and j // 4 < NB:
                    fn(j // 4)
            if i > 4 * HB + 8:
                next(bg, None)
                next(bg, None)
        for _ in bg:
            pass

        if stop == "B":
            finish(P, nc, dma, X, out, [tB["x2", b] for b in range(NB)])
            return

        WS = [at(f"WS{k}", WE, off=r3 + 4608 * k)[:, :] for k in range(3)]
        HS = [at(f"HS{k}", 384, off=o_ot + 1536 * k)[:, :] for k in range(2)]
        AC = [at(f"AC{k}", 384, off=o_ot + 3072 + 1536 * k)[:, :] for k in range(2)]
        b_end = [tB["r", NB - 1], tB["ot", NB - 1], tB["y_pe"]]
        regs = {}

        def staged(o, w, width, idx, wait, inc):
            def fn(e):
                if "r" not in regs:
                    regs["r"] = e.alloc_register("expert")
                e.reg_load(regs["r"], idx)
                v = e.snap(regs["r"], min_val=0, max_val=7)
                return e.tensor_copy(o, w[:, bass.ds(v * width, width)])
            return P.add("dve", fn, wait, inc)

        def C_load(t):
            h, j, k = t // NT, t % NT, t % 4
            tC["xs", t] = dma(XS[k], xs[h][128 * j:128 * j + 128, :],
                                 wait=[tC["sc", h], tA["end"], tA["end_pe"]] + last(("XS", k)), inc=f"C.xs{k}")

        def C_T(t):
            h, j = t // NT, t % NT
            m = m_bank()
            g = tp(bank[m][:, 0:128], XS[t % 4], wait=[tC["xs", t]] + last(("M", m)), inc="C.t")
            rel[("XS", t % 4)] = [g]
            g = cp(XST[t % 2], bank[m][:, 0:128], wait=[g] + last(("XST", t % 2)), inc="C.tc", eng="act")
            rel[("M", m)] = [g]
            tC["xt", t] = g
            tC["ws", t] = staged(WS[t % 3], WCt, WE, TE[h][0:1, j:j + 1],
                                    [tC["te", h], t_wc] + last(("WS", t % 3)) + b_end, "C.ws")

        def C_GU(t):
            for u in range(2):
                bk = 1 + 2 * u + t % 2
                for f in range(3):
                    g = mm(bank[bk][:, 128 * f:128 * f + 128], WS[t % 3][:, 384 * u + 128 * f:384 * u + 128 * f + 128],
                           XST[t % 2], wait=([tC["xt", t], tC["ws", t]] + last(("GU", bk))) if f == 0 else (),
                           inc="C.gu" if f == 2 else None)
                if u == 0:
                    s = act(HS[t % 2], bank[bk][:, 0:384], ACT.Silu, wait=[g] + last(("HS", t % 2)), inc="C.si")
                    rel[("GU", bk)] = [s]
            rel[("XST", t % 2)] = [g]
            g = tt(AC[t % 2], HS[t % 2], bank[3 + t % 2][:, 0:384], ALU.mult, wait=[s, g] + last(("AC", t % 2)),
                   inc="C.ac")
            rel[("GU", 3 + t % 2)] = [g]
            rel[("HS", t % 2)] = [g]
            tC["ac", t] = g

        def C_D(t):
            h, j = t // NT, t % NT
            for f in range(3):
                g = mm(bank[7][:, 0:128], AC[t % 2][:, 128 * f:128 * f + 128],
                       WS[t % 3][:, 768 + 128 * f:768 + 128 * f + 128], start=(f == 0), stop=(f == 2),
                       wait=([tC["ac", t]] + last("CY")) if f == 0 else (), inc="C.d" if f == 2 else None)
            rel[("WS", t % 3)] = [g]
            rel[("AC", t % 2)] = [g]
            tC["d_pe"] = g
            k = t % 4
            g = cp(YS[k], bank[7][:, 0:128], wait=[g] + last(("YS", k)), inc="C.yc", eng="act")
            rel["CY"] = [g]
            tC["y_act"] = g
            g = dma(ys[h][128 * j:128 * j + 128, :], YS[k], wait=[g], inc=f"C.ys{k}", eng="act")
            rel[("YS", k)] = [g]
            tC["ys", h, k] = g

        rel["DT"], rel["CY"] = last(("S", 0)), last("Y")
        for k, key in ((1, ("S", 1)), (2, ("T", 0)), (3, ("T", 1)), (4, "O")):
            rel[("GU", k)] = last(key)

        def experts(beside):
            n = 2 * NT
            for i in range(n + 4):
                if i < n:
                    C_load(i)
                if 2 <= i < n + 2:
                    C_T(i - 2)
                if 3 <= i < n + 3:
                    C_GU(i - 3)
                if i >= 4:
                    C_D(i - 4)
                beside(i)

        def gather(b):
            h, k = b // HB, b % 4
            for n in range(2):
                idx = POS[h][:, n, b - HB * h:b - HB * h + 1]
                g = P.add("pool", lambda e, idx=idx, n=n: e.indirect_dma_start(
                    GA[k][:, n, :], None, ys[h], bass.IndirectOffsetOnAxis(ap=idx, axis=0)),
                    [tC["ys", h, q] for q in range(4)] + last(("GA", k)), f"C.ga{k}", 16)
            return g

        def combine(b, g):
            h, k = b // HB, b % 4
            g = stt(X[:, b, :], GA[k][:, 0, :], WR[h][:, 0, b % HB:b % HB + 1], X[:, b, :], ALU.mult, ALU.add,
                    wait=[g], inc="C.z")
            g = stt(X[:, b, :], GA[k][:, 1, :], WR[h][:, 1, b % HB:b % HB + 1], X[:, b, :], ALU.mult, ALU.add,
                    wait=[g], inc="C.z")
            rel[("GA", k)] = [g]
            return ln_stats(X[:, b, :], [g])

        bg = steps([lambda: route(1), lambda: scatter(1)])

        CU = at("CU", 2048, off=r0)[0:16, :].rearrange("p (h l) -> p h l", h=16)
        XP = at("XP", 3 * 132, off=r0 + 8192)[:, :].rearrange("p (k s) -> p k s", k=3)
        CO = at("CO", 384, off=r0 + 9792)[:, :].rearrange("p (k s) -> p k s", k=3)
        XTK = at("XTK", 128, off=r0 + 11328)[:, :]
        CUT = at("CUT", 16, off=r0 + 11840)[:, :]
        WDT = at("WDT", 1024, off=r0 + 12288)[:, :].rearrange("p (b c) -> p b c", b=8)
        CM = at("CM", 2048, off=r2 + 33024)[:, :].rearrange("p (h l) -> p h l", h=16)
        X3T = [at(f"X3T{k}", 128, off=r2 + 41216 + 512 * k)[:, :] for k in range(4)]
        WIN = at("WIN", 384, off=r2 + 43264)[:, :].rearrange("p (k c) -> p k c", k=3)
        WOD = at("WOD", 128, off=r2 + 44800)[:, :]
        EL = at("EL", 512, off=r2 + 45312)[:, :].rearrange("p (j l) -> p j l", j=4)
        Y0 = at("Y0", 128, off=r2 + 47360)[:, :]
        Y0T = at("Y0T", 128, off=r2 + 47872)[:, :]
        RN = [at(f"RN{g}", 128, off=o_ot + 6144 + 512 * g)[:, :] for g in range(4)]
        DW = [at(f"DW{k}", 128, off=o_bt if k == 3 else None)[:, :] for k in range(4)]
        DO = [at(f"DO{k}", 256, off=r3 + 14336 + 1024 * k)[:, :].rearrange("p (j s) -> p j s", j=2) for k in range(2)]
        WX = at("WX", 1024, off=r4)[:, :].rearrange("p (k c) -> p k c", k=8)
        SEL = KON[:, C_SEL:C_SEL + 1024].rearrange("p (b c) -> p b c", b=8)
        ones = KON[:, C_ONE:C_ONE + 128]
        t_win = dma(WIN, a["win"], wait=b_end + [tB["av_pe"]], inc="ld.win", eng="act")
        t_wdt = dma(WDT, a["wdt"], wait=b_end, inc="ld.wdt", eng="act")
        t_wod = dma(WOD, a["wod"], wait=b_end + [tB["av_pe"]], inc="ld.wod", eng="act")
        t_wf = dma(WFt, a["wf"], wait=b_end + [tB["av_pe"]], inc="ld.wf", eng="act")
        t_xp = fill(XP, 0.0, wait=b_end, inc="D.xp", eng="pool")
        tD = {}
        queue = []

        def D_tp(b):
            m = m_bank()
            g = tp(bank[m][:, 0:128], X[:, b, :], wait=[tC["x3", b]] + last(("M", m)), inc="D.xt")
            g = cp(X3T[b % 4], bank[m][:, 0:128], wait=[g, tB["av_pe"]] + last(("X3T", b % 4)), inc="D.xtc", eng="act")
            rel[("M", m)] = [g]
            tD["x3t", b] = g

        def D_dt(b):
            g = mm(bank[0][:, 0:128], WDT[:, b % 8, :], X3T[b % 4], start=(b % 8 == 0), stop=(b % 8 == 7),
                   wait=[tD["x3t", b], t_wdt] + (last("DT") if b % 8 == 0 else []), inc="D.dt")
            rel[("X3T", b % 4)] = [g]
            tD["dt", b] = g

        def D_conv():
            m = m_bank()
            for k in range(3):
                g = mm(bank[m][:, 128 * k:128 * k + 128], WIN[:, k, :], X3T[0],
                       wait=([tD["x3t", 0], t_win] + last(("M", m))) if k == 0 else (), inc="D.in" if k == 2 else None)
            rel[("X3T", 0)] = [g]
            g = cp(XP[:, :, 3:131], bank[m][:, 0:384].rearrange("p (k s) -> p k s", k=3), wait=[g, t_xp], inc="S")
            rel[("M", m)] = [g]
            tD["conv"] = g

        def ssd():
            g = tD["conv"]
            for k in range(3):
                w = S_CW + 4 * k
                g = ts(CO[:, k, :], XP[:, k, 0:128], PAR[:, w:w + 1], PAR[:, S_CB + k:S_CB + k + 1], ALU.mult, ALU.add,
                       wait=[g, t_xp], inc="S")
                for i in range(1, 4):
                    g = stt(CO[:, k, :], XP[:, k, i:i + 128], PAR[:, w + i:w + i + 1], CO[:, k, :], ALU.mult, ALU.add,
                            wait=[g], inc="S")
                    yield
            c = tt(CM, CO[:, 0, :].unsqueeze(1).broadcast_to((128, 16, 128)),
                   KON[:, C_HM:C_HM + 16].unsqueeze(2).broadcast_to((128, 16, 128)), ALU.mult,
                   wait=[g, tB["av_pe"]], inc="S", eng="pool")
            m = m_bank()
            k = tp(bank[m][:, 0:128], CO[:, 2, :], wait=[g] + last(("M", m)), inc="S")
            k = cp(XTK, bank[m][:, 0:128], wait=[k], inc="S")
            rel[("M", m)] = [k]
            yield
            u = tt(CU, DW[2][0:16, :].unsqueeze(1).broadcast_to((16, 16, 128)),
                   KON[0:16, C_I16:C_I16 + 16].unsqueeze(2).broadcast_to((16, 16, 128)), ALU.mult,
                   wait=[tD["cum", 0], t_kon] + b_end, inc="S")
            m = m_bank()
            q = P.add("pe", lambda e: e.transpose(bank[m][:, 0:16], DW[2][0:16, :], ident[0:16, 0:16]),
                      [tD["cum", 0]] + last(("M", m)), "S")
            q = ts(CUT, bank[m][:, 0:16], -1.0, None, ALU.mult, wait=[q], inc="S")
            rel[("M", m)] = [q]
            rel["DW2"] = [q, u]
            yield
            for hg in range(4):
                m = m_bank()
                mm(bank[m], identb, masksb, start=True, stop=False, wait=[t_bf2] + last(("M", m)))
                d = mm(bank[m], ones[0:16, :], CU[:, 4 * hg:4 * hg + 4, :], start=False, stop=True, wait=[u], inc="S")
                for j in range(4):
                    d = act(EL[:, j, :], bank[m][:, 128 * j:128 * j + 128], ACT.Exp,
                            bias=CUT[:, 4 * hg + j:4 * hg + j + 1], wait=[d, q, tB["av_pe"]] + last("EL"), inc="S")
                rel[("M", m)] = [d]
                m = m_bank()
                w = mm(bank[m], CO[:, 1, :], CM[:, 4 * hg:4 * hg + 4, :], wait=[c, g] + last(("M", m)), inc="S")
                w = tt(EL, EL, bank[m].rearrange("p (j l) -> p j l", j=4), ALU.mult, wait=[w, d], inc="S")
                rel[("M", m)] = [w]
                yield
                yield
                m = m_bank()
                for j in range(4):
                    h = 4 * hg + j
                    y = mm(bank[m][:, 8 * j:8 * j + 8], EL[:, j, :], XTK[:, 8 * h:8 * h + 8],
                           wait=([w, k] + last(("M", m))) if j == 0 else (), inc="S")
                rel["EL"] = [y]
                y = cp(Y0[:, 32 * hg:32 * hg + 32], bank[m][:, 0:32], wait=[y, tB["av_pe"]], inc="S")
                rel[("M", m)] = [y]
                yield
            m = m_bank()
            y = tp(bank[m][:, 0:128], Y0, wait=[y] + last(("M", m)), inc="S")
            y = cp(Y0T, bank[m][:, 0:128], wait=[y], inc="S")
            rel[("M", m)] = [y]
            tD["y0"] = y
            yield

        def dgroup(g):
            n = "D.n"
            x = stt(DW[1], RN[g], -1.0, RN[g], ALU.mult, ALU.max, wait=[tD["dtb", g]] + last("DW"), inc=n)
            yield
            x = act(DW[1], DW[1], ACT.Exp, scale=-1.0, wait=[x], inc=n)
            x = act(DW[1], DW[1], ACT.Ln, bias=1.0, wait=[x], inc=n)
            yield
            x = stt(DW[0], RN[g], 0.0, DW[1], ALU.max, ALU.add, wait=[x], inc=n)
            x = ts(DW[0], DW[0], PAR[:, S_AP:S_AP + 1], None, ALU.mult, wait=[x], inc=n)
            yield
            x = scan(DW[2], ones, DW[0], wait=[x] + last("DW2"), inc=n)
            tD["cum", g] = x
            yield
            y = act(DW[1], DW[2], ACT.Exp, wait=[x], inc=n)
            x = act(DW[0], DW[2], ACT.Exp, scale=-1.0, wait=[x], inc=n)
            yield
            rel["DW2"] = [x]
            x = scan(DW[3], ones, DW[0], wait=[x, tA["xb", NB - 1]], inc=n)
            yield
            x = tt(DW[1], DW[1], DW[3], ALU.mult, wait=[x, y], inc=n)
            x = rcp(RN[g], DW[1], wait=[x, tB["y_pe"]], inc=n)
            rel["DW"] = [x]
            tD["rn", g] = x
            yield
            if g == 0:
                yield from ssd()

        def front(bs):
            st = {}
            n = len(bs)
            for i in range(n + 8):
                if i < n:
                    st["g", i] = gather(bs[i])
                if 3 <= i < n + 3:
                    st["l", i - 3] = combine(bs[i - 3], st["g", i - 3])
                if 4 <= i < n + 4:
                    b = bs[i - 4]
                    tC["x3", b] = ln_apply(X[:, b, :], X[:, b, :], st["l", i - 4], [], "C.x3")
                if 6 <= i < n + 6:
                    D_tp(bs[i - 6])
                if 7 <= i < n + 7:
                    b = bs[i - 7]
                    D_dt(b)
                    if b == 0:
                        D_conv()
                    if b % 8 == 7:
                        tD["dtb", b // 8] = ts(RN[b // 8], bank[0][:, 0:128], PAR[:, S_DTB:S_DTB + 1], None, ALU.add,
                                               wait=[tD["dt", b], tB["y_pe"]], inc="D.n")
                        rel["DT"] = [tD["dtb", b // 8]]
                        queue.append(dgroup(b // 8))
                yield

        def from_queue():
            if queue and next(queue[0], "end") == "end":
                queue.pop(0)

        fr = front(range(HB))

        def beside(i):
            if i < NT - 1:
                next(bg, None)
                next(bg, None)
            elif i == NT - 1:
                for _ in bg:
                    pass
                tD["wx"] = dma(WX, a["wx"], wait=[tC["te", 1]] + last("route"), inc="ld.wx", eng="act")
            elif i >= NT + 4:
                next(fr, None)
                from_queue()
                from_queue()

        experts(beside)
        while queue:
            from_queue()
        if stop == "C":
            finish(P, nc, dma, X, out, [tC["x3", b] for b in range(HB)] + [t_wod, t_wf, tD["wx"]])
            return

        def D_expand(v):
            m = m_bank()
            for j in range(2):
                b = 2 * v + j
                g = mm(bank[m][:, 128 * j:128 * j + 128], SEL[:, b % 8, :], RN[b // 8],
                       wait=([tD["rn", b // 8]] + last(("M", m))) if j == 0 else (), inc="D.e" if j else None)
            g = tt(DO[v % 2], bank[m][:, 0:256].rearrange("p (j s) -> p j s", j=2),
                   Y0T.unsqueeze(1).broadcast_to((128, 2, 128)), ALU.mult,
                   wait=[g, tD["y0"], tB["y_pe"]] + last(("DO", v % 2)), inc="D.o")
            rel[("M", m)] = [g]
            tD["o", v] = g

        def D_out(v):
            m = m_bank()
            for j in range(2):
                g = mm(bank[m][:, 128 * j:128 * j + 128], DO[v % 2][:, j, :], WOD,
                       wait=([tD["o", v], t_wod] + last(("M", m))) if j == 0 else (), inc="D.y" if j else None)
            rel[("DO", v % 2)] = [g]
            x = X[:, 2 * v:2 * v + 2, :]
            g = tt(x, bank[m][:, 0:256].rearrange("p (j s) -> p j s", j=2), x, ALU.add,
                   wait=[g] + [tC["x3", 2 * v + j] for j in range(2)] + [tD["x3t", 2 * v + j] for j in range(2)],
                   inc="D.z")
            rel[("M", m)] = [g]
            for j in range(2):
                tD["ln", 2 * v + j] = ln_stats(X[:, 2 * v + j, :], [g])

        def D_ln(v):
            for b in (2 * v, 2 * v + 1):
                tD["x4", b] = ln_apply(X[:, b, :], X[:, b, :], tD["ln", b], [], "D.x4")

        def D_x4t(v):
            m = m_bank()
            for j in range(2):
                g = tp(bank[m][:, 128 * j:128 * j + 128], X[:, 2 * v + j, :],
                       wait=([tD["x4", 2 * v], tD["x4", 2 * v + 1]] + last(("M", m))) if j == 0 else (),
                       inc="D.x4t" if j else None)
            g = cp(XT[:, 256 * v:256 * v + 256], bank[m][:, 0:256],
                   wait=[g, tD["y0"], tD["rn", 3] if v >= 12 else None], inc="D.x4c", eng="act")
            rel[("M", m)] = [g]
            tD["x4t", v] = g

        EQ = [at(f"EQ{k}", 1024, off=r1 + 4096 * k)[:, :].rearrange("p (k n) -> p k n", k=4) for k in range(3)]
        EV = [at(f"EV{k}", 512, off=r1 + 12288 + 2048 * k)[:, :].rearrange("p (j c) -> p j c", j=4) for k in range(3)]
        WSF = [at(f"WSF{k}", WF, off=r1 + 18432 + 4160 * k)[:, :] for k in range(3)]
        EC = [at(f"EC{k}", 512, off=r3 + 2048 * k)[:, :].rearrange("p (d n) -> p d n", d=2) for k in range(2)]
        EX = [at(f"EX{k}", 256, off=r3 + 4096 + 1024 * k)[:, :] for k in range(2)]
        ED = [at(f"ED{k}", 256, off=r3 + 6144 + 1024 * k)[:, :] for k in range(2)]
        EZ = [at(f"EZ{k}", 256, off=r3 + 8192 + 1024 * k)[:, :] for k in range(2)]
        HT = [at(f"HT{k}", 512, off=r3 + 10240 + 2048 * k)[:, :].rearrange("p (k n) -> p k n", k=4) for k in range(2)]
        X5T = [at(f"X5T{k}", 128, off=r1 + 30912 + 512 * k)[:, :] for k in range(8)]
        FZ = [at(f"FZ{k}", 128, off=r4 + 11264 + 512 * k)[:, :] for k in range(2)]
        FS = at("FS", 64, off=r4 + 12288)[:, :].rearrange("p (k e) -> p k e", k=8)
        FI = at("FI", 64, U32, off=r4 + 12544)[:, :].rearrange("p (k e) -> p k e", k=8)
        MS = at("MS", 16, off=r4 + 12800)[:, :]
        c_end = [tC["ac", 2 * NT - 1], tC["d_pe"], tC["y_act"]] + [tC["ys", 1, q] for q in range(4)]
        SCL = float(1.0 / np.sqrt(np.float32(128.0)))
        t_nbg = ts(PAR[:, S_N + 1:S_N + 2], PAR[:, S_BG:S_BG + 1], -1.0, None, ALU.mult, wait=[t_par], inc="E.nbg")
        tE = {}

        def par(k):
            return PAR[:, k:k + 1]

        def E_qk(v):
            x4 = XT[:, 256 * v:256 * v + 256]
            cx = CT[:, 256 * v:256 * v + 256]
            r = v % 3
            xw = [tD["x4t", v], tD["wx"]]
            m = m_bank()
            mm(bank[m][:, 0:256], WX[:, 0, :], x4, wait=xw + last(("M", m)))
            g = mm(bank[m][:, 256:512], WX[:, 3, :], cx, inc="E.q")
            g0 = ts(EQ[r][:, 0, :], bank[m][:, 0:256], par(S_BQC), SCL, ALU.add, ALU.mult,
                    wait=[g] + last(("EQ", r)) + c_end, inc="E.qc")
            tE["q", v] = ts(EQ[r][:, 1, :], bank[m][:, 256:512], par(S_BQS), SCL, ALU.add, ALU.mult, inc="E.qc")
            rel[("M", m)] = [tE["q", v]]
            m = m_bank()
            mm(bank[m][:, 0:256], WX[:, 1, :], cx, wait=last(("M", m)))
            g = mm(bank[m][:, 256:512], WX[:, 4, :], x4, inc="E.k")
            act(EQ[r][:, 2, :], bank[m][:, 0:256], ACT.Identity, bias=par(S_BKS), wait=[g] + last(("EQ", r)) + c_end)
            tE["k", v] = act(EQ[r][:, 3, :], bank[m][:, 256:512], ACT.Identity, bias=par(S_BKC), inc="E.kc")
            rel[("M", m)] = [tE["k", v]]

        def E_v(v):
            x4 = XT[:, 256 * v:256 * v + 256]
            cx = CT[:, 256 * v:256 * v + 256]
            r = v % 3
            m = m_bank()
            for j in range(4):
                src = (cx if j < 2 else x4)[:, 128 * (j % 2):128 * (j % 2) + 128]
                g = mm(bank[m][:, 128 * j:128 * j + 128], src, WX[:, 2 if j < 2 else 5, :],
                       wait=last(("M", m)) if j == 0 else (), inc="E.v" if j == 3 else None)
            tE["v", v] = cp(EV[r], bank[m].rearrange("p (j c) -> p j c", j=4), wait=[g] + last(("EV", r)) + c_end,
                            inc="E.vc", eng="act")
            rel[("M", m)] = [tE["v", v]]

        def E_S(v):
            sb, r = bank[1], v % 3
            for j in range(4):
                c = slice(128 * (j % 2), 128 * (j % 2) + 128)
                g = mm(sb[:, 128 * j:128 * j + 128], EQ[r][:, j // 2, c], EQ[r][:, 2 + j // 2, c],
                       wait=([tE["q", v], tE["k", v]] + last("ES")) if j == 0 else (),
                       inc="E.s" if j == 3 else None)
            rel[("EQ", r)] = [g]
            s3 = sb.rearrange("p (j s) -> p j s", j=4)
            g = sm_max("E", v, s3, g)
            g = sm_exp("E", v, s3, g)
            rel["ES"] = [g]
            tE["e", v] = g

        def E_norm(v):
            tE["n", v] = sm_nrm("E", v, sm_rec("E", v, tE["e", v]))

        def E_T(v):
            g = sm_tp("E", v, bank[3], tE["n", v], last("ET"))
            g = cp(PT[v % 3], bank[3].rearrange("p (j s) -> p j s", j=4), wait=[g] + last(("PT", v % 3)), inc="E.pt")
            rel["ET"] = [g]
            tE["pt", v] = g

        def E_AV(v):
            for j in range(4):
                g = mm(bank[4][:, 128 * j:128 * j + 128], EV[v % 3][:, j, :], PT[v % 3][:, j, :],
                       wait=([tE["pt", v], tE["v", v]] + last("EO")) if j == 0 else (), inc="E.av" if j == 3 else None)
            rel[("PT", v % 3)] = [g]
            rel[("EV", v % 3)] = [g]
            act(EC[v % 2][:, 0, :], bank[4][:, 0:256], ACT.Identity, bias=par(S_BVS),
                wait=[g] + last(("EC", v % 2)) + c_end)
            g = act(EC[v % 2][:, 1, :], bank[4][:, 256:512], ACT.Identity, bias=par(S_BVC), inc="E.ec")
            rel["EO"] = [g]
            tE["ec", v] = g
            tE["d", v] = tt(ED[v % 2], EC[v % 2][:, 0, :], EC[v % 2][:, 1, :], ALU.subtract,
                            wait=[g] + last(("ED", v % 2)) + c_end, inc="E.d", eng="pool")

        def E_gate(v):
            m = m_bank()
            mm(bank[m][:, 0:256], WX[:, 6, :], EC[v % 2][:, 0, :], start=True, stop=False,
               wait=[tE["ec", v]] + last(("M", m)))
            g = mm(bank[m][:, 0:256], WX[:, 7, :], EC[v % 2][:, 1, :], start=False, stop=True, inc="E.g")
            tE["g", v] = g
            g = act(EX[v % 2], bank[m][:, 0:256], ACT.Exp, bias=PAR[:, S_N + 1:S_N + 2], scale=-1.0,
                    wait=[g, t_nbg] + last(("EX", v % 2)) + c_end, inc="E.ex")
            rel[("M", m)] = [g]
            tE["ex", v] = g

        def E_mix(v):
            g = ts(EX[v % 2], EX[v % 2], 1.0, None, ALU.add, wait=[tE["ex", v]], inc="E.e1")
            g = rcp(EX[v % 2], EX[v % 2], wait=[g], inc="E.r")
            g = tt(ED[v % 2], ED[v % 2], EX[v % 2], ALU.mult, wait=[g, tE["d", v]], inc="E.m", eng="pool")
            rel[("EX", v % 2)] = [g]
            g = tt(ED[v % 2], ED[v % 2], EC[v % 2][:, 1, :], ALU.add, wait=[g], inc="E.m", eng="pool")
            rel[("EC", v % 2)] = [g, tE["g", v]]
            g = tt(EZ[v % 2], ED[v % 2], XT[:, 256 * v:256 * v + 256], ALU.add, wait=[g] + last(("EZ", v % 2)) + c_end,
                   inc="E.z", eng="pool")
            rel[("ED", v % 2)] = [g]
            tE["z", v] = g

        def E_tp(v):
            m = m_bank()
            for j in range(2):
                g = tp(bank[m][:, 128 * j:128 * j + 128], EZ[v % 2][:, 128 * j:128 * j + 128],
                       wait=([tE["z", v]] + last(("M", m))) if j == 0 else (), inc="E.zt" if j else None)
            rel[("EZ", v % 2)] = [g]
            g = cp(X[:, 2 * v:2 * v + 2, :], bank[m][:, 0:256].rearrange("p (j s) -> p j s", j=2),
                   wait=[g, tD["x4t", v]], inc="E.zc", eng="act")
            rel[("M", m)] = [g]
            tE["zc", v] = g

        def E_st(v):
            for b in (2 * v, 2 * v + 1):
                tE["ln", b] = ln_stats(X[:, b, :], [tE["zc", v]])

        def E_ln(v):
            for b in (2 * v, 2 * v + 1):
                tE["x5", v] = ln_apply(X[:, b, :], X[:, b, :], tE["ln", b], [], "E.x5")

        tF = {}

        def F_top(v):
            m = m_bank()
            for j in range(2):
                g = tp(bank[m][:, 128 * j:128 * j + 128], X[:, 2 * v + j, :],
                       wait=([tE["x5", v]] + last(("M", m))) if j == 0 else (), inc="F.xt" if j else None)
            tF["xt", v] = g
            for j in range(2):
                b = 2 * v + j
                g = act(X5T[b % 8], bank[m][:, 128 * j:128 * j + 128], ACT.Copy, accum=MS[:, b % 16:b % 16 + 1],
                        wait=[tF["xt", v]] + last(("X5T", b % 8)) + last(("MS", b % 16)) + c_end, inc="F.x")
                tF["x", b] = g
            rel[("M", m)] = [g]

        def F_score(v):
            m = m_bank()
            for j in range(2):
                b = 2 * v + j
                g = mm(bank[m][0:1, 8 * j:8 * j + 8], MS[:, b % 16:b % 16 + 1], PAR[:, S_WR1:S_WR1 + 8],
                       wait=[tF["x", b]] + (last(("M", m)) if j == 0 else []), inc="F.s")
                rel[("MS", b % 16)] = [g]
            for j in range(2):
                b = 2 * v + j
                k = b % 4
                s = FS[0:1, k, :]
                q = stt(s, bank[m][0:1, 8 * j:8 * j + 8], 1.0 / 128, PAR[0:1, S_BR:S_BR + 8], ALU.mult, ALU.add,
                        wait=[g] + c_end, inc="F.t")
                if j == 1:
                    rel[("M", m)] = [q]
                q = P.add("dve", lambda e, k=k: e.max(FS[0:1, 4 + k, :], FS[0:1, k, :]), [q], "F.t")
                q = P.add("dve", lambda e, k=k: e.max_index(FI[0:1, k, :], FS[0:1, 4 + k, :], FS[0:1, k, :]),
                          [q], "F.t")
                tF["i", b] = q

        def F_w(b):
            tF["w", b] = staged(WSF[b % 3], WFt, WF, FI[0:1, b % 4, 0:1], [tF["i", b], t_wf] + last(("WSF", b % 3))
                                + c_end, "F.w")

        def F_h(b):
            w, k = WSF[b % 3], b % 2
            for f in range(4):
                g = mm(bank[7][:, 128 * f:128 * f + 128], w[:, 128 * f:128 * f + 128], X5T[b % 8],
                       wait=([tF["w", b], tF["x", b]] + last("FH")) if f == 0 else (), inc="F.h" if f == 3 else None)
            for f in range(4):
                q = act(HT[k][:, f, :], bank[7][:, 128 * f:128 * f + 128], ACT.Relu, bias=w[:, 1024 + f:1025 + f],
                        wait=([g] + last(("HT", k)) + c_end) if f == 0 else (), inc="F.r" if f == 3 else None)
            rel["FH"] = [q]
            tF["h", b] = q

        def F_out(b):
            w, k = WSF[b % 3], b % 2
            m = m_bank()
            for f in range(4):
                g = mm(bank[m][:, 0:128], w[:, 512 + 128 * f:640 + 128 * f], HT[k][:, f, :], start=(f == 0),
                       stop=(f == 3), wait=([tF["h", b]] + last(("M", m))) if f == 0 else (),
                       inc="F.o" if f == 3 else None)
            rel[("HT", k)] = [g]
            g = stt(FZ[k], bank[m][:, 0:128], w[:, 1028:1029], X5T[b % 8], ALU.add, ALU.add,
                    wait=[g] + last(("FZ", k)) + c_end, inc="F.z")
            rel[("M", m)] = [g]
            rel[("WSF", b % 3)] = [g]
            rel[("X5T", b % 8)] = [g]
            tF["z", b] = g

        def F_tp(b):
            m = m_bank()
            g = tp(bank[m][:, 0:128], FZ[b % 2], wait=[tF["z", b]] + last(("M", m)), inc="F.zt")
            rel[("FZ", b % 2)] = [g]
            g = cp(X[:, b, :], bank[m][:, 0:128], wait=[g, tF["xt", b // 2]], inc="F.zc", eng="act")
            rel[("M", m)] = [g]
            tF["zc", b] = g

        def F_st(b):
            tF["ln", b] = ln_stats(X[:, b, :], [tF["zc", b]])

        def F_ln(b):
            g = ln_apply(X[:, b, :], X[:, b, :], tF["ln", b], [], "F.y")
            tF["st"] = dma(out[b], X[:, b, :], wait=[g], inc="st")

        fr = front(range(HB, NB))
        rel["FH"], rel["EO"], rel["ET"] = last("CY"), last(("GU", 4)), last(("GU", 3))
        rel["ES"], rel[("M", 2)] = last(("GU", 1)), last(("GU", 2))
        ring.append(2)
        NV = NB // 2

        def first(fn):
            return lambda v: fn(2 * v)

        def second(fn):
            return lambda v: fn(2 * v + 1)

        def both(fn):
            return lambda v: (fn(2 * v), fn(2 * v + 1))

        plan = ((D_expand, 0), (D_ln, 1), (E_norm, 3), (E_AV, 4), (E_qk, 2), (first(F_w), 8), (E_mix, 5), (F_top, 7),
                (E_st, 6), (E_v, 3), (first(F_out), 9), (second(F_tp), 10), (second(F_h), 9), (both(F_ln), 11),
                (E_S, 2), (D_out, 0), (E_gate, 4), (second(F_w), 8), (E_T, 3), (D_x4t, 1), (second(F_out), 9),
                (E_tp, 5), (first(F_h), 8), (F_score, 7), (E_ln, 6), (first(F_tp), 9), (both(F_st), 10))
        for s in range(NV + 12):
            next(fr, None)
            next(fr, None)
            for _ in range(4):
                from_queue()
            for fn, lag in plan:
                if 0 <= s - lag < NV:
                    fn(s - lag)
        finish(P, nc, dma, X, out, [], [tF["st"]])


def finish(P, nc, dma, X, out, toks, done=None):
    if done is None:
        done = [dma(out.rearrange("b t c -> t b c"), X, wait=toks, inc="st")]
    P.add("sp", lambda e: e.nop(), done, None)
    with nc.Block() as blk:
        @blk.sync
        def _(e):
            P.play("sp", e)

        @blk.scalar
        def _(e):
            P.play("act", e)

        @blk.vector
        def _(e):
            P.play("dve", e)

        @blk.gpsimd
        def _(e):
            P.play("pool", e)

        @blk.tensor
        def _(e):
            P.play("pe", e)


def layouts(i):
    f = np.float32

    def pad_heads(w, times):
        n = w.shape[0] // 8
        o = np.zeros((128, 8, 32), f)
        o[:, :, :n * times] = np.tile(w.T.reshape(128, 8, n), (1, 1, times))
        return o.reshape(128, 256)

    par = np.zeros((128, S_N), f)
    par[:, S_SCALE] = i["L0_attn_scale"]
    par[:, S_GAMMA] = i["L0_xattn_ln_gamma"]
    par[:, S_BETA] = i["L0_xattn_ln_beta"]
    par[:, S_GATE] = i["L0_xattn_gate"][0]
    par[:, S_DTB] = np.tile(i["L1_attn_dt_bias"], 8)
    par[:, S_AP] = np.tile(i["L1_attn_A_param"], 8)
    par[:, S_CW:S_CW + 12] = i["L1_attn_conv_w"].reshape(3, 128, 4).transpose(1, 0, 2).reshape(128, 12)
    par[:, S_CB:S_CB + 3] = i["L1_attn_conv_b"].reshape(3, 128).T
    for k, n in enumerate(("bq_c", "bk_s", "bv_s", "bq_s", "bk_c", "bv_c", "bg")):
        par[:, S_BQC + k] = i["L1_xattn_" + n]
    par[:, S_BR:S_BR + 8] = i["L1_ffn_br"]
    par[:, S_WR0:S_WR0 + 8] = i["L0_ffn_router_w"]
    par[:, S_WR1:S_WR1 + 8] = i["L1_ffn_Wr"]

    x, ctx = i["x"], i["ctx_1024"]
    wo = np.zeros((8, 32, 128), f)
    wo[:, :16] = i["L0_attn_Wo"].T.reshape(8, 16, 128)
    wkv = i["L0_xattn_w_kv"]
    we = np.zeros((128, 8, WE), f)
    we[:, :, 0:352] = i["L0_ffn_gate_proj"].transpose(1, 0, 2)
    we[:, :, 384:736] = i["L0_ffn_up_proj"].transpose(1, 0, 2)
    dn = np.zeros((8, 384, 128), f)
    dn[:, :352] = i["L0_ffn_down_proj"]
    we[:, :, 768:1152] = dn.reshape(8, 3, 128, 128).transpose(2, 0, 1, 3).reshape(128, 8, 384)
    win = i["L1_attn_W_in"]
    wdt = np.zeros((128, 8, 8, 16), f)
    for b in range(8):
        wdt[:, b, b, :] = win[384:400].T
    wf = np.zeros((128, 8, WF), f)
    wf[:, :, 0:512] = i["L1_ffn_W1"].transpose(1, 0, 2)
    wf[:, :, 512:1024] = i["L1_ffn_W2"].reshape(8, 4, 128, 128).transpose(2, 0, 1, 3).reshape(128, 8, 512)
    wf[:, :, 1024:1028] = i["L1_ffn_b1"].reshape(8, 4, 128).transpose(2, 0, 1)
    wf[:, :, 1028] = i["L1_ffn_b2"].T
    wg = i["L1_xattn_Wg"]
    wx = np.stack([i["L1_xattn_" + n].T for n in ("Wq_c", "Wk_s", "Wv_s", "Wq_s", "Wk_c", "Wv_c")]
                  + [wg[:, :128].T, wg[:, 128:].T], 1)
    return {
        "par": par, "kon": constants(),
        "x": x.transpose(1, 0, 2), "xT": x.transpose(2, 0, 1).reshape(128, 4096),
        "cT": ctx.transpose(2, 0, 1).reshape(128, 4096),
        "wqr": i["L0_attn_Wq"], "wk": pad_heads(i["L0_attn_Wk"], 4).reshape(128, 2, 128),
        "wv": pad_heads(i["L0_attn_Wv"], 1),
        "wo": wo.reshape(2, 128, 128).transpose(1, 0, 2),
        "wqT": i["L0_xattn_w_q"].T.reshape(16, 64, 128).transpose(1, 0, 2),
        "wkT": wkv[:, :1024].T.reshape(16, 64, 128).transpose(1, 0, 2),
        "wvb": wkv[:, 1024:], "wob": i["L0_xattn_w_out"].reshape(8, 128, 128).transpose(1, 0, 2),
        "bo": np.broadcast_to(i["L0_xattn_b_out"], (128, 128)),
        "we": we.reshape(128, 8 * WE),
        "win": win[0:384].reshape(3, 128, 128).transpose(2, 0, 1), "wdt": wdt.reshape(128, 1024),
        "wod": i["L1_attn_W_out"].T, "wx": wx, "wf": wf.reshape(128, 8 * WF),
    }


def kernel(**inputs):
    import concourse.bacc as bacc
    from concourse.bass_utils import run_bass_kernel_spmd

    arrays = {n: np.ascontiguousarray(v) for n, v in layouts({k: np.asarray(v) for k, v in inputs.items()}).items()}
    nc = bacc.Bacc("TRN2", target_bir_lowering=False, num_devices=1)
    aps = {n: nc.dram_tensor(n, v.shape, mybir.dt.from_np(v.dtype), kind="ExternalInput").ap()
           for n, v in arrays.items()}
    out = nc.dram_tensor("out", (NB, 128, 128), F32, kind="ExternalOutput").ap()
    build(nc, aps, out)
    r = run_bass_kernel_spmd(nc, [arrays], core_ids=[0])
    return r.results[0]["out"]
```

```python
from contextlib import ExitStack

import numpy as np
import concourse.bass as bass
from concourse import mybir

F32 = mybir.dt.float32
F32R = mybir.dt.float32r
BF16 = mybir.dt.bfloat16
I32 = mybir.dt.int32
U32 = mybir.dt.uint32
ALU = mybir.AluOpType
ACT = mybir.ActivationFunctionType
AX = mybir.AxisListType

NB = 32
HB = 16
NT = 39
EPS = 1e-5
NEG = -1e38
WE = 1152
WF = 1030

S_SCALE, S_GAMMA, S_BETA, S_GATE, S_DTB, S_AP = 0, 1, 2, 3, 4, 5
S_CW, S_CB = 6, 18
S_BQC, S_BKS, S_BVS, S_BQS, S_BKC, S_BVC, S_BG = 21, 22, 23, 24, 25, 26, 27
S_BR = 28
S_WR0, S_WR1 = 36, 44
S_N = 52

C_E, C_DD, C_MQ, C_MK, C_N0 = 0, 256, 512, 513, 514
C_ID, C_MASK, C_N1 = 514, 642, 770
C_TRI, C_ONE, C_MASKS = 770, 898, 1026
C_SEL = 1154
C_HM = C_SEL + 1024
C_I16 = C_HM + 16
C_E8 = C_I16 + 16
C_RST = C_E8 + 8
C_J = C_RST + 128
C_N = C_J + 40


def constants():
    c = np.zeros((128, C_N), np.float32)
    p = np.arange(128)
    c[:, C_ID:C_ID + 128] = np.eye(128)
    c[:, C_MASK:C_MASK + 128] = np.where(p[None, :] > p[:, None], NEG, 0.0)
    c[:, C_TRI:C_TRI + 128] = (p[:, None] < p[None, :])
    c[:, C_ONE:C_ONE + 128] = 1.0
    c[:, C_MASKS:C_MASKS + 128] = np.where(p[None, :] < p[:, None], NEG, 0.0)
    signs = np.array([[a, b, d] for a in (-1, 1) for b in (-1, 1) for d in (-1, 1)], np.float32)
    dirs = signs / np.linalg.norm(signs, axis=1, keepdims=True)
    for h in range(8):
        col = 128 * (h // 4) + 32 * (h % 4)
        for i in range(3):
            for r in range(4):
                c[3 * h + i, C_E + col + 3 * r + i] = 1.0
                for j in range(3):
                    c[3 * h + j, C_DD + col + 3 * r + i] = dirs[h, i] * dirs[h, j]
    for b in range(8):
        for h in range(16):
            c[16 * b + h, C_SEL + 128 * b + 8 * h:C_SEL + 128 * b + 8 * h + 8] = 1.0
    c[p, C_HM + p // 8] = 1.0
    c[p[:16], C_I16 + p[:16]] = 1.0
    c[:, C_E8:C_E8 + 8] = 8.0 - np.arange(8)
    c[:, C_RST:C_RST + 128] = (p % 16 != 0)
    c[:, C_J:C_J + 40] = np.arange(40)
    c[:, C_MQ] = np.where((p % 32) // 6 == 1, -1.0, 0.0)
    c[:, C_MK] = np.where((p % 32) // 3 % 2 == 1, -1.0, 0.0)
    return c


class Prog:

    def __init__(self, nc, ctx):
        self.nc, self.ctx = nc, ctx
        self.q = {n: [] for n in ("pe", "dve", "act", "pool", "sp")}
        self.sems, self.count, self.seen = {}, {}, {}

    def add(self, eng, fn, wait, inc, step=1):
        waits = []
        for t in wait:
            if t is not None and self.seen.get((eng, t[0]), 0) < t[1]:
                self.seen[(eng, t[0])] = t[1]
                waits.append(t)
        if inc is not None:
            inc = (inc.split(".")[0] if step == 1 else inc) + "." + eng
        if inc is not None and inc not in self.sems:
            self.sems[inc] = self.ctx.enter_context(self.nc.semaphore(inc.replace(".", "_")))
            self.count[inc] = 0
        self.q[eng].append((waits, fn, inc, step))
        if inc is None:
            return None
        self.count[inc] += step
        return (inc, self.count[inc])

    def play(self, eng, e):
        for waits, fn, inc, step in self.q[eng]:
            for n, v in waits:
                e.wait_ge(self.sems[n], v)
            ins = fn(e)
            if inc is not None:
                ins.then_inc(self.sems[inc], step)


def build(nc, a, out):
    with ExitStack() as ctx:
        P = Prog(nc, ctx)

        def mm(o, lhsT, rhs, start=True, stop=True, wait=(), inc=None):
            return P.add("pe", lambda e: e.matmul(o, lhsT, rhs, start=start, stop=stop,
                                                  skip_group_check=True), wait, inc)

        def tp(o, i, wait=(), inc=None):
            return P.add("pe", lambda e: e.transpose(o, i, ident), wait, inc)

        def tt(o, x, y, op, wait=(), inc=None, eng="dve"):
            return P.add(eng, lambda e: e.tensor_tensor(o, x, y, op), wait, inc)

        def ts(o, x, s1, s2, op0, op1=None, wait=(), inc=None, eng="dve"):
            if op1 is None:
                return P.add(eng, lambda e: e.tensor_scalar(o, x, s1, None, op0), wait, inc)
            return P.add(eng, lambda e: e.tensor_scalar(o, x, s1, s2, op0, op1), wait, inc)

        def stt(o, x, s, y, op0, op1, wait=(), inc=None):
            return P.add("dve", lambda e: e.scalar_tensor_tensor(out=o, in0=x, scalar=s, in1=y, op0=op0, op1=op1),
                         wait, inc)

        def red(o, x, op, wait=(), inc=None, neg=False):
            return P.add("dve", lambda e: e.tensor_reduce(o, x, AX.X, op, negate=neg), wait, inc)

        def scan(o, x, y, wait=(), inc=None):
            return P.add("dve", lambda e: e.tensor_tensor_scan(o, x, y, 0.0, ALU.mult, ALU.add), wait, inc)

        def cp(o, x, wait=(), inc=None, eng="dve"):
            if eng == "act":
                return P.add("act", lambda e: e.activation(o, x, ACT.Copy), wait, inc)
            return P.add(eng, lambda e: e.tensor_copy(o, x), wait, inc)

        def rcp(o, x, wait=(), inc=None):
            return P.add("dve", lambda e: e.reciprocal(o, x), wait, inc)

        def act(o, x, f, wait=(), inc=None, bias=0.0, scale=1.0, accum=None):
            if accum is None:
                return P.add("act", lambda e: e.activation(o, x, f, bias=bias, scale=scale), wait, inc)
            return P.add("act", lambda e: e.activation(o, x, f, bias=bias, scale=scale, accum_out=accum), wait, inc)

        def fill(o, v, wait=(), inc=None, eng="dve"):
            return P.add(eng, lambda e: e.memset(o, v), wait, inc)

        def dma(o, x, wait=(), inc=None, eng="sp"):
            return P.add(eng, lambda e: e.dma_start(o, x), wait, inc, 16)

        top = [nc.sbuf_base + (-nc.sbuf_base) % 64]

        def at(name, cols, dt=F32, off=None):
            size = cols * (2 if dt == BF16 else 4)
            size += -size % 64
            if off is None:
                off = top[0]
                top[0] += size
            return nc.alloc_sbuf_tensor_at(name, [128, cols], dt, offset=off)

        def region(cols):
            r = top[0]
            top[0] += cols * 4
            return r

        X = at("X", NB * 128)[:, :].rearrange("p (b c) -> p b c", b=NB)
        r0 = top[0]
        XT = at("XT", NB * 128)[:, :]
        CT = at("CT", NB * 128)[:, :]
        KON = at("KON", C_N)[:, :]
        PAR = at("PAR", S_N + 64)[:, :]
        ident = KON[:, C_ID:C_ID + 128]
        identb = at("identb", 128, BF16)[:, :]
        maskb = at("maskb", 512, BF16)[:, :]
        masksb = at("masksb", 512, BF16)[:, :]
        trib = at("trib", 128, BF16)[:, :]
        oneb = at("oneb", 128, BF16)[:, :]
        r1 = region(8 * WE)
        KB = [at(f"KB{i}", 4096, F32R, off=r1 + 16384 * i)[:, :].rearrange("p (t b j s) -> p t b j s", t=2, b=4, j=4)
              for i in range(2)]
        WVH = at("WVH", 1024, F32R, off=r1)[:, :]
        XR = [at(f"XR{i}", 512, F32R, off=r1 + 4096 + 2048 * i)[:, :].rearrange("p (k n) -> p k n", k=2) for i in range(2)]
        CR = [at(f"CR{i}", 512, F32R, off=r1 + 8192 + 2048 * i)[:, :].rearrange("p (k n) -> p k n", k=2) for i in range(2)]
        WCt = at("WCt", 8 * WE, off=r1)[:, :]
        r2 = region(12288)
        QB = [at(f"QB{i}", 4096, off=r2 + 16384 * i)[:, :].rearrange("p (h t) -> p h t", h=16) for i in range(2)]
        VB = [at(f"VB{i}", 2048, off=r2 + 32768 + 8192 * i)[:, :].rearrange("p (b d) -> p b d", b=2) for i in range(2)]
        HI = [at(f"HI{i}", 512, F32R, off=r2 + 40960 + 2048 * i)[:, :] for i in range(2)]
        KS = [at(f"KS{i}", 512, F32R, off=r2 + 45056 + 2048 * i)[:, :] for i in range(2)]
        WFt = at("WFt", 8 * WF, off=r2)[:, :]
        r3 = region(2048 + 1024 + 1024)
        AL = at("AL", 2048, F32R, off=r3)[:, :].rearrange("p (h c) -> p h c", h=16)
        WVB = at("WVB", 1024, off=r3 + 8192)[:, :]
        WVL = at("WVL", 1024, F32R, off=r3 + 8192)[:, :]
        WOB = at("WOB", 1024, off=r3 + 12288)[:, :].rearrange("p (k c) -> p k c", k=8)
        r4 = region(256 * 3 + 256 + 2 * 1024 + 4 * 256)
        WQA = at("WQA", 256, off=r4)[:, :].rearrange("p (t c) -> p t c", t=2)
        WKA = at("WKA", 256, off=r4 + 1024)[:, :].rearrange("p (t c) -> p t c", t=2)
        WVA = at("WVA", 256, off=r4 + 2048)[:, :]
        AHI = at("AHI", 2048, F32R, off=r4 + 8192)[:, :].rearrange("p (h c) -> p h c", h=16)
        WOA = at("WOA", 256, off=r4 + 3072)[:, :].rearrange("p (t c) -> p t c", t=2)
        QA = [at(f"QA{i}", 1024, F32R, off=r2 + 16384 + 4096 * i)[:, :].rearrange("p (t n) -> p t n", t=2) for i in range(2)]
        VA = [at(f"VA{i}", 256, off=r2 + 24576 + 1024 * i)[:, :] for i in range(4)]
        PP = [at(f"PP{i}", 512)[:, :].rearrange("p (j s) -> p j s", j=4) for i in range(4)]
        PP += [at(f"PP{i}", 512, off=r2 + 28672 + 2048 * (i - 4))[:, :].rearrange("p (j s) -> p j s", j=4) for i in (4, 5)]
        depth = {"A": 6, "B": 4, "E": 4}
        o_pt = top[0]
        PT = [at(f"PT{i}", 512)[:, :].rearrange("p (j s) -> p j s", j=4) for i in range(3)]
        o_ot = top[0]
        OT = [at(f"OT{i}", 1024)[:, :] for i in range(2)]
        SM = at("SM", 24)[:, :].rearrange("p (k j) -> p k j", k=6)
        MX = at("MX", 24)[:, :].rearrange("p (k j) -> p k j", k=6)
        RS = at("RS", 24)[:, :].rearrange("p (k j) -> p k j", k=6)
        ST = [at(f"ST{i}", 8)[:, :] for i in range(12)]
        MV = [at(f"MV{i}", 4)[:, :] for i in range(12)]
        XH = [at(f"XH{i}", 128)[:, :] for i in range(4)]
        SW = at("SW", 16)[:, :]
        o_bt = top[0]
        BT = at("BT", 128)[:, :]
        BTZ = at("BTZ", 128)[:, :]
        RTE = at("RTE", 360)[:, :]

        PS = [ctx.enter_context(nc.psum_tensor(f"bank{i}", [128, 512], F32)) for i in range(8)]
        bank = [t[:, :] for t in PS]

        rel = {}

        def last(key):
            return rel.get(key, [])

        WQR = at("WQR", 128, off=r3 + 12288)[:, :]
        t_kon0 = dma(KON[0:128, 0:C_N0], a["kon"][:, 0:C_N0], inc="ld.kon0", eng="act")
        t_par = dma(PAR[:, 0:S_N], a["par"], inc="ld.par")
        t_wqr = dma(WQR[0:24, :], a["wqr"], inc="ld.wqr")
        t_wk = dma(WKA, a["wk"], inc="ld.wk")
        t_kon1 = dma(KON[:, C_N0:C_N1], a["kon"][:, C_N0:C_N1], inc="ld.kon1", eng="act")
        t_wv = dma(WVA, a["wv"], inc="ld.wv", eng="act")
        t_xt, t_x = [], []
        for c in range(8):
            t_xt.append(dma(XT[:, 512 * c:512 * c + 512], a["xT"][:, 512 * c:512 * c + 512], inc=f"ld.xt{c}"))
            if c == 0:
                t_wo = dma(WOA, a["wo"], inc="ld.wo")
                t_bo = dma(BT, a["bo"], inc="ld.bo")
            t_x.append(dma(X[:, 4 * c:4 * c + 4, :], a["x"][:, 4 * c:4 * c + 4, :], inc=f"ld.x{c}"))
        WQT = at("WQT", 2048, off=r2)[0:64, :].rearrange("p (k c) -> p k c", k=16)
        WKT = at("WKT", 2048, off=r2 + 8192)[0:64, :].rearrange("p (k c) -> p k c", k=16)

        t_kb = [fill(KB[0].bitcast(F32), 0.0, inc="k.kb", eng="dve"), fill(KB[1].bitcast(F32), 0.0, inc="k.kb", eng="pool")]
        MF = at("MF", 256, off=r3 + 8192 + 1024)[:, :]
        t_mf = stt(MF[0:24, :], KON[0:24, C_E:C_E + 256], PAR[0:24, S_SCALE:S_SCALE + 1],
                   KON[0:24, C_DD:C_DD + 256], ALU.mult, ALU.add, wait=[t_par, t_kon0], inc="A.mf")
        t = mm(bank[7][:, 0:256], WQR[0:24, :], MF[0:24, :], wait=[t_mf, t_wqr], inc="A.wq")
        t_wq = cp(WQA, bank[7][:, 0:256].rearrange("p (t c) -> p t c", t=2), wait=[t], inc="A.wqc")
        rel["Y"] = [t_wq]
        t_mfr = t
        cp(identb, ident, wait=[t_kon1], inc="k.bf")
        for j in range(4):
            t_bf = cp(maskb[:, 128 * j:128 * j + 128], KON[:, C_MASK:C_MASK + 128], inc="k.bf")
        t_sw = fill(SW[:, 0:1], -0.5, inc="k.sw", eng="pool")

        nln = [0]

        def ln_stats(z, wait):
            k = nln[0] % 12
            nln[0] += 1
            t = P.add("dve", lambda e: e.bn_stats(ST[k][:, 0:6], z), list(wait) + last(("ln", k)), "ln.st")
            t = P.add("dve", lambda e: e.bn_aggr(MV[k][:, 0:2], ST[k][:, 0:6]), [t], "ln.ag")
            t = ts(MV[k][:, 2:3], MV[k][:, 1:2], EPS, None, ALU.add, wait=[t], inc="ln.ep")
            t = tt(MV[k][:, 3:4], MV[k][:, 2:3], SW[:, 0:1], ALU.pow, wait=[t, t_sw], inc="ln.pw", eng="pool")
            return k, t

        def ln_apply(o, z, st, wait, inc):
            k, t = st
            t = ts(o, z, MV[k][:, 0:1], MV[k][:, 3:4], ALU.subtract, ALU.mult, wait=list(wait) + [t], inc=inc)
            rel[("ln", k)] = [t]
            return t

        def sm_max(ph, u, sb, t_s):
            k = u % depth[ph]
            return red(MX[:, k, :], sb, ALU.max, wait=[t_s] + last(("MX", k)), inc=ph + ".max", neg=True)

        def sm_exp(ph, u, sb, t_m):
            k = u % depth[ph]
            for j in range(4):
                t = act(PP[k][:, j, :], sb[:, j, :], ACT.Exp, bias=MX[:, k, j:j + 1],
                        accum=SM[:, k, j:j + 1],
                        wait=([t_m] + last(("PP", k)) + last(("SM", k))) if j == 0 else (),
                        inc=ph + ".exp")
            rel[("MX", k)] = [t]
            return t

        def sm_rec(ph, u, t_e):
            k = u % depth[ph]
            t = rcp(RS[:, k, :], SM[:, k, :], wait=[t_e] + last(("RS", k)), inc=ph + ".rec")
            rel[("SM", k)] = [t]
            return t

        def sm_nrm(ph, u, t_r):
            k = u % depth[ph]
            t = tt(PP[k], PP[k], RS[:, k, :].unsqueeze(2).broadcast_to((128, 4, 128)), ALU.mult,
                   wait=[t_r], inc=ph + ".nrm", eng="pool")
            rel[("RS", k)] = [t]
            return t

        def sm_tp(ph, u, tb, t_n, free):
            k = u % depth[ph]
            for j in range(4):
                t = tp(tb[:, 128 * j:128 * j + 128], PP[k][:, j, :], wait=([t_n] + free) if j == 0 else (),
                       inc=ph + ".tp" if j == 3 else None)
            rel[("PP", k)] = [t]
            return t

        nM, ring = [0], [5, 3]

        def m_bank():
            k = ring[nM[0] % len(ring)]
            nM[0] += 1
            return k

        tA = {}

        def A_q(c, t):
            m = tA["qm", c, t] = m_bank()
            g = mm(bank[m], WQA[:, t, :], XT[:, 512 * c:512 * c + 512], wait=[t_wq, t_xt[c]] + last(("M", m)), inc="A.q")
            tA["qh", c, t] = cp(HI[0], bank[m], wait=[g] + last(("HI", 0)), inc="A.hi", eng="act")

        def A_q2(c, t):
            m = tA["qm", c, t]
            g = stt(QA[c % 2][:, t, :], HI[0].bitcast(F32), KON[:, C_MQ:C_MQ + 1], bank[m], ALU.mult, ALU.add,
                    wait=[tA["qh", c, t]] + last(("QA", c % 2)), inc="A.qc")
            rel[("M", m)] = rel[("HI", 0)] = [g]
            tA["q", c, t] = g

        def A_k(c, t):
            m = tA["km", c, t] = m_bank()
            g = mm(bank[m], WKA[:, t, :], XT[:, 512 * c:512 * c + 512], wait=[t_wk, t_xt[c]] + last(("M", m)), inc="A.k")
            tA["kh", c, t] = cp(HI[1], bank[m], wait=[g] + last(("HI", 1)), inc="A.hi", eng="act")

        def A_k2(c, t):
            m = tA["km", c, t]
            g = stt(KS[t], HI[1].bitcast(F32), KON[:, C_MK:C_MK + 1], bank[m], ALU.mult, ALU.add,
                    wait=[tA["kh", c, t]] + last(("KS", t)), inc="A.kc")
            rel[("M", m)] = rel[("HI", 1)] = [g]
            for j in range(4):
                r = slice(32 * j, 32 * j + 32)
                src = KS[t][r, :].rearrange("p (b s) -> p b s", b=4)
                if c == 0:
                    k = cp(KB[0][r, t, :, j, :], src, wait=[g, t_kb[0]], inc="A.kd")
                else:
                    k = dma(KB[c % 2][r, t, :, j, :].bitcast(F32), src.bitcast(F32),
                            wait=[g, t_kb[c % 2]] + last(("KB", c % 2)), inc=f"A.kd{c % 2}{t}")
            rel[("KS", t)] = [k]
            tA["k", c, t] = k

        def A_v(b):
            m = m_bank()
            v = bank[m][:, 0:256]
            g = mm(v, XT[:, 128 * b:128 * b + 128], WVA, wait=[t_wv, t_xt[b // 4]] + last(("M", m)), inc="A.v")
            rel[("XT", b)] = [g]
            g = cp(VA[b % 4], v, wait=[g] + last(("VA", b % 4)), inc="A.vc", eng="act")
            rel[("M", m)] = [g]
            tA["v", b] = g

        def A_S(u):
            b, t = u // 2, u % 2
            c = b // 4
            sb = bank[u % 2]
            mm(sb, identb, maskb, start=True, stop=False,
               wait=[t_bf, tA["q", c, t], tA["k", c, t]] + last(("S", u % 2)))
            g = mm(sb, QA[c % 2][:, t, 128 * (b % 4):128 * (b % 4) + 128], KB[c % 2][:, t, b % 4, :, :],
                   start=False, stop=True, inc="A.s")
            if u % 8 == 7:
                rel[("QA", c % 2)] = [g]
                rel[("KB", c % 2)] = [g]
            s3 = sb.rearrange("p (j s) -> p j s", j=4)
            g = sm_max("A", u, s3, g)
            g = sm_exp("A", u, s3, g)
            rel[("S", u % 2)] = [g]
            tA["e", u] = g

        def A_norm(u):
            tA["n", u] = sm_nrm("A", u, sm_rec("A", u, tA["e", u]))

        def A_T(u):
            tb = bank[(2, 6)[u % 2]]
            g = sm_tp("A", u, tb, tA["n", u], last(("T", u % 2)))
            g = cp(PT[u % 3], tb.rearrange("p (j s) -> p j s", j=4), wait=[g] + last(("PT", u % 3)), inc="A.pt",
                   eng="act")
            rel[("T", u % 2)] = [g]
            tA["pt", u] = g

        def A_AV(u):
            b, t = u // 2, u % 2
            for j in range(4):
                g = mm(bank[4][32 * j:32 * j + 32, 128 * t:128 * t + 128],
                       VA[b % 4][:, 128 * t + 32 * j:128 * t + 32 * j + 32], PT[u % 3][:, j, :],
                       wait=([tA["pt", u], tA["v", b]] + (last("O") if t == 0 else [])) if j == 0 else (),
                       inc="A.av" if j == 3 else None)
            rel[("PT", u % 3)] = [g]
            if t == 1:
                rel[("VA", b % 4)] = [g]
                g = cp(OT[b % 2][:, 0:256], bank[4][:, 0:256], wait=[g] + last(("OT", b % 2)), inc="A.ot", eng="dve")
                rel["O"] = [g]
                tA["ot", b] = g

        def A_out(b):
            for t in range(2):
                g = mm(bank[7][:, 0:128], OT[b % 2][:, 128 * t:128 * t + 128], WOA[:, t, :], start=(t == 0),
                       stop=(t == 1), wait=([tA["ot", b], t_wo] + last("Y")) if t == 0 else (),
                       inc="A.y" if t else None)
            rel[("OT", b % 2)] = [g]
            g = tt(X[:, b, :], bank[7][:, 0:128], X[:, b, :], ALU.add, wait=[g, t_x[b // 4]], inc="A.z")
            rel["Y"] = [g]
            tA["ln", b] = ln_stats(X[:, b, :], [g])

        def A_ln(b):
            g = ln_apply(X[:, b, :], X[:, b, :], tA["ln", b], [], "A.x1")
            tA["x1", b] = g
            tA["ln2", b] = ln_stats(X[:, b, :], [g])

        def A_ln2(b):
            g = ln_apply(XH[b % 4], X[:, b, :], tA["ln2", b], last(("XH", b % 4)), "A.xh")
            tA["xh", b] = g
            tA["xb", b] = tt(X[:, b, :], X[:, b, :], BT, ALU.add, wait=[g, t_bt], inc="A.xb", eng="pool")

        def A_xn(b):
            m = 7
            g = tp(bank[m][:, 0:128], XH[b % 4], wait=[tA["xh", b]] + last("Y"), inc="A.xt")
            rel[("XH", b % 4)] = [g]
            tA["xt_pe"] = g
            g = ts(XT[:, 128 * b:128 * b + 128], bank[m][:, 0:128], PAR[:, S_GAMMA:S_GAMMA + 1],
                   PAR[:, S_BETA:S_BETA + 1], ALU.mult, ALU.add, wait=[g] + last(("XT", b)), inc="A.xn")
            rel["Y"] = [g]
            tA["xn", b] = g

        for t in range(2):
            A_k(0, t)
            A_q(0, t)
            A_k2(0, t)
            A_q2(0, t)
        t_tg = act(PAR[:, S_N:S_N + 1], PAR[:, S_GATE:S_GATE + 1], ACT.Tanh, wait=[t_par], inc="B.tg")
        t_bt = ts(BT, BT, PAR[:, S_N:S_N + 1], None, ALU.mult, wait=[t_tg, t_bo], inc="B.bt")
        def B_ah(k):
            m = m_bank()
            for j in range(4):
                h = 4 * k + j
                g = mm(bank[m][:, 128 * j:128 * j + 128], WQT[:, h, :], WKT[:, h, :],
                       wait=([t_wqt, t_wkt] + last(("M", m))) if j == 0 else (), inc="B.ah" if j == 3 else None)
            rel["WQT"] = [g]
            x = bank[m].rearrange("p (h c) -> p h c", h=4)
            g = act(AHI[:, 4 * k:4 * k + 4, :], x, ACT.Copy, scale=0.125, wait=[g], inc="B.ahc")
            g = stt(AL[:, 4 * k:4 * k + 4, :], x, 0.125, AHI[:, 4 * k:4 * k + 4, :].bitcast(F32), ALU.mult, ALU.subtract, wait=[g],
                    inc="B.ahc")
            rel[("M", m)] = [g]
            tA["ah", k] = g

        tB = {}

        def parts(o, x, wait):
            g = cp(o[0], x, wait=wait, inc="B.hi", eng="act")
            return tt(o[1], x, o[0].bitcast(F32), ALU.subtract, wait=[g], inc="B.lo", eng="pool")

        def mm3(o, lhsT, rhs, wait, inc):
            mm(o, lhsT[0], rhs[0], start=True, stop=False, wait=wait)
            mm(o, lhsT[0], rhs[1], start=False, stop=False)
            return mm(o, lhsT[1], rhs[0], start=False, stop=True, inc=inc)

        def B_parts(c):
            k, n = c % 2, slice(256 * c, 256 * c + 256)
            tB["xr", c] = parts((XR[k][:, 0, :], XR[k][:, 1, :]), XT[:, n],
                                [tA["xn", 2 * c], tA["xn", 2 * c + 1]] + last(("XR", k)))
            tB["cr", c] = parts((CR[k][:, 0, :], CR[k][:, 1, :]), CT[:, n], [t_ct] + last(("CR", k)))

        def B_q(c, k):
            m = m_bank()
            for j in range(2):
                h = 2 * k + j
                g = mm3(bank[m][:, 256 * j:256 * j + 256], (AHI[:, h, :], AL[:, h, :]),
                        (XR[c % 2][:, 0, :], XR[c % 2][:, 1, :]),
                        ([tA["ah", h // 4], tB["xr", c]] + last(("M", m))) if j == 0 else (), "B.q" if j else None)
            rel[("XR", c % 2)] = [g]
            g = cp(QB[c % 2][:, 2 * k:2 * k + 2, :], bank[m].rearrange("p (h t) -> p h t", h=2),
                   wait=[g] + last(("QB", c % 2)) + last("WQT"), inc="B.qc", eng="act" if k % 2 else "dve")
            rel[("M", m)] = [g]
            tB["q", c, k] = g

        def B_v(c, k):
            m = m_bank()
            b, n = slice(128 * (k // 2), 128 * (k // 2) + 128), slice(512 * (k % 2), 512 * (k % 2) + 512)
            g = mm3(bank[m], (CR[c % 2][:, 0, b], CR[c % 2][:, 1, b]), (WVH[:, n], WVL[:, n]),
                    [tB["cr", c], tB["wv"]] + last(("M", m)), "B.v")
            rel[("CR", c % 2)] = [g]
            g = cp(VB[c % 2][:, k // 2, n], bank[m],
                   wait=[g] + last(("VB", c % 2)), inc="B.vc", eng="act" if k % 2 else "dve")
            rel[("M", m)] = [g]
            tB["v", c, k] = g

        def jobs(c):
            q = [lambda k=k: B_q(c, k) for k in range(8)]
            v = [lambda k=k: B_v(c, k) for k in range(4)]
            return q[0:2] + v[0:1] + q[2:4] + v[1:2] + q[4:6] + v[2:3] + q[6:8] + v[3:4]

        NU = 2 * NB
        sched = {}
        for c in range(1, 8):
            for n, (fn, t) in enumerate(((A_k, 0), (A_q, 0), (A_k, 1), (A_q, 1))):
                sched[max(8 * c - 9 + 2 * n, n)] = (fn, c, t)
        def A_tail(i):
            for fn, lag in ((A_xn, 13), (A_ln2, 11), (A_ln, 9), (A_out, 8)):
                j = i - lag
                if j >= 0 and j % 2 == 0 and j // 2 < NB:
                    fn(j // 2)

        NA = NU + 6
        for i in range(NA):
            if i < NU:
                A_S(i)
            if i < NU:
                if i % 2 == 0:
                    A_v(i // 2)
            if i == 9:
                t_wqt = dma(WQT, a["wqT"], inc="ld.wqt")
                t_wkt = dma(WKT, a["wkT"], inc="ld.wkt")
                t_ct = dma(CT, a["cT"], inc="ld.ct")
                t_kon = dma(KON[:, C_N1:C_N], a["kon"][:, C_N1:C_N], inc="ld.kon")
                t_wvb = dma(WVB, a["wvb"], wait=[t_mfr], inc="ld.wvb")
                t_wob = dma(WOB, a["wob"], wait=[t_mfr], inc="ld.wob")
            if i == 50:
                t_wob = ts(WOB, WOB, PAR[:, S_N:S_N + 1], None, ALU.mult, wait=[t_tg, t_wob], inc="B.wob", eng="pool")
            if 4 <= i < NU + 4:
                A_T(i - 4)
            if 6 <= i < NU + 6:
                A_AV(i - 6)
            A_tail(i)
            if i - 1 in sched:
                fn, c, t = sched[i - 1]
                (A_k2 if fn is A_k else A_q2)(c, t)
            if i in (27, 31, 35, 39):
                B_ah((27, 31, 35, 39).index(i))
            if i in sched:
                fn, c, t = sched[i]
                fn(c, t)
            if 1 <= i <= NU:
                A_norm(i - 1)
            if i == NU - 7:
                for k in (0, 1):
                    rel[("XR", k)] = rel[("CR", k)] = last(("KB", 0))
                B_parts(0)
                tB["wv"] = parts((WVH, WVL), WVB, [t_wvb] + last(("KB", 0)))
                B_parts(1)
                first_jobs = jobs(0)
            elif i > NU - 7:
                first_jobs.pop(0)()

        a_pe = last(("VA", (NB - 1) % 4)) + last(("KB", 1))
        rel[("QB", 1)] = a_pe + last(("VA", 2))
        rel[("VB", 1)] = last(("HI", 0)) + last(("HI", 1)) + last(("KS", 0)) + last(("KS", 1))
        rel[("M", 6)] = last(("T", 1))
        rel[("T", 1)] = last(("M", 3))
        ring[:] = [5, 6]
        for j in range(4):
            cp(masksb[:, 128 * j:128 * j + 128], KON[:, C_MASKS:C_MASKS + 128], wait=[t_kon], eng="act")
        cp(trib, KON[:, C_TRI:C_TRI + 128], eng="act")
        t_bf2 = cp(oneb, KON[:, C_ONE:C_ONE + 128], inc="k.bf", eng="act")

        def B_S(u):
            c, bb, hq = u // 8, (u // 4) % 2, u % 4
            b = 2 * c + bb
            sb = bank[u % 2]
            for j in range(4):
                h = 4 * hq + j
                g = mm(sb[:, 128 * j:128 * j + 128], QB[c % 2][:, h, 128 * bb:128 * bb + 128],
                       CT[:, 128 * b:128 * b + 128],
                       wait=([t_ct, tB["q", c, 2 * hq], tB["q", c, 2 * hq + 1]] + last(("S", u % 2)))
                       if j == 0 else (), inc="B.s" if j == 3 else None)
            if u % 8 == 7:
                rel[("QB", c % 2)] = [g]
            s3 = sb.rearrange("p (j s) -> p j s", j=4)
            g = sm_max("B", u, s3, g)
            g = sm_exp("B", u, s3, g)
            rel[("S", u % 2)] = [g]
            tB["e", u] = g

        def B_norm(u):
            tB["n", u] = sm_nrm("B", u, sm_rec("B", u, tB["e", u]))

        def B_T(u):
            tb = bank[2 + u % 2]
            g = sm_tp("B", u, tb, tB["n", u], last(("T", u % 2)))
            g = cp(PT[u % 3], tb.rearrange("p (j s) -> p j s", j=4), wait=[g] + last(("PT", u % 3)), inc="B.pt",
                   eng="dve")
            rel[("T", u % 2)] = [g]
            tB["pt", u] = g

        def B_AV(u):
            c, bb, hq = u // 8, (u // 4) % 2, u % 4
            b = 2 * c + bb
            for j in range(4):
                h = 4 * hq + j
                g = mm(bank[4][64 * (j % 2):64 * (j % 2) + 64, 128 * (j // 2):128 * (j // 2) + 128],
                       VB[c % 2][:, bb, 64 * h:64 * h + 64], PT[u % 3][:, j, :],
                       wait=([tB["pt", u], tB["v", c, 2 * bb + hq // 2]] + last("O")) if j == 0 else (),
                       inc="B.av" if j == 3 else None)
            rel[("PT", u % 3)] = [g]
            tB["av_pe"] = g
            if u % 8 == 7:
                rel[("VB", c % 2)] = [g]
            g = cp(OT[b % 2][:, 256 * hq:256 * hq + 256], bank[4][:, 0:256],
                   wait=[g] + (last(("OT", b % 2)) if hq == 0 else []), inc="B.ot", eng="dve")
            rel["O"] = [g]
            tB["ot", b] = g

        def B_out(b):
            for k in range(8):
                g = mm(bank[7][:, 0:128], OT[b % 2][:, 128 * k:128 * k + 128], WOB[:, k, :], start=(k == 0),
                       stop=(k == 7), wait=([tB["ot", b], t_wob] + last("Y")) if k == 0 else (),
                       inc="B.y" if k == 7 else None)
            rel[("OT", b % 2)] = [g]
            tB["y_pe"] = g
            g = tt(X[:, b, :], bank[7][:, 0:128], X[:, b, :], ALU.add, wait=[g, tA["xb", b]], inc="B.z")
            rel["Y"] = [g]
            tB["ln", b] = ln_stats(X[:, b, :], [g])

        def B_ln(b):
            tB["x2", b] = ln_apply(X[:, b, :], X[:, b, :], tB["ln", b], [], "B.x2")

        def B_tp(b):
            m = m_bank()
            g = tp(bank[m][:, 0:128], X[:, b, :], wait=[tB["x2", b]] + last(("M", m)), inc="B.xt")
            g = cp(XH[b % 4], bank[m][:, 0:128], wait=[g] + last(("XH", b % 4)), inc="B.xtc", eng="act")
            rel[("M", m)] = [g]
            tB["xt", b] = g

        SC = at("SC", 256)[:, :].rearrange("p (b e) -> p b e", e=8)

        def B_route(b):
            m = m_bank()
            g = mm(bank[m][:, 0:8], XH[b % 4], PAR[:, S_WR0:S_WR0 + 8], wait=[tB["xt", b]] + last(("M", m)),
                   inc="B.r")
            rel[("XH", b % 4)] = [g]
            g = cp(SC[:, b, :], bank[m][:, 0:8], wait=[g], inc="B.rc")
            rel[("M", m)] = [g]
            tB["r", b] = g

        RW = [at(f"RW{k}", 128, off=r4 + 512 * k)[:, :] for k in range(10)]
        POS = [at(f"POS{h}", 32, I32, off=r4 + 5120 + 128 * h)[:, :].rearrange("p (k b) -> p k b", k=2)
               for h in range(2)]
        WR = [at(f"WR{h}", 32, off=r4 + 5376 + 128 * h)[:, :].rearrange("p (k b) -> p k b", k=2) for h in range(2)]
        TE = [at(f"TE{h}", 40, I32, off=r4 + 5632 + 192 * h)[:, :] for h in range(2)]
        RV = at("RV", 16 * 12, off=r4 + 6016)[:, :].rearrange("p (k b) -> p k b", k=12)
        MB = at("MB", 128, BF16, off=r4 + 6784)[:, :]
        GA = [at(f"GA{k}", 256, off=r4 + 7168 + 1024 * k)[:, :].rearrange("p (k c) -> p k c", k=2) for k in range(4)]
        XS = [at(f"XS{k}", 128, off=r4 + 11264 + 512 * k)[:, :] for k in range(4)]
        YS = [at(f"YS{k}", 128, off=r4 + 13312 + 512 * k)[:, :] for k in range(4)]
        XST = [at(f"XST{k}", 128, off=r4 + 15360 + 512 * k)[:, :] for k in range(2)]
        NTI = at("NTI", 8, I32)[:, :]
        xs = [nc.dram_tensor(f"xs{h}", [NT * 128, 128], F32, kind="Internal").ap() for h in range(2)]
        ys = [nc.dram_tensor(f"ys{h}", [NT * 128, 128], F32, kind="Internal").ap() for h in range(2)]
        t_z = fill(BTZ, 0.0, inc="k.z", eng="pool")
        t_xz = [dma(xs[h].rearrange("(t p) c -> p t c", p=128), BTZ.unsqueeze(1).broadcast_to((128, NT, 128)),
                    wait=[t_z], inc=f"C.xz{h}", eng="act") for h in range(2)]
        tC = {}

        def route(h):
            s = SC[:, HB * h:HB * h + HB, :]

            def v3(x):
                return x.rearrange("p (b e) -> p b e", e=8)

            def wide(x):
                return x.unsqueeze(2).broadcast_to((128, HB, 8))

            e8 = KON[:, C_E8:C_E8 + 8].unsqueeze(1).broadcast_to((128, HB, 8))
            p, oh1, oh2, t1, t2 = (v3(RW[k]) for k in range(5))
            m1, mp, m2, mv, mv2, den = (RV[:, k, :] for k in range(6))
            n = "R"
            g = red(m1, s, ALU.max, wait=[tB["r", HB * h + HB - 1], tA["xn", NB - 1]] + last("route"), inc=n)
            yield
            g = tt(t1, s, wide(m1), ALU.subtract, wait=[g], inc=n)
            yield
            g = act(p, t1, ACT.Exp, wait=[g], inc=n)
            yield
            g = red(mp, p, ALU.max, wait=[g], inc=n)
            yield
            for oh, m, v in ((oh1, mp, mv), (oh2, m2, mv2)):
                src = p if oh is oh1 else t1
                if oh is oh2:
                    g = stt(RW[3], RW[1], -2.0, RW[0], ALU.mult, ALU.add, wait=[g], inc=n)
                    yield
                    g = red(m, t1, ALU.max, wait=[g], inc=n)
                    yield
                g = tt(t2, src, wide(m), ALU.is_equal, wait=[g], inc=n)
                yield
                g = tt(t2, t2, e8, ALU.mult, wait=[g], inc=n)
                yield
                g = red(v, t2, ALU.max, wait=[g], inc=n)
                yield
                g = tt(oh, t2, wide(v), ALU.is_equal, wait=[g], inc=n)
                yield
            g = tt(MB, RW[1], RW[2], ALU.add, wait=[g], inc=n)
            m = m_bank()
            mm(bank[m][:, 0:128], trib, MB, wait=[g, t_bf2] + last(("M", m)))
            k = mm(bank[m][:, 128:256], oneb, MB, inc="R.mm")
            excl, cnt, incl, off = RW[5], RW[6], RW[7], RW[8]

            def eb(x):
                return x.rearrange("p (e b) -> p e b", b=HB)

            g = cp(excl, bank[m][:, 0:128], wait=[g, k], inc=n)
            g = cp(eb(cnt), bank[m][:, 128:256].rearrange("p (b e) -> p e b", e=8), wait=[g], inc=n)
            rel[("M", m)] = [g]
            yield
            g = tt(den, mp, m2, ALU.add, wait=[g], inc=n)
            g = rcp(RV[:, 6, :], den, wait=[g], inc=n)
            yield
            g = tt(WR[h][:, 0, :], mp, RV[:, 6, :], ALU.mult, wait=[g], inc=n)
            g = tt(WR[h][:, 1, :], m2, RV[:, 6, :], ALU.mult, wait=[g], inc=n)
            yield
            g = scan(incl, KON[:, C_RST:C_RST + 128], cnt, wait=[g], inc=n)
            yield
            g = tt(off, incl, cnt, ALU.subtract, wait=[g], inc=n)
            yield
            nt, tend, tst = (RV[:, k, 0:8] for k in (7, 8, 9))
            g = ts(NTI, eb(incl)[:, :, HB - 1], 127.0, None, ALU.add, wait=[g], inc=n)
            yield
            g = ts(NTI, NTI, 7, None, ALU.logical_shift_right, wait=[g], inc=n)
            g = cp(nt, NTI, wait=[g], inc=n)
            yield
            g = scan(tend, KON[:, C_ONE:C_ONE + 8], nt, wait=[g], inc=n)
            g = tt(tst, tend, nt, ALU.subtract, wait=[g], inc=n)
            yield
            g = ts(tst, tst, 128.0, None, ALU.mult, wait=[g], inc=n)
            g = tt(eb(off), eb(off), tst.unsqueeze(2).broadcast_to((128, 8, HB)), ALU.add, wait=[g], inc=n)
            yield
            g = tt(v3(excl), v3(excl), off.rearrange("p (e b) -> p b e", b=HB), ALU.add, wait=[g], inc=n)
            yield
            for k, oh in enumerate((oh1, oh2)):
                g = tt(t1, oh, v3(excl), ALU.mult, wait=[g], inc=n)
                yield
                g = red(RV[:, 10, :], t1, ALU.add, wait=[g], inc=n)
                g = cp(POS[h][:, k, :], RV[:, 10, :], wait=[g], inc=n)
                yield
            tC["pos", h] = g
            te = RTE[0:1, 0:NT * 8].rearrange("p (j e) -> p j e", e=8)
            g = tt(te, KON[0:1, C_J:C_J + NT].unsqueeze(2).broadcast_to((1, NT, 8)),
                   tend[0:1, :].unsqueeze(1).broadcast_to((1, NT, 8)), ALU.is_ge, wait=[g], inc=n)
            yield
            g = red(RTE[0:1, 320:320 + NT], te, ALU.add, wait=[g], inc=n)
            yield
            g = ts(TE[h][0:1, 0:NT], RTE[0:1, 320:320 + NT], 7.0, None, ALU.min, wait=[g], inc=n)
            tC["te", h] = g
            rel["route"] = [g]
            yield

        def scatter(h):
            for b in range(HB * h, HB * h + HB):
                for k in range(2):
                    idx = POS[h][:, k, b - HB * h:b - HB * h + 1]
                    tC["sc", h] = P.add("pool", lambda e, idx=idx, b=b: e.indirect_dma_start(
                        xs[h], bass.IndirectOffsetOnAxis(ap=idx, axis=0), X[:, b, :], None),
                        [tC["pos", h], tB["x2", b], t_xz[h]], f"C.sc{h}", 16)
                    yield

        def steps(gens):
            for g in gens:
                yield from g()

        WS = [at(f"WS{k}", WE, off=o_pt if k == 3 else r3 + 4608 * k)[:, :] for k in range(4)]
        HS = [at(f"HS{k}", 384, off=o_ot + 1536 * k)[:, :] for k in range(2)]
        AC = [at(f"AC{k}", 384, off=o_ot + 3072 + 1536 * k)[:, :] for k in range(2)]
        HS0 = [at(f"HSB{k}", 384, off=r0 + 1536 * k)[:, :] for k in range(2)]
        AC0 = [at(f"ACB{k}", 384, off=r0 + 3072 + 1536 * k)[:, :] for k in range(2)]

        def q_end():
            return [r for k in range(2) for n in ("XR", "CR") for r in last((n, k))]

        regs = {}

        def staged(o, w, width, idx, wait, inc):
            def fn(e):
                if "r" not in regs:
                    regs["r"] = e.alloc_register("expert")
                e.reg_load(regs["r"], idx)
                v = e.snap(regs["r"], min_val=0, max_val=7)
                return e.tensor_copy(o, w[:, bass.ds(v * width, width)])
            return P.add("dve", fn, wait, inc)

        def C_load(t):
            h, j, k = t // NT, t % NT, t % 4
            tC["xs", t] = dma(XS[k], xs[h][128 * j:128 * j + 128, :],
                                 wait=[tC["sc", h]] + q_end() + last(("XS", k)), inc=f"C.xs{k}")

        def C_T(t):
            bk = 1 + t % 2
            g = tp(bank[bk][:, 384:512], XS[t % 4], wait=[tC["xs", t]] + last(("GU", bk)), inc="C.t")
            rel[("XS", t % 4)] = [g]
            g = cp(XST[t % 2], bank[bk][:, 384:512], wait=[g] + last(("XST", t % 2)), inc="C.tc", eng="act")
            rel[("GU", bk)] = [g]
            tC["xt", t] = g

        def C_W(t):
            h, j = t // NT, t % NT
            tC["ws", t] = staged(WS[t % 4], WCt, WE, TE[h][0:1, j:j + 1],
                                 [tC["te", h]] + t_wc + last(("WS", t % 4)) + q_end()
                                 + ([tB["ot", NB - 1], tB["y_pe"]] if t >= 2 else []), "C.ws")

        TS = NT + 20

        def C_GU(t):
            hs, ac = (HS0[t % 2], AC0[t % 2]) if t < 4 else (HS[t % 2], AC[t % 2])
            for u in range(2):
                bk = 1 + 2 * u + t % 2
                for f in range(3):
                    g = mm(bank[bk][:, 128 * f:128 * f + 128], WS[t % 4][:, 384 * u + 128 * f:384 * u + 128 * f + 128],
                           XST[t % 2], wait=([tC["xt", t], tC["ws", t]] + last(("GU", bk))) if f == 0 else (),
                           inc="C.gu" if f == 2 else None)
                if u == 0:
                    if t < TS:
                        s = act(hs, bank[bk][:, 0:384], ACT.Silu, wait=[g] + last(("HS", t % 2)), inc="C.si")
                    else:
                        s = act(hs, bank[bk][:, 0:384], ACT.Tanh, scale=0.5, wait=[g] + last(("HS", t % 2)), inc="C.si")
                        s = stt(hs, hs, 1.0, bank[bk][:, 0:384], ALU.add, ALU.mult, wait=[s], inc="C.si")
                    rel[("GU", bk)] = [s]
            rel[("XST", t % 2)] = [g]
            g = tt(ac, hs, bank[3 + t % 2][:, 0:384], ALU.mult, wait=[s, g] + last(("AC", t % 2)),
                   inc="C.ac")
            rel[("GU", 3 + t % 2)] = [g]
            rel[("HS", t % 2)] = [g]
            tC["ac", t] = g

        def C_D(t):
            h, j = t // NT, t % NT
            ac = AC0[t % 2] if t < 4 else AC[t % 2]
            for f in range(3):
                g = mm(bank[7][:, 0:128], ac[:, 128 * f:128 * f + 128],
                       WS[t % 4][:, 768 + 128 * f:768 + 128 * f + 128], start=(f == 0), stop=(f == 2),
                       wait=([tC["ac", t]] + last("CY")) if f == 0 else (), inc="C.d" if f == 2 else None)
            rel[("WS", t % 4)] = [g]
            rel[("AC", t % 2)] = [g]
            tC["d_pe"] = g
            k = t % 4
            g = act(YS[k], bank[7][:, 0:128], ACT.Copy, wait=[g] + last(("YS", k)), inc="C.yc", scale=0.5 if t >= TS else 1.0)
            rel["CY"] = [g]
            tC["y_act"] = g
            g = dma(ys[h][128 * j:128 * j + 128, :], YS[k], wait=[g], inc=f"C.ys{k}", eng="act")
            rel[("YS", k)] = [g]
            tC["ys", h, k] = g

        def experts():
            n = 2 * NT
            for i in range(n + 5):
                if i < n:
                    C_load(i)
                if i >= 5:
                    C_D(i - 5)
                if 1 <= i < n + 1:
                    C_W(i - 1)
                if 3 <= i < n + 3:
                    C_GU(i - 3)
                if 2 <= i < n + 2:
                    C_T(i - 2)
                yield i

        NU = 4 * NB
        todo = []

        t_wc = [dma(WCt[:, 3072:8 * WE], a["we"][:, 3072:8 * WE], wait=a_pe, inc="ld.wc0")]
        ex = experts()
        EB = 8
        bg = steps([lambda: route(0), lambda: scatter(0)])
        for i in range(NU + EB):
            if i < 13:
                A_tail(NA + i)
            if i < NU:
                B_S(i)
            if 1 <= i <= NU:
                B_norm(i - 1)
            if i < NU:
                if i % 8 == 0 and i // 8 + 1 < NB // 2:
                    todo = jobs(i // 8 + 1)
                if i % 8 == 4 and i // 8 + 2 < NB // 2:
                    B_parts(i // 8 + 2)
                if i == NU - 8:
                    t_wc.append(dma(WCt[:, 0:3072], a["we"][:, 0:3072],
                                    wait=[r for k in range(2) for n in ("XR", "CR") for r in last((n, k))], inc="ld.wc1"))
                n = 2 if i % 2 == 0 else 1
                for _ in range(n):
                    if todo:
                        todo.pop(0)()
            if 2 <= i < NU + 2:
                B_T(i - 2)
            if 3 <= i < NU + 3:
                B_AV(i - 3)
            for fn, lag in ((B_route, 11), (B_tp, 10), (B_ln, 8), (B_out, 7)):
                j = i - lag
                if j >= 0 and j % 4 == 0 and j // 4 < NB:
                    fn(j // 4)
            if i > 4 * HB + 8:
                next(bg, None)
                next(bg, None)
            if i == NU + 2:
                rel["DT"] = last(("S", 0))
                for k, key in ((1, ("S", 1)), (2, ("T", 0)), (3, ("T", 1)), (4, "O")):
                    rel[("GU", k)] = last(key)
            if i == NU + 4:
                rel["CY"] = last("Y")
            if NU <= i < NU + EB:
                next(ex)
        for _ in bg:
            pass
        b_end = [tB["r", NB - 1], tB["ot", NB - 1], tB["y_pe"]]

        def gather(b):
            h, k = b // HB, b % 4
            for n in range(2):
                idx = POS[h][:, n, b - HB * h:b - HB * h + 1]
                g = P.add("pool", lambda e, idx=idx, n=n: e.indirect_dma_start(
                    GA[k][:, n, :], None, ys[h], bass.IndirectOffsetOnAxis(ap=idx, axis=0)),
                    [tC["ys", h, q] for q in range(4)] + last(("GA", k)), f"C.ga{k}", 16)
            return g

        def combine(b, g):
            h, k = b // HB, b % 4
            g = stt(X[:, b, :], GA[k][:, 0, :], WR[h][:, 0, b % HB:b % HB + 1], X[:, b, :], ALU.mult, ALU.add,
                    wait=[g], inc="C.z")
            g = stt(X[:, b, :], GA[k][:, 1, :], WR[h][:, 1, b % HB:b % HB + 1], X[:, b, :], ALU.mult, ALU.add,
                    wait=[g], inc="C.z")
            rel[("GA", k)] = [g]
            return ln_stats(X[:, b, :], [g])

        bg = steps([lambda: route(1), lambda: scatter(1)])

        CU = at("CU", 2048, off=r0)[:, :].rearrange("p (h l) -> p h l", h=16)
        XP = at("XP", 3 * 132, off=r0 + 8192)[:, :].rearrange("p (k s) -> p k s", k=3)
        CO = at("CO", 384, off=r0 + 9792)[:, :].rearrange("p (k s) -> p k s", k=3)
        XTK = at("XTK", 128, off=r0 + 11328)[:, :]
        CUT = at("CUT", 16, off=r0 + 11840)[:, :]
        WDT = at("WDT", 1024, off=r0 + 12288)[:, :].rearrange("p (b c) -> p b c", b=8)
        CM = at("CM", 2048, off=r2 + 33024)[:, :].rearrange("p (h l) -> p h l", h=16)
        X3T = [at(f"X3T{k}", 128, off=r2 + 41216 + 512 * k)[:, :] for k in range(4)]
        WIN = at("WIN", 384, off=r2 + 43264)[:, :].rearrange("p (k c) -> p k c", k=3)
        WOD = at("WOD", 128, off=r2 + 44800)[:, :]
        EL = PP[0:3]
        Y0 = at("Y0", 128, off=r2 + 47360)[:, :]
        Y0T = at("Y0T", 128, off=r2 + 47872)[:, :]
        RN = [at(f"RN{g}", 128, off=o_ot + 6144 + 512 * g)[:, :] for g in range(4)]
        DW = [at(f"DW{k}", 128, off=o_bt if k == 3 else None)[:, :] for k in range(4)]
        DO = [at(f"DO{k}", 256, off=r3 + 14336 + 1024 * k)[:, :].rearrange("p (j s) -> p j s", j=2) for k in range(2)]
        WX = at("WX", 1024, off=r4)[:, :].rearrange("p (k c) -> p k c", k=8)
        SEL = KON[:, C_SEL:C_SEL + 1024].rearrange("p (b c) -> p b c", b=8)
        ones = KON[:, C_ONE:C_ONE + 128]
        t_xp = fill(XP, 0.0, wait=b_end, inc="D.xp", eng="pool")
        tD = {}
        queue, squeue = [], []

        def D_tp(b):
            m = m_bank()
            g = tp(bank[m][:, 0:128], X[:, b, :], wait=[tC["x3", b]] + last(("M", m)), inc="D.xt")
            g = cp(X3T[b % 4], bank[m][:, 0:128], wait=[g, tB["av_pe"]] + last(("X3T", b % 4)), inc="D.xtc", eng="act")
            rel[("M", m)] = [g]
            tD["x3t", b] = g

        def D_dt(b):
            g = mm(bank[0][:, 0:128], WDT[:, b % 8, :], X3T[b % 4], start=(b % 8 == 0), stop=(b % 8 == 7),
                   wait=[tD["x3t", b], t_wdt] + (last("DT") if b % 8 == 0 else []), inc="D.dt")
            rel[("X3T", b % 4)] = [g]
            tD["dt", b] = g

        def D_conv():
            m = m_bank()
            for k in range(3):
                g = mm(bank[m][:, 128 * k:128 * k + 128], WIN[:, k, :], X3T[0],
                       wait=([tD["x3t", 0], t_win] + last(("M", m))) if k == 0 else (), inc="D.in" if k == 2 else None)
            rel[("X3T", 0)] = [g]
            g = cp(XP[:, :, 3:131], bank[m][:, 0:384].rearrange("p (k s) -> p k s", k=3), wait=[g, t_xp], inc="S")
            rel[("M", m)] = [g]
            tD["conv"] = g

        def ssd():
            g = tD["conv"]
            for k in range(3):
                w = S_CW + 4 * k
                g = ts(CO[:, k, :], XP[:, k, 0:128], PAR[:, w:w + 1], PAR[:, S_CB + k:S_CB + k + 1], ALU.mult, ALU.add,
                       wait=[g, t_xp], inc="S")
                for i in range(1, 4):
                    g = stt(CO[:, k, :], XP[:, k, i:i + 128], PAR[:, w + i:w + i + 1], CO[:, k, :], ALU.mult, ALU.add,
                            wait=[g], inc="S")
                if k == 0:
                    c = tt(CM, CO[:, 0, :].unsqueeze(1).broadcast_to((128, 16, 128)),
                           KON[:, C_HM:C_HM + 16].unsqueeze(2).broadcast_to((128, 16, 128)), ALU.mult,
                           wait=[g, tB["av_pe"]], inc="S", eng="pool")
                yield
            yield
            m = m_bank()
            k = tp(bank[m][:, 0:128], CO[:, 2, :], wait=[g] + last(("M", m)), inc="S")
            k = cp(XTK, bank[m][:, 0:128], wait=[k], inc="S")
            rel[("M", m)] = [k]
            yield
            while ("cum", 0) not in tD:
                yield
            yield
            u = tt(CU[0:16, :, :], DW[2][0:16, :].unsqueeze(1).broadcast_to((16, 16, 128)),
                   KON[0:16, C_I16:C_I16 + 16].unsqueeze(2).broadcast_to((16, 16, 128)), ALU.mult,
                   wait=[tD["cum", 0], t_kon, t_cu] + b_end, inc="S")
            m = m_bank()
            q = P.add("pe", lambda e, o=bank[m][:, 0:16]: e.transpose(o, DW[2][0:16, :], ident[0:16, 0:16]),
                      [tD["cum", 0]] + last(("M", m)), "S")
            q = ts(CUT, bank[m][:, 0:16], -1.0, None, ALU.mult, wait=[q], inc="S")
            rel[("M", m)] = [q]
            rel["DW2"] = [q, u]
            yield
            d, w = {}, {}
            for n in range(6):
                if 2 <= n:
                    hg = n - 2
                    m = m_bank()
                    for j in range(4):
                        h = 4 * hg + j
                        y = mm(bank[m][:, 8 * j:8 * j + 8], EL[hg % 3][:, j, :], XTK[:, 8 * h:8 * h + 8],
                               wait=([w[hg], k] + last(("M", m))) if j == 0 else (), inc="S")
                    rel[("PP", hg % 3)] = [y]
                    y = cp(Y0[:, 32 * hg:32 * hg + 32], bank[m][:, 0:32], wait=[y, tB["av_pe"]], inc="S")
                    rel[("M", m)] = [y]
                if 1 <= n < 5:
                    hg = n - 1
                    m = m_bank()
                    x = mm(bank[m], CO[:, 1, :], CM[:, 4 * hg:4 * hg + 4, :], wait=[c, g] + last(("M", m)), inc="S")
                    w[hg] = tt(EL[hg % 3], EL[hg % 3], bank[m].rearrange("p (j l) -> p j l", j=4), ALU.mult,
                               wait=[x, d[hg]], inc="S")
                    rel[("M", m)] = [w[hg]]
                if n < 4:
                    m = m_bank()
                    mm(bank[m], identb, masksb, start=True, stop=False, wait=[t_bf2] + last(("M", m)))
                    x = mm(bank[m], ones, CU[:, 4 * n:4 * n + 4, :], start=False, stop=True, wait=[u], inc="S")
                    for j in range(4):
                        x = act(EL[n % 3][:, j, :], bank[m][:, 128 * j:128 * j + 128], ACT.Exp,
                                bias=CUT[:, 4 * n + j:4 * n + j + 1], wait=[x, q] + last(("PP", n % 3)), inc="S")
                    d[n] = x
                    rel[("M", m)] = [x]
                yield
            m = m_bank()
            y = tp(bank[m][:, 0:128], Y0, wait=[y] + last(("M", m)), inc="S")
            y = cp(Y0T, bank[m][:, 0:128], wait=[y], inc="S")
            rel[("M", m)] = [y]
            tD["y0"] = y
            yield

        def dgroup(g):
            n = "D.n"
            x = stt(DW[1], RN[g], -1.0, RN[g], ALU.mult, ALU.max, wait=[tD["dtb", g]] + last("DW"), inc=n)
            yield
            x = act(DW[1], DW[1], ACT.Exp, scale=-1.0, wait=[x], inc=n)
            x = act(DW[1], DW[1], ACT.Ln, bias=1.0, wait=[x], inc=n)
            yield
            x = stt(DW[0], RN[g], 0.0, DW[1], ALU.max, ALU.add, wait=[x], inc=n)
            x = ts(DW[0], DW[0], PAR[:, S_AP:S_AP + 1], None, ALU.mult, wait=[x], inc=n)
            yield
            x = scan(DW[2], ones, DW[0], wait=[x] + last("DW2"), inc=n)
            tD["cum", g] = x
            yield
            y = act(DW[1], DW[2], ACT.Exp, wait=[x], inc=n)
            x = act(DW[0], DW[2], ACT.Exp, scale=-1.0, wait=[x], inc=n)
            yield
            rel["DW2"] = [x]
            x = scan(DW[3], ones, DW[0], wait=[x, tA["xb", NB - 1]], inc=n)
            yield
            x = tt(DW[1], DW[1], DW[3], ALU.mult, wait=[x, y], inc=n)
            x = rcp(RN[g], DW[1], wait=[x, tB["y_pe"]], inc=n)
            rel["DW"] = [x]
            tD["rn", g] = x
            yield

        def front(bs):
            st = {}
            n = len(bs)
            for i in range(n + 8):
                if i < n:
                    st["g", i] = gather(bs[i])
                if 3 <= i < n + 3:
                    st["l", i - 3] = combine(bs[i - 3], st["g", i - 3])
                if 4 <= i < n + 4:
                    b = bs[i - 4]
                    tC["x3", b] = ln_apply(X[:, b, :], X[:, b, :], st["l", i - 4], [], "C.x3")
                if 6 <= i < n + 6:
                    D_tp(bs[i - 6])
                if 7 <= i < n + 7:
                    b = bs[i - 7]
                    D_dt(b)
                    if b == 0:
                        D_conv()
                        squeue.append(ssd())
                    if b % 8 == 7:
                        tD["dtb", b // 8] = ts(RN[b // 8], bank[0][:, 0:128], PAR[:, S_DTB:S_DTB + 1], None, ALU.add,
                                               wait=[tD["dt", b], tB["y_pe"]], inc="D.n")
                        rel["DT"] = [tD["dtb", b // 8]]
                        queue.append(dgroup(b // 8))
                yield

        def from_queue():
            for q in (queue, squeue):
                if q and next(q[0], "end") == "end":
                    q.pop(0)

        def D_expand(v):
            m = m_bank()
            for j in range(2):
                b = 2 * v + j
                g = mm(bank[m][:, 128 * j:128 * j + 128], SEL[:, b % 8, :], RN[b // 8],
                       wait=([tD["rn", b // 8]] + last(("M", m))) if j == 0 else (), inc="D.e" if j else None)
            g = tt(DO[v % 2], bank[m][:, 0:256].rearrange("p (j s) -> p j s", j=2),
                   Y0T.unsqueeze(1).broadcast_to((128, 2, 128)), ALU.mult,
                   wait=[g, tD["y0"], tB["y_pe"]] + last(("DO", v % 2)), inc="D.o")
            rel[("M", m)] = [g]
            tD["o", v] = g

        def D_out(v):
            m = m_bank()
            for j in range(2):
                g = mm(bank[m][:, 128 * j:128 * j + 128], DO[v % 2][:, j, :], WOD,
                       wait=([tD["o", v], t_wod] + last(("M", m))) if j == 0 else (), inc="D.y" if j else None)
            rel[("DO", v % 2)] = [g]
            x = X[:, 2 * v:2 * v + 2, :]
            g = tt(x, bank[m][:, 0:256].rearrange("p (j s) -> p j s", j=2), x, ALU.add,
                   wait=[g] + [tC["x3", 2 * v + j] for j in range(2)] + [tD["x3t", 2 * v + j] for j in range(2)],
                   inc="D.z")
            rel[("M", m)] = [g]
            for j in range(2):
                tD["ln", 2 * v + j] = ln_stats(X[:, 2 * v + j, :], [g])

        def D_ln(v):
            for b in (2 * v, 2 * v + 1):
                tD["x4", b] = ln_apply(X[:, b, :], X[:, b, :], tD["ln", b], [], "D.x4")

        def D_x4t(v):
            m = m_bank()
            for j in range(2):
                g = tp(bank[m][:, 128 * j:128 * j + 128], X[:, 2 * v + j, :],
                       wait=([tD["x4", 2 * v], tD["x4", 2 * v + 1]] + last(("M", m))) if j == 0 else (),
                       inc="D.x4t" if j else None)
            g = cp(XT[:, 256 * v:256 * v + 256], bank[m][:, 0:256],
                   wait=[g, tD["y0"], tD["rn", 3] if v >= 12 else None], inc="D.x4c", eng="act")
            rel[("M", m)] = [g]
            tD["x4t", v] = g

        fr = front(range(HB))

        def beside(i):
            if i < NT - 1:
                for _ in range(2 if i < 24 else 3):
                    next(bg, None)
            elif i == NT - 1:
                for _ in bg:
                    pass
                tD["wx"] = dma(WX, a["wx"], wait=[tC["te", 1]] + last("route"), inc="ld.wx", eng="act")
            elif i >= NT + 5:
                next(fr, None)
                from_queue()
                if ("y0" in tD and ("rn", 1) in tD) or D_next[0]:
                    for fn, n in ((D_x4t, 3), (D_out, 1), (D_ln, 2), (D_expand, 0)):
                        if 0 <= D_next[0] - n < NB // 4:
                            fn(D_next[0] - n)
                    D_next[0] += 1

        D_next = [0]
        t_wf = []
        for i in ex:
            beside(i)
            if i == 12:
                t_win = dma(WIN, a["win"], wait=b_end + [tB["av_pe"]], inc="ld.win")
                t_wdt = dma(WDT, a["wdt"], wait=b_end, inc="ld.wdt")
                t_wod = dma(WOD, a["wod"], wait=b_end + [tB["av_pe"]], inc="ld.wod")
            if 16 <= i < 24:
                e = i - 16
                t_wf.append(dma(WFt[:, WF * e:WF * e + WF], a["wf"][:, WF * e:WF * e + WF],
                                wait=b_end + [tB["av_pe"]], inc="ld.wf"))
            if i == 8:
                t_cu = fill(CU, 0.0, wait=b_end + [tC["d_pe"]], inc="D.xp", eng="pool")
        assert D_next[0] >= NB // 4 + 3, D_next
        EQ = [at(f"EQ{k}", 1024, off=r1 + 4096 * k)[:, :].rearrange("p (k n) -> p k n", k=4) for k in range(3)]
        EV = [at(f"EV{k}", 512, off=r1 + 12288 + 2048 * k)[:, :].rearrange("p (j c) -> p j c", j=4) for k in range(3)]
        WSF = [at(f"WSF{k}", WF, off=r1 + 18432 + 4160 * k)[:, :] for k in range(3)]
        EC = [at(f"EC{k}", 512, off=r3 + 2048 * k)[:, :].rearrange("p (d n) -> p d n", d=2) for k in range(2)]
        EX = [at(f"EX{k}", 256, off=r3 + 4096 + 1024 * k)[:, :] for k in range(2)]
        ED = [at(f"ED{k}", 256, off=r3 + 6144 + 1024 * k)[:, :] for k in range(2)]
        EZ = [at(f"EZ{k}", 256, off=r3 + 8192 + 1024 * k)[:, :] for k in range(2)]
        HT = [at(f"HT{k}", 512, off=r3 + 10240 + 2048 * k)[:, :].rearrange("p (k n) -> p k n", k=4) for k in range(2)]
        X5T = [at(f"X5T{k}", 128, off=r1 + 30912 + 512 * k)[:, :] for k in range(8)]
        FZ = [at(f"FZ{k}", 128, off=r4 + 11264 + 512 * k)[:, :] for k in range(2)]
        FS = at("FS", 64, off=r4 + 12288)[:, :].rearrange("p (k e) -> p k e", k=8)
        FI = at("FI", 64, U32, off=r4 + 12544)[:, :].rearrange("p (k e) -> p k e", k=8)
        MS = at("MS", 16, off=r4 + 12800)[:, :]
        c_end = [tC["ac", 2 * NT - 1], tC["d_pe"], tC["y_act"]] + [tC["ys", 1, q] for q in range(4)]
        SCL = float(1.0 / np.sqrt(np.float32(128.0)))
        t_nbg = ts(PAR[:, S_N + 1:S_N + 2], PAR[:, S_BG:S_BG + 1], 0.5, None, ALU.mult, wait=[t_par], inc="E.nbg")
        for k in range(3):
            rel[("PT", k)] = [tC["d_pe"]]
        tE = {}

        def par(k):
            return PAR[:, k:k + 1]

        def E_qk(v):
            x4 = XT[:, 256 * v:256 * v + 256]
            cx = CT[:, 256 * v:256 * v + 256]
            r = v % 3
            xw = [tD["x4t", v], tD["wx"]]
            m = m_bank()
            mm(bank[m][:, 0:256], WX[:, 0, :], x4, wait=xw + last(("M", m)))
            g = mm(bank[m][:, 256:512], WX[:, 3, :], cx, inc="E.q")
            g0 = ts(EQ[r][:, 0, :], bank[m][:, 0:256], par(S_BQC), SCL, ALU.add, ALU.mult,
                    wait=[g] + last(("EQ", r)) + c_end, inc="E.qc")
            tE["q", v] = ts(EQ[r][:, 1, :], bank[m][:, 256:512], par(S_BQS), SCL, ALU.add, ALU.mult, inc="E.qc")
            rel[("M", m)] = [tE["q", v]]
            m = m_bank()
            mm(bank[m][:, 0:256], WX[:, 1, :], cx, wait=last(("M", m)))
            g = mm(bank[m][:, 256:512], WX[:, 4, :], x4, inc="E.k")
            act(EQ[r][:, 2, :], bank[m][:, 0:256], ACT.Identity, bias=par(S_BKS), wait=[g] + last(("EQ", r)) + c_end)
            tE["k", v] = act(EQ[r][:, 3, :], bank[m][:, 256:512], ACT.Identity, bias=par(S_BKC), inc="E.kc")
            rel[("M", m)] = [tE["k", v]]

        def E_v(v):
            x4 = XT[:, 256 * v:256 * v + 256]
            cx = CT[:, 256 * v:256 * v + 256]
            r = v % 3
            m = m_bank()
            for j in range(4):
                src = (cx if j < 2 else x4)[:, 128 * (j % 2):128 * (j % 2) + 128]
                g = mm(bank[m][:, 128 * j:128 * j + 128], src, WX[:, 2 if j < 2 else 5, :],
                       wait=last(("M", m)) if j == 0 else (), inc="E.v" if j == 3 else None)
            tE["v", v] = cp(EV[r], bank[m].rearrange("p (j c) -> p j c", j=4), wait=[g] + last(("EV", r)) + c_end,
                            inc="E.vc", eng="act")
            rel[("M", m)] = [tE["v", v]]

        def E_S(v):
            sb, r = bank[1], v % 3
            for j in range(4):
                c = slice(128 * (j % 2), 128 * (j % 2) + 128)
                g = mm(sb[:, 128 * j:128 * j + 128], EQ[r][:, j // 2, c], EQ[r][:, 2 + j // 2, c],
                       wait=([tE["q", v], tE["k", v]] + last("ES")) if j == 0 else (),
                       inc="E.s" if j == 3 else None)
            rel[("EQ", r)] = [g]
            s3 = sb.rearrange("p (j s) -> p j s", j=4)
            g = sm_max("E", v, s3, g)
            g = sm_exp("E", v, s3, g)
            rel["ES"] = [g]
            tE["e", v] = g

        def E_norm(v):
            tE["n", v] = sm_nrm("E", v, sm_rec("E", v, tE["e", v]))

        def E_T(v):
            g = sm_tp("E", v, bank[3], tE["n", v], last("ET"))
            g = cp(PT[v % 3], bank[3].rearrange("p (j s) -> p j s", j=4), wait=[g] + last(("PT", v % 3)), inc="E.pt",
                   eng="act")
            rel["ET"] = [g]
            tE["pt", v] = g

        def E_AV(v):
            for j in range(4):
                g = mm(bank[4][:, 128 * j:128 * j + 128], EV[v % 3][:, j, :], PT[v % 3][:, j, :],
                       wait=([tE["pt", v], tE["v", v]] + last("EO")) if j == 0 else (), inc="E.av" if j == 3 else None)
            rel[("PT", v % 3)] = [g]
            rel[("EV", v % 3)] = [g]
            act(EC[v % 2][:, 0, :], bank[4][:, 0:256], ACT.Identity, bias=par(S_BVS),
                wait=[g] + last(("EC", v % 2)) + c_end)
            g = act(EC[v % 2][:, 1, :], bank[4][:, 256:512], ACT.Identity, bias=par(S_BVC), inc="E.ec")
            rel["EO"] = [g]
            tE["ec", v] = g
            tE["d", v] = tt(ED[v % 2], EC[v % 2][:, 0, :], EC[v % 2][:, 1, :], ALU.subtract,
                            wait=[g] + last(("ED", v % 2)) + c_end, inc="E.d", eng="pool")

        def E_gate(v):
            m = m_bank()
            mm(bank[m][:, 0:256], WX[:, 6, :], EC[v % 2][:, 0, :], start=True, stop=False,
               wait=[tE["ec", v]] + last(("M", m)))
            g = mm(bank[m][:, 0:256], WX[:, 7, :], EC[v % 2][:, 1, :], start=False, stop=True, inc="E.g")
            tE["g", v] = g
            g = act(EX[v % 2], bank[m][:, 0:256], ACT.Tanh, bias=PAR[:, S_N + 1:S_N + 2], scale=0.5,
                    wait=[g, t_nbg] + last(("EX", v % 2)) + c_end, inc="E.ex")
            rel[("M", m)] = [g]
            tE["ex", v] = g

        def E_mix(v):
            g = stt(ED[v % 2], EX[v % 2], 1.0, ED[v % 2], ALU.add, ALU.mult, wait=[tE["ex", v], tE["d", v]], inc="E.m")
            rel[("EX", v % 2)] = [g]
            g = stt(ED[v % 2], ED[v % 2], 0.5, EC[v % 2][:, 1, :], ALU.mult, ALU.add, wait=[g], inc="E.m")
            rel[("EC", v % 2)] = [g, tE["g", v]]
            g = tt(EZ[v % 2], ED[v % 2], XT[:, 256 * v:256 * v + 256], ALU.add, wait=[g] + last(("EZ", v % 2)) + c_end,
                   inc="E.z", eng="pool")
            rel[("ED", v % 2)] = [g]
            tE["z", v] = g

        def E_tp(v):
            m = m_bank()
            for j in range(2):
                g = tp(bank[m][:, 128 * j:128 * j + 128], EZ[v % 2][:, 128 * j:128 * j + 128],
                       wait=([tE["z", v]] + last(("M", m))) if j == 0 else (), inc="E.zt" if j else None)
            rel[("EZ", v % 2)] = [g]
            g = cp(X[:, 2 * v:2 * v + 2, :], bank[m][:, 0:256].rearrange("p (j s) -> p j s", j=2),
                   wait=[g, tD["x4t", v]], inc="E.zc", eng="act")
            rel[("M", m)] = [g]
            tE["zc", v] = g

        def E_st(v):
            for b in (2 * v, 2 * v + 1):
                tE["ln", b] = ln_stats(X[:, b, :], [tE["zc", v]])

        def E_ln(v):
            for b in (2 * v, 2 * v + 1):
                tE["x5", v] = ln_apply(X[:, b, :], X[:, b, :], tE["ln", b], [], "E.x5")

        tF = {}

        def F_top(v):
            m = m_bank()
            for j in range(2):
                g = tp(bank[m][:, 128 * j:128 * j + 128], X[:, 2 * v + j, :],
                       wait=([tE["x5", v]] + last(("M", m))) if j == 0 else (), inc="F.xt" if j else None)
            tF["xt", v] = g
            for j in range(2):
                b = 2 * v + j
                g = act(X5T[b % 8], bank[m][:, 128 * j:128 * j + 128], ACT.Copy, accum=MS[:, b % 16:b % 16 + 1],
                        wait=[tF["xt", v]] + last(("X5T", b % 8)) + last(("MS", b % 16)) + c_end, inc="F.x")
                tF["x", b] = g
            rel[("M", m)] = [g]

        def F_score(v):
            m = m_bank()
            for j in range(2):
                b = 2 * v + j
                g = mm(bank[m][0:1, 8 * j:8 * j + 8], MS[:, b % 16:b % 16 + 1], PAR[:, S_WR1:S_WR1 + 8],
                       wait=[tF["x", b]] + (last(("M", m)) if j == 0 else []), inc="F.s")
                rel[("MS", b % 16)] = [g]
            for j in range(2):
                b = 2 * v + j
                k = b % 4
                s = FS[0:1, k, :]
                q = stt(s, bank[m][0:1, 8 * j:8 * j + 8], 1.0 / 128, PAR[0:1, S_BR:S_BR + 8], ALU.mult, ALU.add,
                        wait=[g] + c_end, inc="F.t")
                if j == 1:
                    rel[("M", m)] = [q]
                q = P.add("dve", lambda e, k=k: e.max(FS[0:1, 4 + k, :], FS[0:1, k, :]), [q], "F.t")
                q = P.add("dve", lambda e, k=k: e.max_index(FI[0:1, k, :], FS[0:1, 4 + k, :], FS[0:1, k, :]),
                          [q], "F.t")
                tF["i", b] = q

        def F_w(b):
            tF["w", b] = staged(WSF[b % 3], WFt, WF, FI[0:1, b % 4, 0:1], [tF["i", b], t_wf[-1]] + last(("WSF", b % 3))
                                + c_end, "F.w")

        def F_h(b):
            w, k = WSF[b % 3], b % 2
            for f in range(4):
                g = mm(bank[7][:, 128 * f:128 * f + 128], w[:, 128 * f:128 * f + 128], X5T[b % 8],
                       wait=([tF["w", b], tF["x", b]] + last("FH")) if f == 0 else (), inc="F.h" if f == 3 else None)
            for f in range(4):
                q = act(HT[k][:, f, :], bank[7][:, 128 * f:128 * f + 128], ACT.Relu, bias=w[:, 1024 + f:1025 + f],
                        wait=([g] + last(("HT", k)) + c_end) if f == 0 else (), inc="F.r" if f == 3 else None)
            rel["FH"] = [q]
            tF["h", b] = q

        def F_out(b):
            w, k = WSF[b % 3], b % 2
            m = m_bank()
            for f in range(4):
                g = mm(bank[m][:, 0:128], w[:, 512 + 128 * f:640 + 128 * f], HT[k][:, f, :], start=(f == 0),
                       stop=(f == 3), wait=([tF["h", b]] + last(("M", m))) if f == 0 else (),
                       inc="F.o" if f == 3 else None)
            rel[("HT", k)] = [g]
            g = stt(FZ[k], bank[m][:, 0:128], w[:, 1028:1029], X5T[b % 8], ALU.add, ALU.add,
                    wait=[g] + last(("FZ", k)) + c_end, inc="F.z")
            rel[("M", m)] = [g]
            rel[("WSF", b % 3)] = [g]
            rel[("X5T", b % 8)] = [g]
            tF["z", b] = g

        def F_tp(b):
            m = m_bank()
            g = tp(bank[m][:, 0:128], FZ[b % 2], wait=[tF["z", b]] + last(("M", m)), inc="F.zt")
            rel[("FZ", b % 2)] = [g]
            g = cp(X[:, b, :], bank[m][:, 0:128], wait=[g, tF["xt", b // 2]], inc="F.zc", eng="act")
            rel[("M", m)] = [g]
            tF["zc", b] = g

        def F_st(b):
            tF["ln", b] = ln_stats(X[:, b, :], [tF["zc", b]])

        def F_ln(b):
            g = ln_apply(X[:, b, :], X[:, b, :], tF["ln", b], [], "F.y")
            tF["st"] = dma(out[b], X[:, b, :], wait=[g], inc="st")

        fr = front(range(HB, NB))
        rel["FH"], rel["EO"], rel["ET"] = last("CY"), last(("GU", 4)), last(("GU", 3))
        rel["ES"], rel[("M", 2)] = last(("GU", 1)), last(("GU", 2))
        ring.append(2)
        NV = NB // 2

        def first(fn):
            return lambda v: fn(2 * v)

        def second(fn):
            return lambda v: fn(2 * v + 1)

        def both(fn):
            return lambda v: (fn(2 * v), fn(2 * v + 1))

        def later(fn):
            return lambda v: fn(v) if v >= NB // 4 else None

        plan = ((later(D_expand), 0), (later(D_ln), 1), (E_norm, 3), (E_AV, 4), (E_mix, 5), (E_qk, 2),
                (first(F_w), 8), (F_top, 7), (E_st, 6), (E_v, 3), (second(F_h), 9), (first(F_out), 9),
                (second(F_tp), 10), (both(F_ln), 11), (E_S, 2), (later(D_out), 0), (E_gate, 4), (second(F_w),
                8), (E_T, 3), (later(D_x4t), 1), (second(F_out), 9), (E_tp, 5), (first(F_h), 8),
                (F_score, 7), (E_ln, 6), (first(F_tp), 9), (both(F_st), 10))
        for s in range(2, NV + 12):
            next(fr, None)
            for _ in range(4):
                from_queue()
            for fn, lag in plan:
                if 0 <= s - lag < NV:
                    fn(s - lag)
            next(fr, None)
            next(fr, None)
            if ("dtb", 3) in tD and 0 not in ring:
                rel[("M", 0)] = last("DT")
                ring.append(0)
        finish(P, nc, dma, X, out, [], [tF["st"]])


def finish(P, nc, dma, X, out, toks, done=None):
    if done is None:
        done = [dma(out.rearrange("b t c -> t b c"), X, wait=toks, inc="st")]
    P.add("sp", lambda e: e.nop(), done, None)
    with nc.Block() as blk:
        @blk.sync
        def _(e):
            P.play("sp", e)

        @blk.scalar
        def _(e):
            P.play("act", e)

        @blk.vector
        def _(e):
            P.play("dve", e)

        @blk.gpsimd
        def _(e):
            P.play("pool", e)

        @blk.tensor
        def _(e):
            P.play("pe", e)


def layouts(i):
    f = np.float32

    def pad_heads(w, times):
        n = w.shape[0] // 8
        o = np.zeros((128, 8, 32), f)
        o[:, :, :n * times] = np.tile(w.T.reshape(128, 8, n), (1, 1, times))
        return o.reshape(128, 256)

    par = np.zeros((128, S_N), f)
    par[:, S_SCALE] = i["L0_attn_scale"]
    par[:, S_GAMMA] = i["L0_xattn_ln_gamma"]
    par[:, S_BETA] = i["L0_xattn_ln_beta"]
    par[:, S_GATE] = i["L0_xattn_gate"][0]
    par[:, S_DTB] = np.tile(i["L1_attn_dt_bias"], 8)
    par[:, S_AP] = np.tile(i["L1_attn_A_param"], 8)
    par[:, S_CW:S_CW + 12] = i["L1_attn_conv_w"].reshape(3, 128, 4).transpose(1, 0, 2).reshape(128, 12)
    par[:, S_CB:S_CB + 3] = i["L1_attn_conv_b"].reshape(3, 128).T
    for k, n in enumerate(("bq_c", "bk_s", "bv_s", "bq_s", "bk_c", "bv_c", "bg")):
        par[:, S_BQC + k] = i["L1_xattn_" + n]
    par[:, S_BR:S_BR + 8] = i["L1_ffn_br"]
    par[:, S_WR0:S_WR0 + 8] = i["L0_ffn_router_w"]
    par[:, S_WR1:S_WR1 + 8] = i["L1_ffn_Wr"]

    x, ctx = i["x"], i["ctx_1024"]
    wo = np.zeros((8, 32, 128), f)
    wo[:, :16] = i["L0_attn_Wo"].T.reshape(8, 16, 128)
    wkv = i["L0_xattn_w_kv"]
    we = np.zeros((128, 8, WE), f)
    we[:, :, 0:352] = i["L0_ffn_gate_proj"].transpose(1, 0, 2)
    we[:, :, 384:736] = i["L0_ffn_up_proj"].transpose(1, 0, 2)
    dn = np.zeros((8, 384, 128), f)
    dn[:, :352] = i["L0_ffn_down_proj"]
    we[:, :, 768:1152] = dn.reshape(8, 3, 128, 128).transpose(2, 0, 1, 3).reshape(128, 8, 384)
    win = i["L1_attn_W_in"]
    wdt = np.zeros((128, 8, 8, 16), f)
    for b in range(8):
        wdt[:, b, b, :] = win[384:400].T
    wf = np.zeros((128, 8, WF), f)
    wf[:, :, 0:512] = i["L1_ffn_W1"].transpose(1, 0, 2)
    wf[:, :, 512:1024] = i["L1_ffn_W2"].reshape(8, 4, 128, 128).transpose(2, 0, 1, 3).reshape(128, 8, 512)
    wf[:, :, 1024:1028] = i["L1_ffn_b1"].reshape(8, 4, 128).transpose(2, 0, 1)
    wf[:, :, 1028] = i["L1_ffn_b2"].T
    wg = i["L1_xattn_Wg"]
    wx = np.stack([i["L1_xattn_" + n].T for n in ("Wq_c", "Wk_s", "Wv_s", "Wq_s", "Wk_c", "Wv_c")]
                  + [wg[:, :128].T, wg[:, 128:].T], 1)
    return {
        "par": par, "kon": constants(),
        "x": x.transpose(1, 0, 2), "xT": x.transpose(2, 0, 1).reshape(128, 4096),
        "cT": ctx.transpose(2, 0, 1).reshape(128, 4096),
        "wqr": i["L0_attn_Wq"], "wk": pad_heads(i["L0_attn_Wk"], 4).reshape(128, 2, 128),
        "wv": pad_heads(i["L0_attn_Wv"], 1),
        "wo": wo.reshape(2, 128, 128).transpose(1, 0, 2),
        "wqT": i["L0_xattn_w_q"].T.reshape(16, 64, 128).transpose(1, 0, 2),
        "wkT": wkv[:, :1024].T.reshape(16, 64, 128).transpose(1, 0, 2),
        "wvb": wkv[:, 1024:], "wob": i["L0_xattn_w_out"].reshape(8, 128, 128).transpose(1, 0, 2),
        "bo": np.broadcast_to(i["L0_xattn_b_out"], (128, 128)),
        "we": we.reshape(128, 8 * WE),
        "win": win[0:384].reshape(3, 128, 128).transpose(2, 0, 1), "wdt": wdt.reshape(128, 1024),
        "wod": i["L1_attn_W_out"].T, "wx": wx, "wf": wf.reshape(128, 8 * WF),
    }


def kernel(**inputs):
    import concourse.bacc as bacc
    from concourse.bass_utils import run_bass_kernel_spmd

    arrays = {n: np.ascontiguousarray(v) for n, v in layouts({k: np.asarray(v) for k, v in inputs.items()}).items()}
    nc = bacc.Bacc("TRN2", target_bir_lowering=False, num_devices=1)
    aps = {n: nc.dram_tensor(n, v.shape, mybir.dt.from_np(v.dtype), kind="ExternalInput").ap()
           for n, v in arrays.items()}
    out = nc.dram_tensor("out", (NB, 128, 128), F32, kind="ExternalOutput").ap()
    build(nc, aps, out)
    r = run_bass_kernel_spmd(nc, [arrays], core_ids=[0])
    return r.results[0]["out"]
```
